# Optimizing a Trainium2 kernel written in Bass

```python
import numpy as np
import jax
import jax.numpy as jnp

def _softmax(x, axis=-1):
    return jax.nn.softmax(x, axis=axis)

def _gelu(x):
    return jax.nn.gelu(x, approximate=True)

def _silu(x):
    return jax.nn.silu(x)

def _sigmoid(x):
    return jax.nn.sigmoid(x)

def _layernorm(x, axis=-1, eps=1e-05):
    m = jnp.mean(x, axis=axis, keepdims=True)
    v = jnp.var(x, axis=axis, keepdims=True)
    return (x - m) / jnp.sqrt(v + eps)

def _scatter_add(tgt, idx, src, axis=0):
    return tgt.at[idx].add(src)

def _segment_sum(src, seg, n):
    return jax.ops.segment_sum(src, seg, n)
kernel_name = 'mk_vit_tower_d1_tok_img768_r4_cbe535'

def setup_inputs(seed: int=0):
    np.random.seed(seed)
    _w = jnp.asarray

    def _rec_inputs():
        import jax
        import jax.numpy as jnp
        _rk = jax.random.key(seed)
        x = -9.30917e-05 + 1.0002 * jax.random.normal(jax.random.fold_in(_rk, 1), (64, 3, 224, 224), jnp.float32)
        return x
    x = _rec_inputs()

    def _L0_tok_setup():
        import jax, jax.numpy as jnp
        import numpy as np
        IMAGE_SIZE = 224
        NUM_CHANNELS = 3
        PATCH_SIZE = 16
        EMBED_DIM = 192
        NUM_PATCHES = (IMAGE_SIZE // PATCH_SIZE) ** 2
        PATCH_DIM = PATCH_SIZE * PATCH_SIZE
        BATCH = 32
        key = jax.random.key(seed)
        k1, k2, k3 = jax.random.split(key, 3)
        x = jax.random.normal(k1, (BATCH, NUM_CHANNELS, IMAGE_SIZE, IMAGE_SIZE), dtype=jnp.float32)
        decode_weights = 0.01 * jax.random.normal(k2, (NUM_PATCHES, EMBED_DIM, PATCH_DIM), dtype=jnp.float32)
        decode_biases = jnp.zeros((NUM_PATCHES, EMBED_DIM), dtype=jnp.float32)
        merge_weights = 0.01 * jax.random.normal(k3, (NUM_PATCHES, NUM_CHANNELS), dtype=jnp.float32)
        merge_biases = jnp.zeros((NUM_PATCHES,), dtype=jnp.float32)
        return {'x': x, 'decode_weights': decode_weights, 'decode_biases': decode_biases, 'merge_weights': merge_weights, 'merge_biases': merge_biases}
    _L0_tok_all = _L0_tok_setup()
    _L0_tok_in = {k: v for k, v in _L0_tok_all.items() if k in ('decode_weights', 'decode_biases', 'merge_weights', 'merge_biases')}
    del _L0_tok_all

    def _L0_attn_setup():
        import jax, jax.numpy as jnp
        import numpy as np
        D_MODEL = 192
        H = 6
        DQK = 128
        DV = 64
        SCALE_BASE = 512.0

        def _xpos(x, sign):
            B, T, Hn, d = x.shape
            half = d // 2
            pos = jnp.arange(T, dtype=jnp.float32)
            inv_freq = 1.0 / 10000.0 ** (jnp.arange(half, dtype=jnp.float32) / half)
            angles = pos[:, None] * inv_freq[None, :]
            zeta = (jnp.arange(half, dtype=jnp.float32) + half) / d
            decay = zeta[None, :] ** (sign * pos[:, None] / SCALE_BASE)
            cos_a = (jnp.cos(angles) * decay)[None, :, None, :]
            sin_a = (jnp.sin(angles) * decay)[None, :, None, :]
            x1, x2 = (x[..., :half], x[..., half:])
            return jnp.concatenate([x1 * cos_a - x2 * sin_a, x1 * sin_a + x2 * cos_a], axis=-1)

        def _decay_mask(T):
            gammas = jnp.array([1.0 - 2.0 ** (-(5 + h)) for h in range(H)], dtype=jnp.float32)
            i = jnp.arange(T, dtype=jnp.float32)
            diff = i[:, None] - i[None, :]
            causal = (diff >= 0).astype(jnp.float32)
            D = gammas[:, None, None] ** jnp.clip(diff, 0.0)[None] * causal[None]
            row = jnp.clip(jnp.sum(D, axis=-1, keepdims=True), 1e-06)
            return D / jnp.sqrt(row)
        key = jax.random.key(seed)
        ks = jax.random.split(key, 6)
        B, T = (2, 512)

        def xavier(k, shape):
            lim = float(np.sqrt(6.0 / (shape[0] + shape[1])))
            return jax.random.uniform(k, shape, jnp.float32, -lim, lim)
        return {'x': jax.random.normal(ks[0], (B, T, D_MODEL), jnp.float32), 'Wq': xavier(ks[1], (D_MODEL, H * DQK)), 'Wk': xavier(ks[2], (D_MODEL, H * DQK)), 'Wv': xavier(ks[3], (D_MODEL, H * DV)), 'Wg': xavier(ks[4], (D_MODEL, H * DV)), 'Wo': xavier(ks[5], (H * DV, D_MODEL)), 'gn_weight': jnp.ones((H * DV,), jnp.float32), 'gn_bias': jnp.zeros((H * DV,), jnp.float32)}
    _L0_attn_all = _L0_attn_setup()
    _L0_attn_in = {k: v for k, v in _L0_attn_all.items() if k in ('Wq', 'Wk', 'Wv', 'Wg', 'Wo', 'gn_weight', 'gn_bias')}
    del _L0_attn_all

    def _L0_ffn_setup():
        import jax, jax.numpy as jnp
        import numpy as np
        CAPACITY_FACTOR = 1.25
        key = jax.random.key(seed)
        ks = jax.random.split(key, 5)
        B, S, D, F, E = (8, 512, 192, 768, 8)
        return {'x': jax.random.normal(ks[0], (B, S, D), jnp.float32), 'switch_w': jax.random.normal(ks[1], (D, E), jnp.float32) * 0.02, 'switch_b': jnp.zeros((E,), jnp.float32), 'w1': jax.random.normal(ks[2], (E, D, F), jnp.float32) * 0.02, 'b1': jnp.zeros((E, F), jnp.float32), 'w2': jax.random.normal(ks[3], (E, F, D), jnp.float32) * 0.02, 'b2': jnp.zeros((E, D), jnp.float32)}
    _L0_ffn_all = _L0_ffn_setup()
    _L0_ffn_in = {k: v for k, v in _L0_ffn_all.items() if k in ('switch_w', 'switch_b', 'w1', 'b1', 'w2', 'b2')}
    del _L0_ffn_all
    return {'x': x, 'L0_tok_decode_weights': _L0_tok_in['decode_weights'], 'L0_tok_decode_biases': _L0_tok_in['decode_biases'], 'L0_tok_merge_weights': _L0_tok_in['merge_weights'], 'L0_tok_merge_biases': _L0_tok_in['merge_biases'], 'L0_attn_Wq': _L0_attn_in['Wq'], 'L0_attn_Wk': _L0_attn_in['Wk'], 'L0_attn_Wv': _L0_attn_in['Wv'], 'L0_attn_Wg': _L0_attn_in['Wg'], 'L0_attn_Wo': _L0_attn_in['Wo'], 'L0_attn_gn_weight': _L0_attn_in['gn_weight'], 'L0_attn_gn_bias': _L0_attn_in['gn_bias'], 'L0_ffn_switch_w': _L0_ffn_in['switch_w'], 'L0_ffn_switch_b': _L0_ffn_in['switch_b'], 'L0_ffn_w1': _L0_ffn_in['w1'], 'L0_ffn_b1': _L0_ffn_in['b1'], 'L0_ffn_w2': _L0_ffn_in['w2'], 'L0_ffn_b2': _L0_ffn_in['b2']}

def reference(x, L0_tok_decode_weights, L0_tok_decode_biases, L0_tok_merge_weights, L0_tok_merge_biases, L0_attn_Wq, L0_attn_Wk, L0_attn_Wv, L0_attn_Wg, L0_attn_Wo, L0_attn_gn_weight, L0_attn_gn_bias, L0_ffn_switch_w, L0_ffn_switch_b, L0_ffn_w1, L0_ffn_b1, L0_ffn_w2, L0_ffn_b2):
    import jax
    import jax.numpy as jnp

    def _L0_tok_ref(x, decode_weights, decode_biases, merge_weights, merge_biases):
        import jax, jax.numpy as jnp
        import numpy as np
        IMAGE_SIZE = 224
        NUM_CHANNELS = 3
        PATCH_SIZE = 16
        EMBED_DIM = 192
        NUM_PATCHES = (IMAGE_SIZE // PATCH_SIZE) ** 2
        PATCH_DIM = PATCH_SIZE * PATCH_SIZE
        BATCH = 32
        B, C, H, W = x.shape
        ps = PATCH_SIZE
        Nh, Nw = (H // ps, W // ps)
        N = Nh * Nw
        x_patched = x.reshape(B, C, Nh, ps, Nw, ps).transpose(0, 1, 2, 4, 3, 5).reshape(B, C, N, ps * ps)
        decoded = jnp.einsum('bcnp,nfp->bcnf', x_patched, decode_weights) + decode_biases[None, None, :, :]
        out = jnp.einsum('bcnf,nc->bnf', decoded, merge_weights) + merge_biases[None, :, None]
        return out

    def _L0_attn_ref(x, Wq, Wk, Wv, Wg, Wo, gn_weight, gn_bias):
        import jax, jax.numpy as jnp
        import numpy as np
        D_MODEL = 192
        H = 6
        DQK = 128
        DV = 64
        SCALE_BASE = 512.0

        def _xpos(x, sign):
            B, T, Hn, d = x.shape
            half = d // 2
            pos = jnp.arange(T, dtype=jnp.float32)
            inv_freq = 1.0 / 10000.0 ** (jnp.arange(half, dtype=jnp.float32) / half)
            angles = pos[:, None] * inv_freq[None, :]
            zeta = (jnp.arange(half, dtype=jnp.float32) + half) / d
            decay = zeta[None, :] ** (sign * pos[:, None] / SCALE_BASE)
            cos_a = (jnp.cos(angles) * decay)[None, :, None, :]
            sin_a = (jnp.sin(angles) * decay)[None, :, None, :]
            x1, x2 = (x[..., :half], x[..., half:])
            return jnp.concatenate([x1 * cos_a - x2 * sin_a, x1 * sin_a + x2 * cos_a], axis=-1)

        def _decay_mask(T):
            gammas = jnp.array([1.0 - 2.0 ** (-(5 + h)) for h in range(H)], dtype=jnp.float32)
            i = jnp.arange(T, dtype=jnp.float32)
            diff = i[:, None] - i[None, :]
            causal = (diff >= 0).astype(jnp.float32)
            D = gammas[:, None, None] ** jnp.clip(diff, 0.0)[None] * causal[None]
            row = jnp.clip(jnp.sum(D, axis=-1, keepdims=True), 1e-06)
            return D / jnp.sqrt(row)
        B, T, _ = x.shape
        Q = (x @ Wq).reshape(B, T, H, DQK)
        K = (x @ Wk).reshape(B, T, H, DQK)
        V = (x @ Wv).reshape(B, T, H, DV)
        Q = _xpos(Q, 1.0)
        K = _xpos(K, -1.0)
        scores = jnp.einsum('bihd,bjhd->bhij', Q, K) * DQK ** (-0.5)
        scores = scores * _decay_mask(T)[None]
        out = jnp.einsum('bhij,bjhv->bihv', scores, V)
        concat = out.reshape(B, T, H * DV)
        g = concat.transpose(0, 2, 1).reshape(B, H, DV, T)
        mean = jnp.mean(g, axis=(2, 3), keepdims=True)
        var = jnp.var(g, axis=(2, 3), keepdims=True)
        g = (g - mean) / jnp.sqrt(var + 1e-05)
        g = g.reshape(B, H * DV, T) * gn_weight[None, :, None] + gn_bias[None, :, None]
        normed = g.transpose(0, 2, 1)
        gate = jax.nn.silu(x @ Wg)
        return normed * gate @ Wo

    def _L0_ffn_ref(x, switch_w, switch_b, w1, b1, w2, b2):
        import jax, jax.numpy as jnp
        import numpy as np
        CAPACITY_FACTOR = 1.25
        B, S, D = x.shape
        E = w1.shape[0]
        xf = x.reshape(-1, D)
        N = xf.shape[0]
        capacity = int(CAPACITY_FACTOR * N / E)
        probs = jax.nn.softmax(xf @ switch_w + switch_b, axis=-1)
        prob_max = jnp.max(probs, axis=-1)
        routes = jnp.argmax(probs, axis=-1)
        sort_idx = jnp.lexsort((-prob_max, routes))
        counts = jnp.bincount(routes, length=E)
        starts = jnp.concatenate([jnp.zeros((1,), counts.dtype), jnp.cumsum(counts)[:-1]])
        rank_sorted = jnp.arange(N) - starts[routes[sort_idx]]
        rank = jnp.zeros((N,), jnp.int32).at[sort_idx].set(rank_sorted.astype(jnp.int32))
        keep = rank < capacity
        dest_e = jnp.where(keep, routes, E)
        dest_c = jnp.where(keep, rank, 0)
        buf = jnp.zeros((E + 1, capacity, D), xf.dtype).at[dest_e, dest_c].set(xf)
        h = jax.nn.gelu(jnp.einsum('ecd,edf->ecf', buf[:E], w1) + b1[:, None, :], approximate=False)
        o = jnp.einsum('ecf,efd->ecd', h, w2) + b2[:, None, :]
        y_exp = o[routes, dest_c]
        y = jnp.where(keep[:, None], y_exp, xf)
        out = y * prob_max[:, None]
        return out.reshape(B, S, D)
    h = _L0_tok_ref(x, L0_tok_decode_weights, L0_tok_decode_biases, L0_tok_merge_weights, L0_tok_merge_biases)
    h = h + _L0_attn_ref(_layernorm(h, axis=-1), L0_attn_Wq, L0_attn_Wk, L0_attn_Wv, L0_attn_Wg, L0_attn_Wo, L0_attn_gn_weight, L0_attn_gn_bias)
    h = h + _L0_ffn_ref(_layernorm(h, axis=-1), L0_ffn_switch_w, L0_ffn_switch_b, L0_ffn_w1, L0_ffn_b1, L0_ffn_w2, L0_ffn_b2)
    return h

_drawn_inputs = setup_inputs


def setup_inputs(seed=0):
    import zlib

    import numpy as np

    out = dict(_drawn_inputs(seed))
    spreads = {'L0_tok_decode_biases': (0.0, 0.1),
     'L0_tok_merge_biases': (0.0, 0.1),
     'L0_attn_gn_weight': (1.0, 0.2),
     'L0_attn_gn_bias': (0.0, 0.1),
     'L0_ffn_switch_b': (0.0, 0.1),
     'L0_ffn_b1': (0.0, 0.643),
     'L0_ffn_b2': (0.0, 0.1)}
    factors = {}
    for name, (base, spread) in spreads.items():
        noise = np.random.default_rng([zlib.crc32(name.encode()), seed]).standard_normal(out[name].shape)
        drawn = base * np.exp(spread * noise) if base else spread * noise
        out[name] = jnp.asarray(drawn.astype(out[name].dtype))
    for name, factor in factors.items():
        out[name] = (out[name] * factor).astype(out[name].dtype)
    return out
```

```python
from contextlib import ExitStack

import numpy as np
import concourse.bass as bass
from concourse import mybir

ALU = mybir.AluOpType
ACT = mybir.ActivationFunctionType
AX = mybir.AxisListType
F32 = mybir.dt.float32
I32 = mybir.dt.int32
U32 = mybir.dt.uint32
BF16 = mybir.dt.bfloat16

B = 64
C = 3
N = 196
PD = 256
D = 192
H = 6
DQK = 128
DV = 64
E = 8
F = 768
HALF = N // 2
KC = PD // 128
DC = 96
ND = D // DC
NP = H // 2
NT = 2 * B
TOKENS = B * N
CAP = int(1.25 * TOKENS / E)
EPS = 1e-5

RING = 7
ROUNDS = HALF // RING

G = 256
FM = F // 128
REGION = TOKENS + G
ZROWS = E * REGION + G
NG = (TOKENS + E * (G - 1)) // G
SLOTS = 4
NG += -NG % SLOTS
ROW = D + 4
EMPTY = 16384.0
PSTEPS = 28
ISTEPS = 14


def constants():
    f = np.float32
    pos = np.arange(N, dtype=f)
    half = DQK // 2
    inv = (f(1.0) / f(10000.0) ** (np.arange(half, dtype=f) / f(half))).astype(f)
    angle = pos[:, None] * inv[None, :]
    zeta = (np.arange(half, dtype=f) + f(half)) / f(DQK)
    cos_t = np.zeros((128, 2, 2, N), f)
    sin_t = np.zeros((128, 2, 2, N), f)
    for k, sign in enumerate((1.0, -1.0)):
        decay = zeta[None, :] ** (f(sign) * pos[:, None] / f(512.0))
        c = (np.cos(angle) * decay).T.astype(f)
        s = (np.sin(angle) * decay).T.astype(f)
        for h in range(2):
            cos_t[:, k, h] = np.concatenate([c, c])
            sin_t[:, k, h] = np.concatenate([-s, s])
    gam = np.array([1.0 - 2.0 ** (-(5 + h)) for h in range(H)], dtype=f)
    diff = pos[:, None] - pos[None, :]
    dm = gam[:, None, None] ** np.maximum(diff, 0)[None] * (diff >= 0).astype(f)[None]
    row = np.maximum(dm.sum(-1, keepdims=True), 1e-6)
    dm = (dm / np.sqrt(row) * DQK ** -0.5).astype(f)
    dmt = dm.transpose(2, 0, 1)
    mask = np.concatenate([dmt[:HALF], dmt[HALF:, :, HALF:]], axis=2)
    blk = np.zeros((128, 128), f)
    blk[:64, :64] = blk[64:, 64:] = 1.0 / 64
    steps = np.zeros((PSTEPS + ISTEPS,), f)
    steps[:PSTEPS] = 0.5 ** np.arange(1, PSTEPS + 1)
    steps[PSTEPS:] = 2.0 ** np.arange(ISTEPS - 1, -1, -1)
    tid = (np.arange(NT)[None, :] * HALF + np.arange(HALF)[:, None]).astype(f)
    NK = -(-TOKENS // G)
    fill = np.zeros((128, 2 * ROW), f)
    fill[:, ROW - 1] = fill[:, 2 * ROW - 1] = EMPTY
    regs = (np.arange(E) * REGION).astype(f)
    return {
        "c_cos": cos_t.reshape(128, -1), "c_sin": sin_t.reshape(128, -1),
        "c_mask": np.ascontiguousarray(mask).reshape(HALF, -1),
        "c_block": blk, "c_ident": np.eye(128, dtype=f),
        "c_before": np.triu(np.ones((HALF, HALF), f), 1),
        "c_steps": np.broadcast_to(steps, (HALF, PSTEPS + ISTEPS)).copy(),
        "c_tid": tid,
        "c_region": np.broadcast_to(regs, (HALF, E)).copy(),
        "c_expert": np.broadcast_to(np.tile(np.arange(E, dtype=f), 2), (HALF, 2 * E)).copy(),
        "c_fill": fill,
        "c_sizes": np.broadcast_to(np.arange(NK, dtype=f) * G, (E, NK)).reshape(1, -1).copy(),
        "c_upto": np.tril(np.ones((E, E), f)).reshape(1, -1),
        "c_group": np.arange(NG, dtype=f).reshape(1, -1),
    }


class Chain:

    def __init__(self, eng, sem):
        self.eng, self.sem, self.n, self.off = eng, sem, 0, None

    def now(self):
        return self.n if self.off is None else self.off + self.n

    def enter(self, i, per):
        self.per, self.base = per, self.n
        self.off = i * per + self.base
        self.n = 0

    def leave(self, passes):
        assert self.n == self.per, (self.n, self.per)
        self.off, self.n = None, self.base + passes * self.per

    def link(self, ins, alone=None):
        self.n += 1
        ins.then_inc(self.sem, 1)
        wait = self.eng.wait_ge(self.sem, self.now())
        if alone is not None:
            wait.then_inc(alone, 1)


def later(r):
    return not isinstance(r, int) or r > 0


def before(r, s, d):
    return (r, s - d) if s >= d else (r - 1, s - d + RING)


def rsqrt(dve, chain, v, y, t):
    chain.link(dve.tensor_scalar(t.bitcast(I32), v.bitcast(I32), 1, None, ALU.logical_shift_right))
    chain.link(dve.tensor_scalar(y.bitcast(I32), t.bitcast(I32), -1, 0x5F3759DF, ALU.mult, ALU.add))
    for _ in range(3):
        chain.link(dve.scalar_tensor_tensor(out=t, in0=y, scalar=-0.5, in1=y, op0=ALU.mult, op1=ALU.mult))
        chain.link(dve.tensor_tensor(t, t, v, ALU.mult))
        chain.link(dve.scalar_tensor_tensor(out=y, in0=t, scalar=1.5, in1=y, op0=ALU.add, op1=ALU.mult))


def tokenize(nc, a, h_dram, bias_dram, xT):
    with ExitStack() as ctx:
        def sb(name, shape, dt=F32):
            return ctx.enter_context(nc.sbuf_tensor("tok_" + name, shape, dt))

        def sem(name):
            return ctx.enter_context(nc.semaphore(name))

        pix = sb("pix", [128, RING, 2, C, KC * B])
        wts = sb("wts", [128, RING, 2, KC, D])
        brow = sb("brow", [1, RING, 2, D])
        mix = sb("mix", [128, RING, 2, KC * B])
        hs = sb("hs", [128, RING, D])
        xn = sb("xn", [128, RING, D])
        st = sb("st", [128, RING, 6])
        mv = sb("mv", [128, RING, 2])
        sd = sb("sd", [128, RING])
        rs = sb("rs", [128, RING])
        eps = sb("eps", [128, 1])
        ones = sb("ones", [1, B])
        ident = sb("ident", [128, 128])
        mwb = sb("mwb", [128, HALF * 2 * C])
        dbias = sb("dbias", [HALF, 2, D])
        mrow = sb("mrow", [HALF, 2, C])
        mbias = sb("mbias", [HALF, 2])
        msum = sb("msum", [HALF, 2])
        banks = [ctx.enter_context(nc.psum_tensor(f"tok{i}", [128, 512], F32)) for i in range(8)]
        HB = [0, 1, 2, 3, 0, 1, 2]
        TB = [4, 5, 6, 4, 5, 6, 7]

        const_in = sem("tok_const_in")
        pair_in = [sem(f"tok_pair_in{s}") for s in range(RING)]
        h_out = [sem(f"tok_h_out{s}") for s in range(RING)]
        bias_made, bias_kept = sem("bias_made"), sem("bias_kept")
        setup, scaled, half_mixed, mixed = sem("tok_setup"), sem("scaled"), sem("half_mixed"), sem("mixed")
        multiplied, h_copied, counted, rooted = sem("multiplied"), sem("h_copied"), sem("counted"), sem("rooted")
        inverted, normed, turned, xt_copied = sem("inverted"), sem("normed"), sem("turned"), sem("xt_copied")
        chain_sem, alone = sem("tok_chain"), sem("tok_alone")

        def back(banks_of, s):
            return next(d for d in range(1, RING + 1) if banks_of[(s - d) % RING] == banks_of[s])

        block = ctx.enter_context(nc.Block())

        @block.sync
        def _(sp):
            sp.dma_start(mwb[:], a["mw_b"]).then_inc(const_in, 16)
            sp.dma_start(dbias[:], a["dec_bias"]).then_inc(const_in, 16)
            sp.dma_start(mrow[:], a["mw_rows"]).then_inc(const_in, 16)
            sp.dma_start(mbias[:], a["merge_bias"]).then_inc(const_in, 16)
            sp.dma_start(ident[:], a["c_ident"]).then_inc(const_in, 16)

            def load(j, s, first):
                sp.dma_start(pix[:, s], a["pixels"][bass.ds(j, 1)].rearrange("o p u c q -> (o p) u c q")).then_inc(pair_in[s], 16)
                sp.dma_start(wts[:, s], a["decode"][bass.ds(j, 1)].rearrange("o p u k f -> (o p) u k f")).then_inc(pair_in[s], 16)
                if first and s == 0:
                    sp.wait_ge(bias_kept, 16)
                sp.dma_start(brow[:, s], bias_dram[bass.ds(j, 1)]).then_inc(pair_in[s], 16)

            def store(j, s):
                for u in range(2):
                    sp.dma_start(h_dram[:, bass.ds(j + u * HALF, 1), :].rearrange("b o f -> b (o f)"),
                                 hs[u * B:(u + 1) * B, s]).then_inc(h_out[s], 16)

            for s in range(RING):
                load(s, s, True)
            with sp.Fori(1, ROUNDS) as r:
                for s in range(RING):
                    sp.wait_ge(multiplied, (r - 1) * RING + (s + 1))
                    load(r * RING + s, s, False)
                    sp.wait_ge(h_copied, (r - 1) * RING + (s + 1))
                    store((r - 1) * RING + s, s)
            for s in range(RING):
                sp.wait_ge(h_copied, (ROUNDS - 1) * RING + s + 1)
                store((ROUNDS - 1) * RING + s, s)
            for s in range(RING):
                sp.wait_ge(h_out[s], 32 * ROUNDS)

        @block.gpsimd
        def _(pool):
            pool.wait_ge(bias_made, 2)
            pool.dma_start(bias_dram.rearrange("i u f -> i (u f)"), dbias[:].rearrange("i u f -> i (u f)")).then_inc(bias_kept, 16)

        @block.scalar
        def _(act):
            act.wait_ge(const_in, 80)
            act.wait_ge(setup, 2)

            def scale_first_channel(r, s):
                act.wait_ge(pair_in[s], r * 48 + 48)
                for u in range(2):
                    ins = act.activation(mix[:, s, u], pix[:, s, u, 0], ACT.Copy,
                                         scale=mwb[:, bass.ds(r * (RING * 2 * C) + (s * 2 + u) * C, 1)])
                ins.then_inc(scaled, 1)

            def copy_h(r, s):
                act.wait_ge(multiplied, r * RING + (s + 1))
                if later(r):
                    act.wait_ge(h_out[s], r * 32)
                act.activation(hs[:, s], banks[HB[s]][:, 0:D], ACT.Copy).then_inc(h_copied, 1)

            def root(r, s):
                act.wait_ge(counted, r * RING + (s + 1))
                act.activation(sd[:, s:s + 1], mv[:, s, 1:2], ACT.Sqrt, bias=eps[:]).then_inc(rooted, 1)

            def copy_xt(r, s):
                act.wait_ge(turned, r * RING + (s + 1))
                for c in range(ND):
                    src = banks[TB[s]][0:DC, c * 128:(c + 1) * 128].rearrange("p (u b) -> p u b", u=2)
                    dst = xT.rearrange("p b c (u i) -> p c u b i", u=2)[:, c, :, :, bass.ds(r * RING + s, 1)]
                    ins = act.activation(dst.rearrange("p u b o -> p u (b o)"), src, ACT.Copy)
                ins.then_inc(xt_copied, 1)

            def step(r, s):
                scale_first_channel(r, s)
                if later(r) or s >= 1:
                    copy_h(*before(r, s, 1))
                if later(r) or s >= 2:
                    root(*before(r, s, 2))
                if later(r) or s >= 4:
                    copy_xt(*before(r, s, 4))

            for r in range(2):
                for s in range(RING):
                    step(r, s)
            with act.Fori(2, ROUNDS) as r:
                for s in range(RING):
                    step(r, s)
            copy_h(ROUNDS - 1, RING - 1)
            for s in range(RING - 2, RING):
                root(ROUNDS - 1, s)
            for s in range(RING - 4, RING):
                copy_xt(ROUNDS - 1, s)

        @block.vector
        def _(dve):
            chain = Chain(dve, chain_sem)
            dve.memset(eps[:], EPS).then_inc(setup, 1)
            dve.memset(ones[:], 1.0).then_inc(setup, 1)
            dve.wait_ge(const_in, 80)
            chain.link(dve.tensor_reduce(msum[:], mrow[:], AX.X, ALU.add))
            for u in range(2):
                dve.tensor_scalar(dbias[:, u], dbias[:, u], msum[:, u:u + 1], mbias[:, u:u + 1],
                                  ALU.mult, ALU.add).then_inc(bias_made, 1)

            def merge_channels(r, s):
                dve.wait_ge(scaled, r * RING + (s + 1))
                for c in range(1, C):
                    for u in range(2):
                        ins = dve.scalar_tensor_tensor(
                            out=mix[:, s, u], in0=pix[:, s, u, c],
                            scalar=mwb[:, bass.ds(r * (RING * 2 * C) + (s * 2 + u) * C + c, 1)],
                            in1=mix[:, s, u], op0=ALU.mult, op1=ALU.add)
                    if c == 1:
                        ins.then_inc(half_mixed, 1)
                        dve.wait_ge(half_mixed, r * RING + (s + 1))
                ins.then_inc(mixed, 1)

            def count(r, s):
                dve.wait_ge(h_copied, r * RING + (s + 1))
                chain.link(dve.bn_stats(st[:, s], hs[:, s]), alone)
                dve.bn_aggr(mv[:, s], st[:, s]).then_inc(counted, 1)

            def normalize(r, s):
                dve.wait_ge(rooted, r * RING + (s + 1))
                dve.reciprocal(rs[:, s:s + 1], sd[:, s:s + 1]).then_inc(inverted, 1)
                dve.wait_ge(inverted, r * RING + (s + 1))
                dve.tensor_scalar(xn[:, s], hs[:, s], mv[:, s, 0:1], rs[:, s:s + 1],
                                  ALU.subtract, ALU.mult).then_inc(normed, 1)

            def step(r, s):
                merge_channels(r, s)
                if later(r) or s >= 1:
                    count(*before(r, s, 1))
                if later(r) or s >= 2:
                    normalize(*before(r, s, 2))

            for s in range(RING):
                step(0, s)
            with dve.Fori(1, ROUNDS) as r:
                chain.enter(r - 1, RING)
                for s in range(RING):
                    step(r, s)
            chain.leave(ROUNDS - 1)
            count(ROUNDS - 1, RING - 1)
            for s in range(RING - 2, RING):
                normalize(ROUNDS - 1, s)

        @block.tensor
        def _(pe):
            pe.wait_ge(const_in, 80)
            pe.wait_ge(setup, 2)

            def product(r, s):
                pe.wait_ge(mixed, r * RING + (s + 1))
                if later(r) or s >= back(HB, s):
                    pe.wait_ge(h_copied, r * RING + (s + 1 - back(HB, s)))
                for u in range(2):
                    out = banks[HB[s]][u * B:(u + 1) * B, 0:D]
                    pe.matmul(out, ones[:], brow[:, s, u], start=True, stop=False)
                    for k in range(KC):
                        ins = pe.matmul(out, mix[:, s, u, k * B:(k + 1) * B], wts[:, s, u, k],
                                        start=False, stop=(k == KC - 1))
                ins.then_inc(multiplied, 1)

            def turn(r, s):
                pe.wait_ge(normed, r * RING + (s + 1))
                if later(r) or s >= back(TB, s):
                    pe.wait_ge(xt_copied, r * RING + (s + 1 - back(TB, s)))
                for c in range(ND):
                    ins = pe.transpose(banks[TB[s]][0:DC, c * 128:(c + 1) * 128], xn[:, s, c * DC:(c + 1) * DC], ident[:])
                ins.then_inc(turned, 1)

            def step(r, s):
                product(r, s)
                if later(r) or s >= 3:
                    turn(*before(r, s, 3))

            for r in range(2):
                for s in range(RING):
                    step(r, s)
            with pe.Fori(2, ROUNDS) as r:
                for s in range(RING):
                    step(r, s)
            for s in range(RING - 3, RING):
                turn(ROUNDS - 1, s)


def attend(nc, a, h_dram, z_dram, xT, prob, count):
    with ExitStack() as ctx:
        def sb(name, shape, dt=F32):
            return ctx.enter_context(nc.sbuf_tensor("att_" + name, shape, dt))

        def sem(name):
            return ctx.enter_context(nc.semaphore(name))

        wq = sb("wq", [DC, ND, H * DQK])
        wk = sb("wk", [DC, ND, H * DQK])
        wv = sb("wv", [DC, ND, H * DV])
        wg = sb("wg", [DC, ND, H * DV])
        wo = sb("wo", [128, NP, D])
        gnw = sb("gnw", [128, NP])
        gnb = sb("gnb", [128, NP])
        sw = sb("sw", [DC, ND, E])
        swb = sb("swb", [HALF, 2, E])
        cos_t = sb("cos_t", [128, 2, 2, N])
        sin_t = sb("sin_t", [128, 2, 2, N])
        mask = sb("mask", [HALF, H, N + HALF])
        block64 = sb("block64", [128, 128])
        ident = sb("ident2", [128, 128])
        earlier = sb("earlier", [HALF, HALF])
        ones = sb("ones2", [HALF, HALF])
        tid = sb("tid", [HALF, NT])
        expert = sb("expert", [HALF, 2, E])

        x = sb("x", [DC, ND, N])
        hres = sb("hres", [HALF, 2, D])
        v = sb("v", [HALF, 2, H * DV])
        swapped = sb("swapped", [128, 3, 2, N])
        straight = sb("straight", [128, 3, 2, N])
        rot = sb("rot", [128, 2 * NP, 2, N])
        sm = sb("sm", [HALF, H, N + HALF])
        cc = sb("cc", [128, NP, N])
        gate = sb("gate", [128, NP, N])
        th = sb("th", [128, NP, N])
        gst = sb("gst", [128, NP, 6])
        gmv = sb("gmv", [128, NP, 2])
        gs = sb("gs", [128, 2, NP])
        gg = sb("gg", [128, 2, NP])
        gv, gy, gt = sb("gv", [128, NP]), sb("gy", [128, NP]), sb("gt", [128, NP])
        ga, gb = sb("ga", [128, NP]), sb("gb", [128, NP])
        row = sb("row", [HALF, 2, ROW])
        lst = sb("lst", [HALF, 2, 6])
        lmv = sb("lmv", [HALF, 2, 2])
        lv, lt, ly = sb("lv", [HALF, 2]), sb("lt", [HALF, 2]), sb("ly", [HALF, 2])
        xf = sb("xf", [HALF, 2, D])
        xfT = sb("xfT", [DC, ND, N])
        z = sb("logits", [HALF, 2, E])
        zmax = sb("zmax", [HALF, 2])
        ez = sb("ez", [HALF, 2, E])
        rank = sb("rank", [HALF, 2, E])
        route = sb("route", [HALF, 2])
        esum = sb("esum", [HALF, 2])
        chosen = sb("chosen", [HALF, 2, E])
        slot = sb("slot", [HALF, 2])
        slot_i = sb("slot_i", [HALF, 2], U32)

        qk_bank = [ctx.enter_context(nc.psum_tensor(f"qk{i}", [128, 512], F32)) for i in range(3)]
        s_bank = [ctx.enter_context(nc.psum_tensor(f"s{i}", [128, 512], F32)) for i in range(2)]
        o_bank = ctx.enter_context(nc.psum_tensor("o_bank", [128, 512], F32))
        ma = ctx.enter_context(nc.psum_tensor("ma", [128, 512], F32))
        mb = ctx.enter_context(nc.psum_tensor("mb", [128, 512], F32))

        weights_in, ones_made = sem("weights_in"), sem("ones_made")
        x_in = sem("x_in")
        res_in, res_used = sem("res_in"), sem("res_used")
        v_made, v_copied = sem("v_made"), sem("v_copied")
        g_made, g_tanh, g_gated = sem("g_made"), sem("g_tanh"), sem("g_gated")
        qk_made, qk_swapped, qk_straight, qk_turned, qk_rotated = (
            sem("qk_made"), sem("qk_swapped"), sem("qk_straight"), sem("qk_turned"), sem("qk_rotated"))
        s_made, s_decayed = sem("s_made"), sem("s_decayed")
        o_made, o_copied, stats_ready, stats_summed, stats_read = (
            sem("o_made"), sem("o_copied"), sem("stats_ready"), sem("stats_summed"), sem("stats_read"))
        gated_ready, wo_made = sem("gated_ready"), sem("wo_made")
        xf_ready, xf_turned, xfT_copied = sem("xf_ready"), sem("xf_turned"), sem("xfT_copied")
        z_made, z_shifted, z_exped = sem("z_made"), sem("z_shifted"), sem("z_exped")
        chosen_ready, prefix_made, prefix_read = sem("chosen_ready"), sem("prefix_made"), sem("prefix_read")
        slots_ready, rows_out = sem("slots_ready"), sem("rows_out")
        chain_sem, alone = sem("att_chain"), sem("att_alone")

        block = ctx.enter_context(nc.Block())
        weight_loads = [(wq, "Wq"), (wk, "Wk"), (wv, "Wv"), (wg, "Wg"), (wo, "Wo"), (gnw, "gn_w"), (gnb, "gn_b"),
                        (sw, "sw"), (swb, "sb"), (cos_t, "c_cos"), (sin_t, "c_sin"), (mask, "c_mask"),
                        (block64, "c_block"), (ident, "c_ident"), (earlier, "c_before"), (tid, "c_tid"),
                        (expert, "c_expert"), (count, "c_region")]
        ALL_IN = 16 * len(weight_loads)

        def flat(t):
            ap = t[:] if len(t.shape) == 2 else t[:].rearrange(
                {3: "p x y -> p (x y)", 4: "p x y z -> p (x y z)"}[len(t.shape)])
            return ap

        @block.sync
        def _(sp):
            for t, name in weight_loads:
                src = a[name] if len(a[name].shape) == 2 else a[name].rearrange("p x y -> p (x y)")
                sp.dma_start(flat(t), src).then_inc(weights_in, 16)

            def load_x(b):
                sp.dma_start(x[:], xT[:, bass.ds(b, 1)].rearrange("p o c n -> p (o c) n")).then_inc(x_in, 16)

            def load_residual(b):
                sp.dma_start(hres[:], h_dram[bass.ds(b, 1)].rearrange("o (t p) f -> p (o t) f", t=2)).then_inc(res_in, 16)

            load_x(0)
            load_residual(0)
            with sp.Fori(1, B) as b:
                sp.wait_ge(qk_made, b * 6)
                load_x(b)
                sp.wait_ge(res_used, b)
                load_residual(b)

        @block.tensor
        def _(pe):
            pe.wait_ge(weights_in, ALL_IN)
            pe.wait_ge(ones_made, 1)

            def values(b, t):
                if t == 0:
                    pe.wait_ge(x_in, b * 16 + 16)
                bank = (ma, mb)[t]
                if later(b - 1):
                    pe.wait_ge((z_shifted, prefix_read)[t], b - 1)
                for c in range(ND):
                    ins = pe.matmul(bank[0:HALF, 0:H * DV], x[:, c, t * HALF:(t + 1) * HALF], wv[:, c],
                                    start=(c == 0), stop=(c == ND - 1))
                ins.then_inc(v_made, 1)

            def gates(b, part):
                if part == 0:
                    if later(b):
                        pe.wait_ge(stats_read, b)
                    else:
                        pe.wait_ge(v_copied, 1)
                else:
                    pe.wait_ge(v_copied, b * 2 + 2)
                bank = (ma, mb)[part]
                for n, m in enumerate(((0, 1), (2,))[part]):
                    for c in range(ND):
                        ins = pe.matmul(bank[:, n * N:(n + 1) * N], wg[:, c, m * 128:(m + 1) * 128], x[:, c],
                                        start=(c == 0), stop=(c == ND - 1))
                ins.then_inc(g_made, 1)

            def project(b, n):
                if later(b) or n >= 3:
                    pe.wait_ge(qk_straight, b * 6 + (n - 2))
                w = (wq, wk)[n % 2]
                for i in range(2):
                    h = n // 2 * 2 + i
                    for c in range(ND):
                        ins = pe.matmul(qk_bank[n % 3][:, i * N:(i + 1) * N], w[:, c, h * DQK:(h + 1) * DQK], x[:, c],
                                        start=(c == 0), stop=(c == ND - 1))
                ins.then_inc(qk_made, 1)

            def scores(b, p):
                pe.wait_ge(qk_rotated, b * 6 + (2 * p + 2))
                for i in range(2):
                    h = 2 * p + i
                    if later(b) or h >= 2:
                        pe.wait_ge(s_decayed, b * 6 + (h - 1))
                    q, k = rot[:, 2 * p, i], rot[:, 2 * p + 1, i]
                    pe.matmul(s_bank[i][0:HALF, 0:N], k[:, 0:HALF], q[:, 0:N], start=True, stop=True)
                    pe.matmul(s_bank[i][0:HALF, N:N + HALF], k[:, HALF:N], q[:, HALF:N],
                              start=True, stop=True).then_inc(s_made, 1)

            def outputs(b, p):
                pe.wait_ge(s_decayed, b * 6 + (2 * p + 2))
                if later(b) or p >= 1:
                    pe.wait_ge(o_copied, b * 3 + p)
                for i in range(2):
                    h = 2 * p + i
                    at = slice(i * DV, (i + 1) * DV)
                    pe.matmul(o_bank[at, 0:N], v[:, 0, h * DV:(h + 1) * DV], sm[:, h, 0:N], start=True, stop=False)
                    ins = pe.matmul(o_bank[at, HALF:N], v[:, 1, h * DV:(h + 1) * DV], sm[:, h, N:N + HALF],
                                    start=False, stop=True)
                ins.then_inc(o_made, 1)

            def group_statistics(b, last):
                pe.wait_ge(stats_ready, b + 1)
                if last:
                    pe.wait_ge(z_shifted, b)
                else:
                    pe.wait_ge(v_copied, b * 2 + 3)
                pe.matmul(ma[:, 0:2 * NP], block64[:], gs[:].rearrange("p x y -> p (x y)"),
                          start=True, stop=True).then_inc(stats_summed, 1)

            def project_out(b, last):
                pe.wait_ge(gated_ready, b + 1)
                if not last:
                    pe.wait_ge(g_gated, b * 2 + 3)
                for t in range(2):
                    for m in range(NP):
                        ins = pe.matmul(ma[0:HALF, t * D:(t + 1) * D], cc[:, m, t * HALF:(t + 1) * HALF], wo[:, m],
                                        start=(m == 0), stop=(m == NP - 1))
                ins.then_inc(wo_made, 1)

            def turn(b, last):
                pe.wait_ge(xf_ready, b + 1)
                if last:
                    pe.wait_ge(prefix_read, b)
                else:
                    pe.wait_ge(g_gated, b * 2 + 4)
                for c in range(ND):
                    for t in range(2):
                        ins = pe.transpose(mb[0:DC, c * N + t * HALF:c * N + (t + 1) * HALF],
                                           xf[:, t, c * DC:(c + 1) * DC], ident[0:HALF, 0:HALF])
                ins.then_inc(xf_turned, 1)

            def logits(b):
                pe.wait_ge(xfT_copied, b + 1)
                for t in range(2):
                    for c in range(ND):
                        ins = pe.matmul(ma[0:HALF, t * E:(t + 1) * E], xfT[:, c, t * HALF:(t + 1) * HALF], sw[:, c],
                                        start=(c == 0), stop=(c == ND - 1))
                ins.then_inc(z_made, 1)

            def prefix(b):
                pe.wait_ge(chosen_ready, b + 1)
                one, two = chosen[:, 0], chosen[:, 1]
                pe.matmul(mb[0:HALF, 0:2 * E], earlier[:], chosen[:].rearrange("p t e -> p (t e)"), start=True, stop=False)
                pe.matmul(mb[0:HALF, E:2 * E], ones[:], one, start=False, stop=True)
                pe.matmul(mb[0:HALF, 2 * E:3 * E], ones[:], one, start=True, stop=False)
                pe.matmul(mb[0:HALF, 2 * E:3 * E], ones[:], two, start=False, stop=True).then_inc(prefix_made, 1)

            def image(b, tail):
                values(b, 0)
                values(b, 1)
                if tail is not None:
                    group_statistics(tail, False)
                project(b, 0)
                project(b, 1)
                gates(b, 0)
                gates(b, 1)
                project(b, 2)
                if tail is not None:
                    project_out(tail, False)
                project(b, 3)
                scores(b, 0)
                project(b, 4)
                project(b, 5)
                if tail is not None:
                    turn(tail, False)
                outputs(b, 0)
                scores(b, 1)
                if tail is not None:
                    logits(tail)
                outputs(b, 1)
                scores(b, 2)
                if tail is not None:
                    prefix(tail)
                outputs(b, 2)

            image(0, None)
            image(1, 0)
            with pe.Fori(2, B) as b:
                image(b, b - 1)
            group_statistics(B - 1, True)
            project_out(B - 1, True)
            turn(B - 1, True)
            logits(B - 1)
            prefix(B - 1)

        @block.scalar
        def _(act):
            def image(b, tail):
                for t in range(2):
                    act.wait_ge(v_made, b * 2 + (t + 1))
                    if later(b):
                        act.wait_ge(o_made, b * 3)
                    act.activation(v[:, t], (ma, mb)[t][0:HALF, 0:H * DV], ACT.Copy).then_inc(v_copied, 1)
                for n in range(2 * NP):
                    act.wait_ge(qk_made, b * 6 + (n + 1))
                    if later(b) or n >= 3:
                        act.wait_ge(qk_rotated, b * 6 + (n - 2))
                    src = qk_bank[n % 3][:, 0:2 * N].rearrange("p (i n) -> p i n", i=2)
                    act.activation(swapped[0:64, n % 3], src[64:128], ACT.Copy)
                    act.activation(swapped[64:128, n % 3], src[0:64], ACT.Copy).then_inc(qk_swapped, 1)
                    if n == 1:
                        for part in range(2):
                            act.wait_ge(g_made, b * 2 + (part + 1))
                            if later(b):
                                act.wait_ge(g_gated, b * 2 + part)
                            dst, src = ((th[:, 0:2], ma[:, 0:2 * N].rearrange("p (i n) -> p i n", i=2)),
                                        (th[:, 2], mb[:, 0:N]))[part]
                            act.activation(dst, src, ACT.Tanh, scale=0.5).then_inc(g_tanh, 1)
                if tail is not None:
                    copy_xfT(tail)
                copy_outputs(b, 0)
                if tail is not None:
                    exponentiate(tail)
                copy_outputs(b, 1)
                copy_outputs(b, 2)

            def copy_outputs(b, p):
                act.wait_ge(o_made, b * 3 + (p + 1))
                if later(b):
                    act.wait_ge(wo_made, b)
                act.activation(cc[:, p], o_bank[:, 0:N], ACT.Copy).then_inc(o_copied, 1)

            def copy_xfT(b):
                act.wait_ge(xf_turned, b + 1)
                act.activation(xfT[:].rearrange("p c n -> p (c n)"), mb[0:DC, 0:ND * N], ACT.Copy).then_inc(xfT_copied, 1)

            def exponentiate(b):
                act.wait_ge(z_shifted, b + 1)
                act.activation(ez[:], z[:], ACT.Exp).then_inc(z_exped, 1)

            image(0, None)
            with act.Fori(1, B) as b:
                image(b, b - 1)
            copy_xfT(B - 1)
            exponentiate(B - 1)

        @block.gpsimd
        def _(pool):
            pool.wait_ge(weights_in, ALL_IN)

            def rotate(b, n):
                pool.wait_ge(qk_swapped, b * 6 + (n + 1))
                pool.tensor_tensor(swapped[:, n % 3], swapped[:, n % 3], sin_t[:, n % 2], ALU.mult).then_inc(qk_turned, 1)
                pool.wait_ge(qk_turned, b * 6 + (n + 1))
                pool.wait_ge(qk_straight, b * 6 + (n + 1))
                if later(b):
                    pool.wait_ge(s_made, b * 6)
                pool.tensor_tensor(rot[:, n], straight[:, n % 3], swapped[:, n % 3], ALU.add).then_inc(qk_rotated, 1)

            def dispatch(b):
                pool.wait_ge(slots_ready, b + 1).then_inc(alone, 1)
                for t in range(2):
                    pool.indirect_dma_start(z_dram, bass.IndirectOffsetOnAxis(ap=slot_i[:, t:t + 1], axis=0),
                                            row[:, t], None).then_inc(rows_out, 16)

            def image(b):
                for n in range(2 * NP):
                    rotate(b, n)

            image(0)
            with pool.Fori(1, B) as b:
                image(b)
                dispatch(b - 1)
            dispatch(B - 1)
            pool.wait_ge(rows_out, 32 * B)

        @block.vector
        def _(dve):
            chain = Chain(dve, chain_sem)
            dve.memset(ones[:], 1.0).then_inc(ones_made, 1)
            dve.wait_ge(weights_in, ALL_IN)

            def apply_groupnorm(b):
                dve.wait_ge(stats_summed, b + 1)
                dve.tensor_copy(gg[:].rearrange("p x y -> p (x y)"), ma[:, 0:2 * NP]).then_inc(stats_read, 1)
                dve.wait_ge(stats_read, b + 1)
                chain.link(dve.tensor_tensor(gt[:], gg[:, 0], gg[:, 0], ALU.mult))
                chain.link(dve.tensor_tensor(gv[:], gg[:, 1], gt[:], ALU.subtract))
                chain.link(dve.tensor_scalar(gv[:], gv[:], 0.0, EPS, ALU.max, ALU.add))
                rsqrt(dve, chain, gv[:], gy[:], gt[:])
                chain.link(dve.tensor_tensor(ga[:], gy[:], gnw[:], ALU.mult))
                chain.link(dve.tensor_tensor(gb[:], gg[:, 0], ga[:], ALU.mult))
                chain.link(dve.tensor_tensor(gb[:], gnb[:], gb[:], ALU.subtract))
                for p in range(NP):
                    last = dve.tensor_scalar(cc[:, p], cc[:, p], ga[:, p:p + 1], gb[:, p:p + 1], ALU.mult, ALU.add)
                chain.link(last)
                dve.scalar_tensor_tensor(out=cc[:], in0=cc[:], scalar=0.5, in1=gate[:], op0=ALU.mult,
                                         op1=ALU.mult).then_inc(gated_ready, 1)

            def gates(b):
                for part in range(2):
                    dve.wait_ge(g_tanh, b * 2 + (part + 1))
                    if later(b):
                        dve.wait_ge(gated_ready, b)
                    dst, t, src = ((gate[:, 0:2], th[:, 0:2], ma[:, 0:2 * N].rearrange("p (i n) -> p i n", i=2)),
                                   (gate[:, 2], th[:, 2], mb[:, 0:N]))[part]
                    dve.scalar_tensor_tensor(out=dst, in0=t, scalar=1.0, in1=src, op0=ALU.add,
                                             op1=ALU.mult).then_inc(g_gated, 1)

            def straighten(b, n):
                dve.wait_ge(qk_swapped, b * 6 + (n + 1))
                if later(b) or n >= 3:
                    dve.wait_ge(qk_rotated, b * 6 + (n - 2))
                dve.tensor_tensor(straight[:, n % 3], qk_bank[n % 3][:, 0:2 * N].rearrange("p (i n) -> p i n", i=2),
                                  cos_t[:, n % 2], ALU.mult).then_inc(qk_straight, 1)

            def decay(b, p):
                for i in range(2):
                    h = 2 * p + i
                    dve.wait_ge(s_made, b * 6 + (h + 1))
                    if later(b):
                        dve.wait_ge(o_made, b * 3)
                    dve.tensor_tensor(sm[:, h], s_bank[i][0:HALF, 0:N + HALF], mask[:, h], ALU.mult).then_inc(s_decayed, 1)

            def output_statistics(b, p):
                dve.wait_ge(o_copied, b * 3 + (p + 1))
                chain.link(dve.bn_stats(gst[:, p], cc[:, p]), alone)
                chain.link(dve.bn_aggr(gmv[:, p], gst[:, p]))

            def prepare_statistics():
                chain.link(dve.tensor_copy(gs[:, 0], gmv[:, :, 0]))
                chain.link(dve.tensor_tensor(gs[:, 1], gs[:, 0], gs[:, 0], ALU.mult))
                dve.tensor_tensor(gs[:, 1], gs[:, 1], gmv[:, :, 1], ALU.add).then_inc(stats_ready, 1)

            def second_layernorm(b):
                dve.wait_ge(wo_made, b + 1)
                dve.wait_ge(res_in, b * 16 + 16)
                if later(b):
                    dve.wait_ge(rows_out, b * 32)
                ins = dve.tensor_tensor(row[:, :, 0:D], ma[0:HALF, 0:2 * D].rearrange("p (t f) -> p t f", t=2),
                                        hres[:], ALU.add)
                ins.then_inc(res_used, 1)
                dve.wait_ge(res_used, b + 1)
                for t in range(2):
                    last = dve.bn_stats(lst[:, t], row[:, t, 0:D])
                chain.link(last, alone)
                for t in range(2):
                    last = dve.bn_aggr(lmv[:, t], lst[:, t])
                chain.link(last)
                dve.tensor_copy(row[:, :, D], lmv[:, :, 0])
                chain.link(dve.tensor_scalar(lv[:], lmv[:, :, 1], EPS, None, ALU.add))
                rsqrt(dve, chain, lv[:], ly[:], lt[:])
                chain.link(dve.tensor_copy(row[:, :, D + 1], ly[:]))
                for t in range(2):
                    last = dve.tensor_scalar(xf[:, t], row[:, t, 0:D], lmv[:, t, 0:1], ly[:, t:t + 1],
                                             ALU.subtract, ALU.mult)
                last.then_inc(xf_ready, 1)

            def route_tokens(b):
                dve.wait_ge(z_made, b + 1)
                chain.link(dve.tensor_tensor(z[:], ma[0:HALF, 0:2 * E].rearrange("p (t e) -> p t e", t=2), swb[:], ALU.add))
                chain.link(dve.tensor_reduce(zmax[:], z[:], AX.X, ALU.max))
                dve.tensor_tensor(z[:], z[:], zmax[:].unsqueeze(2).broadcast_to([HALF, 2, E]),
                                  ALU.subtract).then_inc(z_shifted, 1)
                dve.wait_ge(z_shifted, b + 1)
                chain.link(dve.tensor_scalar(rank[:], z[:], 0.0, float(E), ALU.is_lt, ALU.mult))
                chain.link(dve.tensor_tensor(rank[:], rank[:], expert[:], ALU.add))
                chain.link(dve.tensor_reduce(route[:], rank[:], AX.X, ALU.min))
                dve.tensor_tensor(chosen[:], expert[:], route[:].unsqueeze(2).broadcast_to([HALF, 2, E]),
                                  ALU.is_equal).then_inc(chosen_ready, 1)
                dve.wait_ge(z_exped, b + 1)
                chain.link(dve.tensor_reduce(esum[:], ez[:], AX.X, ALU.add))
                chain.link(dve.reciprocal(row[:, :, D + 2], esum[:]))
                dve.wait_ge(chosen_ready, b + 1)
                dve.tensor_tensor(prob.rearrange("p e t -> p t e")[:, bass.ds(b * 2, 2), :], chosen[:],
                                  row[:, :, D + 2:D + 3].broadcast_to([HALF, 2, E]), ALU.mult)
                chain.link(dve.tensor_copy(row[:, :, D + 3], tid[:, bass.ds(b * 2, 2)]))

            def place_tokens(b):
                dve.wait_ge(prefix_made, b + 1)
                free = count[:].unsqueeze(1).broadcast_to([HALF, 2, E])
                chain.link(dve.tensor_tensor(rank[:], mb[0:HALF, 0:2 * E].rearrange("p (t e) -> p t e", t=2), free, ALU.add))
                chain.link(dve.tensor_tensor(rank[:], rank[:], chosen[:], ALU.mult))
                chain.link(dve.tensor_reduce(slot[:], rank[:], AX.X, ALU.add))
                dve.tensor_tensor(count[:], count[:], mb[0:HALF, 2 * E:3 * E], ALU.add).then_inc(prefix_read, 1)
                dve.wait_ge(prefix_read, b + 1)
                dve.tensor_copy(slot_i[:], slot[:]).then_inc(slots_ready, 1)

            def image(b, tail):
                if tail is not None:
                    apply_groupnorm(tail)
                gates(b)
                for n in range(3):
                    straighten(b, n)
                if tail is not None:
                    second_layernorm(tail)
                straighten(b, 3)
                decay(b, 0)
                straighten(b, 4)
                straighten(b, 5)
                decay(b, 1)
                if tail is not None:
                    route_tokens(tail)
                output_statistics(b, 0)
                decay(b, 2)
                output_statistics(b, 1)
                if tail is not None:
                    place_tokens(tail)
                output_statistics(b, 2)
                prepare_statistics()

            image(0, None)
            image(1, 0)
            with dve.Fori(2, B) as b:
                chain.enter(b - 2, PER_IMAGE)
                image(b, b - 1)
            chain.leave(B - 2)
            apply_groupnorm(B - 1)
            second_layernorm(B - 1)
            route_tokens(B - 1)
            place_tokens(B - 1)


PER_IMAGE = 52


def find_limits(nc, a, z_dram, limits_dram, prob, count, groups):
    with ExitStack() as ctx:
        def sb(name, shape, dt=F32):
            return ctx.enter_context(nc.sbuf_tensor("lim_" + name, shape, dt))

        def sem(name):
            return ctx.enter_context(nc.semaphore(name))

        NK = a["c_sizes"].shape[1] // E
        SPAN = 16
        steps = sb("steps", [HALF, PSTEPS + ISTEPS])
        region = sb("region", [HALF, E])
        tid = sb("tid", [HALF, NT])
        sizes = sb("sizes", [1, E, NK])
        upto = sb("upto", [1, E, E])
        number = sb("number", [1, NG])
        fill = sb("fill", [128, 2, ROW])
        ones = sb("ones", [HALF, HALF], BF16)
        hit = sb("hit", [HALF, E, NT], BF16)
        unlike = sb("unlike", [HALF, E, NT])
        late = sb("late", [HALF, E, NT])
        hits = sb("hits", [HALF, E])
        limit = sb("limit", [HALF, E, 2])
        trial = sb("trial", [HALF, E])
        good = sb("good", [HALF, E])
        short = sb("short", [HALF, E])
        kept = sb("kept", [1, E])
        over = sb("over", [1, E, NK])
        ng = sb("ng", [1, E])
        below = sb("below", [1, E, E])
        cum = sb("cum", [1, E])
        past = sb("past", [1, NG, E])
        first = sb("first", [1, NG])
        g_e = sb("g_e", [1, NG])
        g_row = sb("g_row", [1, NG])
        valid = sb("valid", [1, NG])
        ends = sb("ends", [1, E + 1], I32)
        total = ctx.enter_context(nc.psum_tensor("total", [128, 512], F32))

        tables_in, ones_made, counted, summed = sem("tables_in"), sem("lim_ones"), sem("lim_counted"), sem("lim_summed")
        chain_sem, ends_ready, limits_ready = sem("lim_chain"), sem("ends_ready"), sem("limits_ready")
        filled, limits_out = sem("filled"), sem("limits_out")
        block = ctx.enter_context(nc.Block())

        @block.sync
        def _(sp):
            for t, name in ((steps[:], "c_steps"), (region[:], "c_region"), (tid[:], "c_tid"),
                            (sizes[:].rearrange("p x y -> p (x y)"), "c_sizes"),
                            (upto[:].rearrange("p x y -> p (x y)"), "c_upto"), (number[:], "c_group"),
                            (fill[:].rearrange("p x y -> p (x y)"), "c_fill")):
                sp.dma_start(t, a[name]).then_inc(tables_in, 16)
            sp.wait_ge(tables_in, 112)
            sp.wait_ge(ends_ready, 1)
            for e in range(E + 1):
                end = sp.value_load(ends[0:1, e:e + 1], min_val=0, max_val=ZROWS - G)
                sp.dma_start(z_dram[bass.ds(end, G)].rearrange("(t p) f -> p t f", t=2), fill[:]).then_inc(filled, 16)
            sp.wait_ge(limits_ready, 1)
            sp.dma_start(limits_dram.rearrange("e x -> (e x)").unsqueeze(0),
                         limit[0:1].rearrange("p e x -> p (e x)")).then_inc(limits_out, 16)
            sp.wait_ge(filled, 16 * (E + 1))
            sp.wait_ge(limits_out, 16)

        @block.tensor
        def _(pe):
            pe.wait_ge(ones_made, 1)
            with pe.Fori(0, PSTEPS + 1 + ISTEPS) as i:
                pe.wait_ge(counted, i + 1)
                for k in range(NT // SPAN):
                    ins = pe.matmul(total[0:HALF, 0:E * SPAN], ones[:], hit[:, :, k * SPAN:(k + 1) * SPAN],
                                    start=(k == 0), stop=(k == NT // SPAN - 1))
                ins.then_inc(summed, 1)

        @block.vector
        def _(dve):
            chain = Chain(dve, chain_sem)
            wide = [HALF, E, NT]

            def count_hits(i, op, table, bound):
                dve.tensor_tensor(hit[:], table, bound.unsqueeze(2).broadcast_to(wide), op).then_inc(counted, 1)
                dve.wait_ge(summed, i + 1)
                chain.link(dve.tensor_reduce(hits[:], total[0:HALF, 0:E * SPAN].rearrange("p (e k) -> p e k", e=E),
                                             AX.X, ALU.add))

            dve.memset(ones[:], 1.0).then_inc(ones_made, 1)
            chain.link(dve.memset(limit[:], 0.0))
            dve.wait_ge(tables_in, 112)
            dve.tensor_copy(ends[:, 0:E], count[0:1])
            dve.memset(ends[:, E:E + 1], E * REGION).then_inc(ends_ready, 1)

            chain.link(dve.tensor_tensor(kept[:], count[0:1], region[0:1], ALU.subtract))
            chain.link(dve.tensor_tensor(over[:], kept[:].unsqueeze(2).broadcast_to([1, E, NK]), sizes[:], ALU.is_gt))
            chain.link(dve.tensor_reduce(ng[:], over[:], AX.X, ALU.add))
            chain.link(dve.tensor_tensor(below[:], upto[:], ng[:].unsqueeze(1).broadcast_to([1, E, E]), ALU.mult))
            chain.link(dve.tensor_reduce(cum[:], below[:], AX.X, ALU.add))
            chain.link(dve.tensor_tensor(past[:], number[:].unsqueeze(2).broadcast_to([1, NG, E]),
                                         cum[:].unsqueeze(1).broadcast_to([1, NG, E]), ALU.is_ge))
            chain.link(dve.tensor_reduce(g_e[:], past[:], AX.X, ALU.add))
            chain.link(dve.tensor_tensor(past[:], past[:], ng[:].unsqueeze(1).broadcast_to([1, NG, E]), ALU.mult))
            chain.link(dve.tensor_reduce(first[:], past[:], AX.X, ALU.add))
            chain.link(dve.tensor_tensor(first[:], number[:], first[:], ALU.subtract))
            chain.link(dve.tensor_scalar(valid[:], g_e[:], float(E), float(G), ALU.is_lt, ALU.mult))
            chain.link(dve.tensor_tensor(first[:], first[:], valid[:], ALU.mult))
            chain.link(dve.tensor_scalar(g_row[:], g_e[:], float(REGION), None, ALU.mult))
            chain.link(dve.tensor_tensor(g_row[:], g_row[:], first[:], ALU.add))
            chain.link(dve.tensor_copy(groups[:, :, 1], g_row[:]))
            chain.link(dve.tensor_scalar(groups[:, :, 0], g_e[:], float(E - 1), None, ALU.min))

            with dve.Fori(0, PSTEPS) as i:
                chain.enter(i, 4)
                step = steps[:, bass.ds(i, 1)]
                chain.link(dve.tensor_scalar(trial[:], limit[:, :, 0], step, None, ALU.add))
                count_hits(i, ALU.is_ge, prob, trial[:])
                chain.link(dve.tensor_scalar(good[:], hits[:], float(CAP), None, ALU.is_ge))
                chain.link(dve.scalar_tensor_tensor(out=limit[:, :, 0], in0=good[:], scalar=step, in1=limit[:, :, 0],
                                                    op0=ALU.mult, op1=ALU.add))
            chain.leave(PSTEPS)
            count_hits(PSTEPS, ALU.is_gt, prob, limit[:, :, 0])
            chain.link(dve.tensor_scalar(short[:], hits[:], -1.0, float(CAP), ALU.mult, ALU.add))
            chain.link(dve.tensor_tensor(unlike[:], prob, limit[:, :, 0:1].broadcast_to(wide), ALU.not_equal))
            chain.link(dve.scalar_tensor_tensor(out=late[:], in0=unlike[:], scalar=2 * EMPTY,
                                                in1=tid[:].unsqueeze(1).broadcast_to(wide), op0=ALU.mult, op1=ALU.add))
            with dve.Fori(0, ISTEPS) as i:
                chain.enter(i, 4)
                step = steps[:, bass.ds(i + PSTEPS, 1)]
                chain.link(dve.tensor_scalar(trial[:], limit[:, :, 1], step, None, ALU.add))
                count_hits(i + (PSTEPS + 1), ALU.is_lt, late[:], trial[:])
                chain.link(dve.tensor_tensor(good[:], hits[:], short[:], ALU.is_lt))
                chain.link(dve.scalar_tensor_tensor(out=limit[:, :, 1], in0=good[:], scalar=step, in1=limit[:, :, 1],
                                                    op0=ALU.mult, op1=ALU.add))
            chain.leave(ISTEPS)
            dve.tensor_scalar(limit[:, :, 1], limit[:, :, 1], 1.0, None, ALU.add).then_inc(limits_ready, 1)


def experts(nc, a, z_dram, limits_dram, groups, out):
    with ExitStack() as ctx:
        def sb(name, shape, dt=F32):
            return ctx.enter_context(nc.sbuf_tensor("ffn_" + name, shape, dt))

        def sem(name):
            return ctx.enter_context(nc.semaphore(name))

        T = G // 128
        S = SLOTS
        w1 = sb("w1", [DC, S, ND, F])
        w2 = sb("w2", [128, S, FM, D])
        b1 = sb("b1", [128, S, FM])
        b2 = sb("b2", [128, S, D])
        lim = sb("lim", [128, S, 2])
        rows = sb("rows", [128, S, T, ROW])
        xf = sb("xf", [128, S, T, D])
        xfT = sb("xfT", [DC, S, ND, G])
        hid = sb("hid", [128, S, FM, G])
        base = sb("base", [128, S, T, D])
        made = sb("made", [128, S, T, D])
        y = sb("y", [128, S, T, D])
        token = sb("token", [128, S, T], U32)
        above = sb("above", [128, S, T])
        same = sb("same", [128, S, T])
        mine = sb("mine", [128, S, T])
        rest = sb("rest", [128, S, T])
        ident = sb("ident", [128, 128])

        h_bank = [ctx.enter_context(nc.psum_tensor(f"ffn_h{i}", [128, 512], F32)) for i in range(3)]
        o_bank = [ctx.enter_context(nc.psum_tensor(f"ffn_o{i}", [128, 512], F32)) for i in range(2)]
        x_bank = [ctx.enter_context(nc.psum_tensor(f"ffn_x{i}", [128, 512], F32)) for i in range(2)]

        ident_in = sem("ident_in")
        group_in = [sem(f"group_in{s}") for s in range(S)]
        xf_made, xf_turned, xfT_copied = sem("ffn_xf_made"), sem("ffn_xf_turned"), sem("ffn_xfT_copied")
        h_made, h_active, o_made = sem("ffn_h_made"), sem("ffn_h_active"), sem("ffn_o_made")
        o_read, y_made = sem("ffn_o_read"), sem("ffn_y_made")
        y_out = [sem(f"ffn_y_out{s}") for s in range(S)]
        chain_sem, alone = sem("ffn_chain"), sem("ffn_alone")
        block = ctx.enter_context(nc.Block())
        LOADS = 6 * 16

        def group_of(i, s):
            return i * S + s

        @block.sync
        def _(sp):
            sp.dma_start(ident[:], a["c_ident"]).then_inc(ident_in, 16)

            def load(g, s):
                e = sp.value_load(groups[0:1, bass.ds(g, 1), 0], min_val=0, max_val=E - 1)
                r = sp.value_load(groups[0:1, bass.ds(g, 1), 1], min_val=0, max_val=ZROWS - G)
                sp.dma_start(rows[:, s], z_dram[bass.ds(r, G)].rearrange("(t p) f -> p t f", p=128)).then_inc(group_in[s], 16)
                sp.dma_start(w1[:, s], a["w1"][bass.ds(e, 1)].rearrange("o p c f -> (o p) c f")).then_inc(group_in[s], 16)
                sp.dma_start(w2[:, s], a["w2"][bass.ds(e, 1)].rearrange("o p m f -> (o p) m f")).then_inc(group_in[s], 16)
                sp.dma_start(b1[:, s], a["b1"][bass.ds(e, 1)].rearrange("o p m -> (o p) m")).then_inc(group_in[s], 16)
                sp.dma_start(b2[:, s], a["b2"][bass.ds(e, 1)].rearrange("o p f -> (o p) f")).then_inc(group_in[s], 16)
                sp.dma_start(lim[:, s], limits_dram[bass.ds(e, 1)].broadcast_to([128, 2])).then_inc(group_in[s], 16)

            for s in range(S):
                load(s, s)
            with sp.Fori(1, NG // S) as i:
                for s in range(S):
                    sp.wait_ge(y_made, i * S + (s + 1 - S))
                    load(i * S + s, s)

        @block.vector
        def _(dve):
            chain = Chain(dve, chain_sem)

            def normalize(i, s):
                dve.wait_ge(group_in[s], i * LOADS + LOADS)
                for t in range(T):
                    ins = dve.tensor_scalar(xf[:, s, t], rows[:, s, t, 0:D], rows[:, s, t, D:D + 1],
                                            rows[:, s, t, D + 1:D + 2], ALU.subtract, ALU.mult)
                ins.then_inc(xf_made, 1)

            def weigh(i, s):
                p, number = rows[:, s, :, D + 2], rows[:, s, :, D + 3]
                if later(i):
                    dve.wait_ge(y_out[s], i * (T * 16))
                dve.tensor_copy(token[:, s], number)
                dve.tensor_scalar(above[:, s], p, lim[:, s, 0:1], None, ALU.is_gt)
                chain.link(dve.tensor_scalar(same[:, s], p, lim[:, s, 0:1], None, ALU.is_equal))
                chain.link(dve.scalar_tensor_tensor(out=same[:, s], in0=number, scalar=lim[:, s, 1:2], in1=same[:, s],
                                                    op0=ALU.is_lt, op1=ALU.mult))
                chain.link(dve.tensor_tensor(above[:, s], above[:, s], same[:, s], ALU.add))
                chain.link(dve.tensor_tensor(mine[:, s], p, above[:, s], ALU.mult))
                chain.link(dve.tensor_tensor(rest[:, s], p, mine[:, s], ALU.subtract))
                for t in range(T):
                    ins = dve.scalar_tensor_tensor(out=base[:, s, t], in0=xf[:, s, t], scalar=rest[:, s, t:t + 1],
                                                   in1=rows[:, s, t, 0:D], op0=ALU.mult, op1=ALU.add)
                chain.link(ins)

            def combine(i, s):
                dve.wait_ge(o_made, group_of(i, s) + 1)
                src = o_bank[s % 2][:, 0:T * D].rearrange("p (t f) -> p t f", t=T)
                dve.tensor_tensor(made[:, s], src, b2[:, s].unsqueeze(1).broadcast_to([128, T, D]),
                                  ALU.add).then_inc(o_read, 1)
                dve.wait_ge(o_read, group_of(i, s) + 1)
                for t in range(T):
                    ins = dve.scalar_tensor_tensor(out=y[:, s, t], in0=made[:, s, t], scalar=mine[:, s, t:t + 1],
                                                   in1=base[:, s, t], op0=ALU.mult, op1=ALU.add)
                ins.then_inc(y_made, 1)

            def group(i, s):
                weigh(i, s)
                if s + 1 < S:
                    normalize(i, s + 1)
                elif not isinstance(i, int) or i + 1 < NG // S:
                    normalize(i + 1, 0)
                combine(i, s)

            normalize(0, 0)
            for s in range(S):
                group(0, s)
            with dve.Fori(1, NG // S - 1) as i:
                chain.enter(i - 1, 6 * S)
                for s in range(S):
                    group(i, s)
            chain.leave(NG // S - 2)
            for s in range(S):
                group(NG // S - 1, s)

        @block.tensor
        def _(pe):
            pe.wait_ge(ident_in, 16)

            def turn(i, s):
                pe.wait_ge(xf_made, group_of(i, s) + 1)
                if later(i) or s >= 2:
                    pe.wait_ge(xfT_copied, group_of(i, s) - 1)
                for c in range(ND):
                    for t in range(T):
                        ins = pe.transpose(x_bank[s % 2][0:DC, c * G + t * 128:c * G + (t + 1) * 128],
                                           xf[:, s, t, c * DC:(c + 1) * DC], ident[:])
                ins.then_inc(xf_turned, 1)

            def up(i, s):
                pe.wait_ge(xfT_copied, group_of(i, s) + 1)
                for m in range(FM):
                    if (later(i) or s) and m % 2 == 0:
                        pe.wait_ge(h_active, i * (S * FM) + (s - 1) * FM + (m + 2))
                    for c in range(ND):
                        ins = pe.matmul(h_bank[m // 2][:, m % 2 * G:(m % 2 + 1) * G], w1[:, s, c, m * 128:(m + 1) * 128],
                                        xfT[:, s, c], start=(c == 0), stop=(c == ND - 1))
                    if m % 2:
                        ins.then_inc(h_made, 1)

            def down(i, s):
                if later(i) or s >= 2:
                    pe.wait_ge(o_read, group_of(i, s) - 1)
                for t in range(T):
                    for m in range(FM):
                        if t == 0:
                            pe.wait_ge(h_active, i * (S * FM) + (s * FM + m + 1))
                        ins = pe.matmul(o_bank[s % 2][:, t * D:(t + 1) * D], hid[:, s, m, t * 128:(t + 1) * 128],
                                        w2[:, s, m], start=(m == 0), stop=(m == FM - 1))
                ins.then_inc(o_made, 1)

            def group(i, s):
                up(i, s)
                if s + 1 < S:
                    turn(i, s + 1)
                elif not isinstance(i, int) or i + 1 < NG // S:
                    turn(i + 1, 0)
                down(i, s)

            turn(0, 0)
            for s in range(S):
                group(0, s)
            with pe.Fori(1, NG // S - 1) as i:
                for s in range(S):
                    group(i, s)
            for s in range(S):
                group(NG // S - 1, s)

        @block.scalar
        def _(act):
            def copy_x(i, s):
                act.wait_ge(xf_turned, group_of(i, s) + 1)
                act.activation(xfT[:, s].rearrange("p c g -> p (c g)"), x_bank[s % 2][0:DC, 0:ND * G],
                               ACT.Copy).then_inc(xfT_copied, 1)

            def gelu(i, s):
                for m in range(FM):
                    if m % 2 == 0:
                        act.wait_ge(h_made, i * (S * FM // 2) + s * (FM // 2) + (m // 2 + 1))
                    act.activation(hid[:, s, m], h_bank[m // 2][:, m % 2 * G:(m % 2 + 1) * G], ACT.Gelu,
                                   bias=b1[:, s, m:m + 1]).then_inc(h_active, 1)

            def group(i, s):
                gelu(i, s)
                if s + 1 < S:
                    copy_x(i, s + 1)
                elif not isinstance(i, int) or i + 1 < NG // S:
                    copy_x(i + 1, 0)

            copy_x(0, 0)
            for s in range(S):
                group(0, s)
            with act.Fori(1, NG // S - 1) as i:
                for s in range(S):
                    group(i, s)
            for s in range(S):
                group(NG // S - 1, s)

        @block.gpsimd
        def _(pool):
            def scatter(i, s):
                pool.wait_ge(y_made, group_of(i, s) + 1).then_inc(alone, 1)
                for t in range(T):
                    pool.indirect_dma_start(out, bass.IndirectOffsetOnAxis(ap=token[:, s, t:t + 1], axis=0),
                                            y[:, s, t], None, bounds_check=TOKENS - 1,
                                            oob_is_err=False).then_inc(y_out[s], 16)

            with pool.Fori(0, NG // S) as i:
                for s in range(S):
                    scatter(i, s)
            for s in range(S):
                pool.wait_ge(y_out[s], 16 * T * (NG // S))


def laid_out(inputs):
    x = np.asarray(inputs["x"])
    c = np.ascontiguousarray
    x = x.reshape(B, C, 14, 16, 14, 16).transpose(2, 4, 3, 5, 1, 0).reshape(2, HALF, KC, 128, C, B)
    w = np.asarray(inputs["L0_tok_decode_weights"]).reshape(2, HALF, D, KC, 128)
    mw = np.asarray(inputs["L0_tok_merge_weights"]).reshape(2, HALF, C).transpose(1, 0, 2)
    out = {
        "pixels": c(x.transpose(1, 3, 0, 4, 2, 5)).reshape(HALF, 128, 2, C, KC * B),
        "decode": c(w.transpose(1, 4, 0, 3, 2)),
        "mw_b": np.broadcast_to(mw.reshape(1, -1), (128, HALF * 2 * C)).copy(),
        "mw_rows": c(mw),
        "dec_bias": c(np.asarray(inputs["L0_tok_decode_biases"]).reshape(2, HALF, D).transpose(1, 0, 2)),
        "merge_bias": c(np.asarray(inputs["L0_tok_merge_biases"]).reshape(2, HALF).T),
    }
    for n in ("Wq", "Wk", "Wv", "Wg"):
        out[n] = c(np.asarray(inputs["L0_attn_" + n]).reshape(ND, DC, -1).transpose(1, 0, 2))
    out["Wo"] = c(np.asarray(inputs["L0_attn_Wo"]).reshape(NP, 128, D).transpose(1, 0, 2))
    out["gn_w"] = c(np.asarray(inputs["L0_attn_gn_weight"]).reshape(NP, 128).T)
    out["gn_b"] = c(np.asarray(inputs["L0_attn_gn_bias"]).reshape(NP, 128).T)
    out["sw"] = c(np.asarray(inputs["L0_ffn_switch_w"]).reshape(ND, DC, E).transpose(1, 0, 2))
    out["sb"] = np.broadcast_to(np.tile(np.asarray(inputs["L0_ffn_switch_b"]), 2), (HALF, 2 * E)).copy()
    out["w1"] = c(np.asarray(inputs["L0_ffn_w1"]).reshape(E, ND, DC, F).transpose(0, 2, 1, 3))
    out["w2"] = c(np.asarray(inputs["L0_ffn_w2"]).reshape(E, FM, 128, D).transpose(0, 2, 1, 3))
    out["b1"] = c(np.asarray(inputs["L0_ffn_b1"]).reshape(E, FM, 128).transpose(0, 2, 1))
    out["b2"] = np.broadcast_to(np.asarray(inputs["L0_ffn_b2"])[:, None, :], (E, 128, D)).copy()
    out.update(constants())
    return out


def build(nc, a, out):
    h_dram = nc.dram_tensor("h_rows", (B, N, D), F32, kind="Internal").ap()
    bias_dram = nc.dram_tensor("bias_rows", (HALF, 2, D), F32, kind="Internal").ap()
    z_dram = nc.dram_tensor("dispatched", (ZROWS, ROW), F32, kind="Internal").ap()
    limits_dram = nc.dram_tensor("limits", (E, 2), F32, kind="Internal").ap()
    with ExitStack() as ctx:
        prob = ctx.enter_context(nc.sbuf_tensor("prob", [HALF, E, NT], F32))
        count = ctx.enter_context(nc.sbuf_tensor("count", [HALF, E], F32))
        groups = ctx.enter_context(nc.sbuf_tensor("groups", [1, NG, 2], I32))
        with nc.sbuf_tensor("xT", [DC, B, ND, N], F32) as xT:
            tokenize(nc, a, h_dram, bias_dram, xT[:])
            attend(nc, a, h_dram, z_dram, xT[:], prob[:], count)
        find_limits(nc, a, z_dram, limits_dram, prob[:], count, groups)
        experts(nc, a, z_dram, limits_dram, groups, out.rearrange("b n f -> (b n) f"))


def kernel(**inputs):
    import concourse.bacc as bacc
    from concourse.bass_utils import run_bass_kernel_spmd

    nc = bacc.Bacc("TRN2", target_bir_lowering=False, num_devices=1)
    arrays, a = {}, {}
    for name, value in laid_out(inputs).items():
        arrays["in_" + name] = value
        a[name] = nc.dram_tensor("in_" + name, value.shape, F32, kind="ExternalInput").ap()
    out = nc.dram_tensor("out", (B, N, D), F32, kind="ExternalOutput").ap()
    build(nc, a, out)
    r = run_bass_kernel_spmd(nc, [arrays], core_ids=[0])
    return r.results[0]["out"]
```

```python
from contextlib import ExitStack

import numpy as np
import concourse.bass as bass
from concourse import mybir

ALU = mybir.AluOpType
ACT = mybir.ActivationFunctionType
AX = mybir.AxisListType
F32 = mybir.dt.float32
I32 = mybir.dt.int32
U32 = mybir.dt.uint32
BF16 = mybir.dt.bfloat16
F32R = mybir.dt.float32r

B = 64
C = 3
N = 196
PD = 256
D = 192
H = 6
DQK = 128
DV = 64
E = 8
F = 768
HALF = N // 2
KC = PD // 128
DC = 96
ND = D // DC
NP = H // 2
NT = 2 * B
PAIRS = B // 2
TOKENS = B * N
CAP = int(1.25 * TOKENS / E)
EPS = 1e-5

RING = 7
ROUNDS = HALF // RING

G = 256
FM = F // 128
REGION = TOKENS + G
ZROWS = E * REGION + G
NG = (TOKENS + E * (G - 1)) // G
SLOTS = 4
NG += -NG % SLOTS
ROW = D + 4
EMPTY = 16384.0
PSTEPS = 28
ISTEPS = 14


def constants():
    f = np.float32
    pos = np.arange(N, dtype=f)
    half = DQK // 2
    inv = (f(1.0) / f(10000.0) ** (np.arange(half, dtype=f) / f(half))).astype(f)
    angle = pos[:, None] * inv[None, :]
    zeta = (np.arange(half, dtype=f) + f(half)) / f(DQK)
    cos_t = np.zeros((128, 2, N), f)
    sin_t = np.zeros((128, 2, N), f)
    for k, sign in enumerate((1.0, -1.0)):
        decay = zeta[None, :] ** (f(sign) * pos[:, None] / f(512.0))
        c = (np.cos(angle) * decay).T.astype(f)
        s = (np.sin(angle) * decay).T.astype(f)
        cos_t[:, k] = np.concatenate([c, c])
        sin_t[:, k] = np.concatenate([-s, s])
    gam = np.array([1.0 - 2.0 ** (-(5 + h)) for h in range(H)], dtype=f)
    diff = pos[:, None] - pos[None, :]
    dm = gam[:, None, None] ** np.maximum(diff, 0)[None] * (diff >= 0).astype(f)[None]
    row = np.maximum(dm.sum(-1, keepdims=True), 1e-6)
    dm = (dm / np.sqrt(row) * DQK ** -0.5).astype(f)
    dmt = dm.transpose(2, 0, 1)
    mask = np.concatenate([dmt[:HALF], dmt[HALF:, :, HALF:]], axis=2)
    blk = np.zeros((128, 128), f)
    blk[:64, :64] = blk[64:, 64:] = 1.0 / 64
    steps = np.zeros((PSTEPS + ISTEPS,), f)
    steps[:PSTEPS] = 0.5 ** np.arange(1, PSTEPS + 1)
    steps[PSTEPS:] = 2.0 ** np.arange(ISTEPS - 1, -1, -1)
    tid = (np.arange(NT)[None, :] * HALF + np.arange(HALF)[:, None]).astype(f)
    NK = -(-TOKENS // G)
    fill = np.zeros((128, 2 * ROW), f)
    fill[:, ROW - 1] = fill[:, 2 * ROW - 1] = EMPTY
    regs = (np.arange(E) * REGION).astype(f)
    return {
        "c_cos": cos_t.reshape(128, -1), "c_sin": sin_t.reshape(128, -1),
        "c_mask": np.ascontiguousarray(mask).reshape(HALF, -1),
        "c_block": blk, "c_ident": np.eye(128, dtype=f),
        "c_before": np.triu(np.ones((HALF, HALF), f), 1),
        "c_steps": np.broadcast_to(steps, (HALF, PSTEPS + ISTEPS)).copy(),
        "c_tid": tid,
        "c_region": np.broadcast_to(regs, (HALF, E)).copy(),
        "c_expert": np.broadcast_to(np.tile(np.arange(E, dtype=f), 4), (HALF, 4 * E)).copy(),
        "c_fill": fill,
        "c_sizes": np.broadcast_to(np.arange(NK, dtype=f) * G, (E, NK)).reshape(1, -1).copy(),
        "c_upto": np.tril(np.ones((E, E), f)).reshape(1, -1),
        "c_group": np.arange(NG, dtype=f).reshape(1, -1),
    }


class Chain:

    def __init__(self, eng, sem):
        self.eng, self.sem, self.n, self.off = eng, sem, 0, None

    def now(self):
        return self.n if self.off is None else self.off + self.n

    def enter(self, i, per):
        self.per, self.base = per, self.n
        self.off = i * per + self.base
        self.n = 0

    def leave(self, passes):
        assert self.n == self.per, (self.n, self.per)
        self.off, self.n = None, self.base + passes * self.per

    def link(self, ins, alone=None):
        self.n += 1
        ins.then_inc(self.sem, 1)
        wait = self.eng.wait_ge(self.sem, self.now())
        if alone is not None:
            wait.then_inc(alone, 1)


def later(r):
    return not isinstance(r, int) or r > 0


def before(r, s, d):
    return (r, s - d) if s >= d else (r - 1, s - d + RING)


def rsqrt(dve, chain, v, y, t):
    chain.link(dve.tensor_scalar(t.bitcast(I32), v.bitcast(I32), 1, None, ALU.logical_shift_right))
    chain.link(dve.tensor_scalar(y.bitcast(I32), t.bitcast(I32), -1, 0x5F3759DF, ALU.mult, ALU.add))
    for _ in range(3):
        chain.link(dve.scalar_tensor_tensor(out=t, in0=y, scalar=-0.5, in1=y, op0=ALU.mult, op1=ALU.mult))
        chain.link(dve.tensor_tensor(t, t, v, ALU.mult))
        chain.link(dve.scalar_tensor_tensor(out=y, in0=t, scalar=1.5, in1=y, op0=ALU.add, op1=ALU.mult))


def tokenize(nc, a, h_dram, bias_dram, xT):
    with ExitStack() as ctx:
        def sb(name, shape, dt=F32):
            return ctx.enter_context(nc.sbuf_tensor("tok_" + name, shape, dt))

        def sem(name):
            return ctx.enter_context(nc.semaphore(name))

        pix = sb("pix", [128, RING, 2, C, KC * B])
        wts = sb("wts", [128, RING, 2, KC, D])
        brow = sb("brow", [1, RING, 2, D])
        mix = sb("mix", [128, RING, 2, KC * B])
        hs = sb("hs", [128, RING, D])
        xn = sb("xn", [128, RING, D])
        st = sb("st", [128, RING, 6])
        mv = sb("mv", [128, RING, 2])
        sd = sb("sd", [128, RING])
        rs = sb("rs", [128, RING])
        eps = sb("eps", [128, 1])
        ones = sb("ones", [1, B])
        ident = sb("ident", [128, 128])
        mwb = sb("mwb", [128, HALF * 2 * C])
        dbias = sb("dbias", [HALF, 2, D])
        mrow = sb("mrow", [HALF, 2, C])
        mbias = sb("mbias", [HALF, 2])
        msum = sb("msum", [HALF, 2])
        banks = [ctx.enter_context(nc.psum_tensor(f"tok{i}", [128, 512], F32)) for i in range(8)]
        HB = [0, 1, 2, 3, 0, 1, 2]
        TB = [4, 5, 6, 4, 5, 6, 7]

        const_in = sem("tok_const_in")
        pair_in = [sem(f"tok_pair_in{s}") for s in range(RING)]
        h_out = [sem(f"tok_h_out{s}") for s in range(RING)]
        bias_made, bias_kept = sem("bias_made"), sem("bias_kept")
        setup, scaled, half_mixed, mixed = sem("tok_setup"), sem("scaled"), sem("half_mixed"), sem("mixed")
        multiplied, h_copied, counted, rooted = sem("multiplied"), sem("h_copied"), sem("counted"), sem("rooted")
        inverted, normed, turned, xt_copied = sem("inverted"), sem("normed"), sem("turned"), sem("xt_copied")
        chain_sem, alone = sem("tok_chain"), sem("tok_alone")

        def back(banks_of, s):
            return next(d for d in range(1, RING + 1) if banks_of[(s - d) % RING] == banks_of[s])

        block = ctx.enter_context(nc.Block())

        @block.sync
        def _(sp):
            sp.dma_start(mwb[:], a["mw_b"]).then_inc(const_in, 16)
            sp.dma_start(dbias[:], a["dec_bias"]).then_inc(const_in, 16)
            sp.dma_start(mrow[:], a["mw_rows"]).then_inc(const_in, 16)
            sp.dma_start(mbias[:], a["merge_bias"]).then_inc(const_in, 16)
            sp.dma_start(ident[:], a["c_ident"]).then_inc(const_in, 16)

            def load(j, s, first):
                sp.dma_start(pix[:, s], a["pixels"][bass.ds(j, 1)].rearrange("o p u c q -> (o p) u c q")).then_inc(pair_in[s], 16)
                sp.dma_start(wts[:, s], a["decode"][bass.ds(j, 1)].rearrange("o p u k f -> (o p) u k f")).then_inc(pair_in[s], 16)
                if first and s == 0:
                    sp.wait_ge(bias_kept, 16)
                sp.dma_start(brow[:, s], bias_dram[bass.ds(j, 1)]).then_inc(pair_in[s], 16)

            def store(j, s):
                for u in range(2):
                    sp.dma_start(h_dram[:, bass.ds(j + u * HALF, 1), :].rearrange("b o f -> b (o f)"),
                                 hs[u * B:(u + 1) * B, s]).then_inc(h_out[s], 16)

            for s in range(RING):
                load(s, s, True)
            with sp.Fori(1, ROUNDS) as r:
                for s in range(RING):
                    sp.wait_ge(multiplied, (r - 1) * RING + (s + 1))
                    load(r * RING + s, s, False)
                    sp.wait_ge(h_copied, (r - 1) * RING + (s + 1))
                    store((r - 1) * RING + s, s)
            for s in range(RING):
                sp.wait_ge(h_copied, (ROUNDS - 1) * RING + s + 1)
                store((ROUNDS - 1) * RING + s, s)
            for s in range(RING):
                sp.wait_ge(h_out[s], 32 * ROUNDS)

        @block.gpsimd
        def _(pool):
            pool.wait_ge(bias_made, 2)
            pool.dma_start(bias_dram.rearrange("i u f -> i (u f)"), dbias[:].rearrange("i u f -> i (u f)")).then_inc(bias_kept, 16)

        @block.scalar
        def _(act):
            act.wait_ge(const_in, 80)
            act.wait_ge(setup, 2)

            def scale_first_channel(r, s):
                act.wait_ge(pair_in[s], r * 48 + 48)
                for u in range(2):
                    ins = act.activation(mix[:, s, u], pix[:, s, u, 0], ACT.Copy,
                                         scale=mwb[:, bass.ds(r * (RING * 2 * C) + (s * 2 + u) * C, 1)])
                ins.then_inc(scaled, 1)

            def copy_h(r, s):
                act.wait_ge(multiplied, r * RING + (s + 1))
                if later(r):
                    act.wait_ge(h_out[s], r * 32)
                act.activation(hs[:, s], banks[HB[s]][:, 0:D], ACT.Copy).then_inc(h_copied, 1)

            def root(r, s):
                act.wait_ge(counted, r * RING + (s + 1))
                act.activation(sd[:, s:s + 1], mv[:, s, 1:2], ACT.Sqrt, bias=eps[:]).then_inc(rooted, 1)

            def copy_xt(r, s):
                act.wait_ge(turned, r * RING + (s + 1))
                for c in range(ND):
                    src = banks[TB[s]][0:DC, c * 128:(c + 1) * 128].rearrange("p (u b) -> p u b", u=2)
                    dst = xT.rearrange("p b c (u i) -> p c u b i", u=2)[:, c, :, :, bass.ds(r * RING + s, 1)]
                    ins = act.activation(dst.rearrange("p u b o -> p u (b o)"), src, ACT.Copy)
                ins.then_inc(xt_copied, 1)

            def step(r, s):
                scale_first_channel(r, s)
                if later(r) or s >= 1:
                    copy_h(*before(r, s, 1))
                if later(r) or s >= 2:
                    root(*before(r, s, 2))
                if later(r) or s >= 4:
                    copy_xt(*before(r, s, 4))

            for r in range(2):
                for s in range(RING):
                    step(r, s)
            with act.Fori(2, ROUNDS) as r:
                for s in range(RING):
                    step(r, s)
            copy_h(ROUNDS - 1, RING - 1)
            for s in range(RING - 2, RING):
                root(ROUNDS - 1, s)
            for s in range(RING - 4, RING):
                copy_xt(ROUNDS - 1, s)

        @block.vector
        def _(dve):
            chain = Chain(dve, chain_sem)
            dve.memset(eps[:], EPS).then_inc(setup, 1)
            dve.memset(ones[:], 1.0).then_inc(setup, 1)
            dve.wait_ge(const_in, 80)
            chain.link(dve.tensor_reduce(msum[:], mrow[:], AX.X, ALU.add))
            for u in range(2):
                dve.tensor_scalar(dbias[:, u], dbias[:, u], msum[:, u:u + 1], mbias[:, u:u + 1],
                                  ALU.mult, ALU.add).then_inc(bias_made, 1)

            def merge_channels(r, s):
                dve.wait_ge(scaled, r * RING + (s + 1))
                for c in range(1, C):
                    for u in range(2):
                        ins = dve.scalar_tensor_tensor(
                            out=mix[:, s, u], in0=pix[:, s, u, c],
                            scalar=mwb[:, bass.ds(r * (RING * 2 * C) + (s * 2 + u) * C + c, 1)],
                            in1=mix[:, s, u], op0=ALU.mult, op1=ALU.add)
                    if c == 1:
                        ins.then_inc(half_mixed, 1)
                        dve.wait_ge(half_mixed, r * RING + (s + 1))
                ins.then_inc(mixed, 1)

            def count(r, s):
                dve.wait_ge(h_copied, r * RING + (s + 1))
                chain.link(dve.bn_stats(st[:, s], hs[:, s]), alone)
                dve.bn_aggr(mv[:, s], st[:, s]).then_inc(counted, 1)

            def normalize(r, s):
                dve.wait_ge(rooted, r * RING + (s + 1))
                dve.reciprocal(rs[:, s:s + 1], sd[:, s:s + 1]).then_inc(inverted, 1)
                dve.wait_ge(inverted, r * RING + (s + 1))
                dve.tensor_scalar(xn[:, s], hs[:, s], mv[:, s, 0:1], rs[:, s:s + 1],
                                  ALU.subtract, ALU.mult).then_inc(normed, 1)

            def step(r, s):
                merge_channels(r, s)
                if later(r) or s >= 1:
                    count(*before(r, s, 1))
                if later(r) or s >= 2:
                    normalize(*before(r, s, 2))

            for s in range(RING):
                step(0, s)
            with dve.Fori(1, ROUNDS) as r:
                chain.enter(r - 1, RING)
                for s in range(RING):
                    step(r, s)
            chain.leave(ROUNDS - 1)
            count(ROUNDS - 1, RING - 1)
            for s in range(RING - 2, RING):
                normalize(ROUNDS - 1, s)

        @block.tensor
        def _(pe):
            pe.wait_ge(const_in, 80)
            pe.wait_ge(setup, 2)

            def product(r, s):
                pe.wait_ge(mixed, r * RING + (s + 1))
                if later(r) or s >= back(HB, s):
                    pe.wait_ge(h_copied, r * RING + (s + 1 - back(HB, s)))
                for u in range(2):
                    out = banks[HB[s]][u * B:(u + 1) * B, 0:D]
                    pe.matmul(out, ones[:], brow[:, s, u], start=True, stop=False)
                    for k in range(KC):
                        ins = pe.matmul(out, mix[:, s, u, k * B:(k + 1) * B], wts[:, s, u, k],
                                        start=False, stop=(k == KC - 1))
                ins.then_inc(multiplied, 1)

            def turn(r, s):
                pe.wait_ge(normed, r * RING + (s + 1))
                if later(r) or s >= back(TB, s):
                    pe.wait_ge(xt_copied, r * RING + (s + 1 - back(TB, s)))
                for c in range(ND):
                    ins = pe.transpose(banks[TB[s]][0:DC, c * 128:(c + 1) * 128], xn[:, s, c * DC:(c + 1) * DC], ident[:])
                ins.then_inc(turned, 1)

            def step(r, s):
                product(r, s)
                if later(r) or s >= 3:
                    turn(*before(r, s, 3))

            for r in range(2):
                for s in range(RING):
                    step(r, s)
            with pe.Fori(2, ROUNDS) as r:
                for s in range(RING):
                    step(r, s)
            for s in range(RING - 3, RING):
                turn(ROUNDS - 1, s)


def attend(nc, a, h_dram, z_dram, xT, prob, count):
    with ExitStack() as ctx:
        def sb(name, shape, dt=F32):
            return ctx.enter_context(nc.sbuf_tensor("att_" + name, shape, dt))

        def sem(name):
            return ctx.enter_context(nc.semaphore(name))

        wq = sb("wq", [DC, ND, H * DQK])
        wk = sb("wk", [DC, ND, H * DQK])
        wv = sb("wv", [DC, ND, H * DV])
        wg = sb("wg", [DC, ND, H * DV])
        wo = sb("wo", [128, NP, D])
        gnw = sb("gnw", [128, NP])
        gnb = sb("gnb", [128, NP])
        sw = sb("sw", [DC, ND, E])
        swb = sb("swb", [HALF, 4, E])
        cos_t = sb("cos_t", [128, 2, N])
        sin_t = sb("sin_t", [128, 2, N])
        mask = sb("mask", [HALF, H, N + HALF])
        block64 = sb("block64", [128, 128])
        ident = sb("ident2", [128, 128])
        earlier = sb("earlier", [HALF, HALF])
        ones = sb("ones2", [HALF, HALF])
        tid = sb("tid", [HALF, NT])
        expert = sb("expert", [HALF, 4, E])

        x = sb("x", [DC, 2, ND, N])
        hres = sb("hres", [HALF, 4, D])
        v = sb("v", [HALF, 2, 2, H * DV])
        swapped = sb("swapped", [128, 3, 2, N])
        straight = sb("straight", [128, 3, 2, N])
        rot = sb("rot", [128, 2 * NP, 2, N])
        sm = sb("sm", [HALF, H, N + HALF])
        cc = sb("cc", [128, 2, 2, NP, N])
        gate = sb("gate", [128, 2, 2, NP, N])
        gst = sb("gst", [128, 2, NP, 6])
        gmv = sb("gmv", [128, 2, NP, 2])
        gs = sb("gs", [128, 2, 2, NP])
        gg = sb("gg", [128, 2, 2, NP])
        gv, gy, gt = sb("gv", [128, 2, NP]), sb("gy", [128, 2, NP]), sb("gt", [128, 2, NP])
        ga, gb = sb("ga", [128, 2, NP]), sb("gb", [128, 2, NP])
        row = sb("row", [HALF, 4, ROW])
        lst = sb("lst", [HALF, 4, 6])
        lmv = sb("lmv", [HALF, 4, 2])
        lv, lt, ly = sb("lv", [HALF, 4]), sb("lt", [HALF, 4]), sb("ly", [HALF, 4])
        xf = sb("xf", [HALF, 4, D])
        xfT = sb("xfT", [DC, 2, ND, N])
        z = sb("logits", [HALF, 4, E])
        zmax = sb("zmax", [HALF, 4])
        ez = sb("ez", [HALF, 4, E])
        rank = sb("rank", [HALF, 4, E])
        route = sb("route", [HALF, 4])
        esum = sb("esum", [HALF, 4])
        chosen = sb("chosen", [HALF, 4, E])
        slot = sb("slot", [HALF, 4])
        slot_i = sb("slot_i", [HALF, 4], U32)

        qk_bank = [ctx.enter_context(nc.psum_tensor(f"qk{i}", [128, 512], F32)) for i in range(3)]
        s_bank = [ctx.enter_context(nc.psum_tensor(f"s{i}", [128, 512], F32)) for i in range(2)]
        o_bank = ctx.enter_context(nc.psum_tensor("o_bank", [128, 512], F32))
        ma = ctx.enter_context(nc.psum_tensor("ma", [128, 512], F32))
        mb = ctx.enter_context(nc.psum_tensor("mb", [128, 512], F32))

        v_weights_in, weights_in, ones_made = sem("v_weights_in"), sem("weights_in"), sem("ones_made")
        x_in = [sem(f"x_in{i}") for i in range(2)]
        res_in, res_added = sem("res_in"), sem("res_added")
        v_made, v_copied = sem("v_made"), sem("v_copied")
        g_made, g_tanh, g_gated = sem("g_made"), sem("g_tanh"), sem("g_gated")
        qk_made, qk_swapped, qk_straight, qk_turned, qk_rotated = (
            sem("qk_made"), sem("qk_swapped"), sem("qk_straight"), sem("qk_turned"), sem("qk_rotated"))
        s_made, s_decayed = sem("s_made"), sem("s_decayed")
        o_made, o_copied, stats_ready, stats_summed, stats_read = (
            sem("o_made"), sem("o_copied"), sem("stats_ready"), sem("stats_summed"), sem("stats_read"))
        gated_ready, wo_made = sem("gated_ready"), sem("wo_made")
        xf_ready, xf_turned, xfT_copied = sem("xf_ready"), sem("xf_turned"), sem("xfT_copied")
        z_made, z_shifted, z_exped = sem("z_made"), sem("z_shifted"), sem("z_exped")
        chosen_ready, prefix_made, prefix_read = sem("chosen_ready"), sem("prefix_made"), sem("prefix_read")
        slots_ready, rows_out = sem("slots_ready"), sem("rows_out")
        chain_sem, alone = sem("att_chain"), sem("att_alone")

        block = ctx.enter_context(nc.Block())
        loads = [(wq, "Wq"), (wk, "Wk"), (wg, "Wg"), (wo, "Wo"), (gnw, "gn_w"), (gnb, "gn_b"),
                 (sw, "sw"), (swb, "sb"), (cos_t, "c_cos"), (sin_t, "c_sin"), (mask, "c_mask"),
                 (block64, "c_block"), (ident, "c_ident"), (earlier, "c_before"), (tid, "c_tid"),
                 (expert, "c_expert"), (count, "c_region")]
        ALL_IN = 16 * len(loads)

        def two(t):
            return t.unsqueeze(1).broadcast_to([128, 2, N])

        @block.sync
        def _(sp):
            def load_x(b, i):
                sp.dma_start(x[:, i], xT[:, bass.ds(b, 1)].rearrange("p o c n -> p (o c) n")).then_inc(x_in[i], 16)

            def load_residual(p):
                sp.dma_start(hres[:], h_dram[bass.ds(p * 2, 2)].rearrange("i (t q) f -> q (i t) f", t=2)).then_inc(res_in, 16)

            sp.dma_start(wv[:].rearrange("p x y -> p (x y)"), a["Wv"].rearrange("p x y -> p (x y)")).then_inc(v_weights_in, 16)
            for i in range(2):
                load_x(i, i)
            for t, name in loads:
                dst = t[:] if len(t.shape) == 2 else t[:].rearrange("p x y -> p (x y)")
                src = a[name] if len(a[name].shape) == 2 else a[name].rearrange("p x y -> p (x y)")
                sp.dma_start(dst, src).then_inc(weights_in, 16)
            load_residual(0)
            with sp.Fori(1, PAIRS) as p:
                for i in range(2):
                    sp.wait_ge(qk_made, p * 12 - (6 - i * 6))
                    load_x(p * 2 + i, i)
                sp.wait_ge(res_added, p * 2)
                load_residual(p)

        @block.tensor
        def _(pe):
            pe.wait_ge(v_weights_in, 16)

            def product(out, lhs, rhs):
                for c in range(ND):
                    ins = pe.matmul(out, lhs(c), rhs(c), start=(c == 0), stop=(c == ND - 1))
                return ins

            def values(p, i, t, free=None):
                b = p * 2 + i
                if t == 0:
                    pe.wait_ge(x_in[i], p * 16 + 16)
                if free is not None:
                    pe.wait_ge(*free)
                product((ma, mb)[t][0:HALF, 0:H * DV], lambda c: x[:, i, c, t * HALF:(t + 1) * HALF],
                        lambda c: wv[:, c]).then_inc(v_made, 1)

            def gates(p, i, part):
                pe.wait_ge(v_copied, (p * 2 + i) * 2 + (part + 1))
                bank = (ma, mb)[part]
                for n, m in enumerate(((0, 1), (2,))[part]):
                    ins = product(bank[:, n * N:(n + 1) * N], lambda c: wg[:, c, m * 128:(m + 1) * 128],
                                  lambda c: x[:, i, c])
                ins.then_inc(g_made, 1)

            def project(p, i, n):
                b = p * 2 + i
                if later(b) or n >= 3:
                    pe.wait_ge(qk_straight, b * 6 + (n - 2))
                w = (wq, wk)[n % 2]
                for j in range(2):
                    h = n // 2 * 2 + j
                    ins = product(qk_bank[n % 3][:, j * N:(j + 1) * N],
                                  lambda c: w[:, c, h * DQK:(h + 1) * DQK], lambda c: x[:, i, c])
                ins.then_inc(qk_made, 1)

            def scores(p, i, hp):
                b = p * 2 + i
                pe.wait_ge(qk_rotated, b * 6 + (2 * hp + 2))
                for j in range(2):
                    h = 2 * hp + j
                    if later(b) or h >= 2:
                        pe.wait_ge(s_decayed, b * 6 + (h - 1))
                    q, k = rot[:, 2 * hp, j], rot[:, 2 * hp + 1, j]
                    pe.matmul(s_bank[j][0:HALF, 0:N], k[:, 0:HALF], q[:, 0:N], start=True, stop=True)
                    pe.matmul(s_bank[j][0:HALF, N:N + HALF], k[:, HALF:N], q[:, HALF:N],
                              start=True, stop=True).then_inc(s_made, 1)

            def outputs(p, i, hp):
                b = p * 2 + i
                pe.wait_ge(s_decayed, b * 6 + (2 * hp + 2))
                if later(b) or hp >= 1:
                    pe.wait_ge(o_copied, b * 3 + hp)
                for j in range(2):
                    h = 2 * hp + j
                    at = slice(j * DV, (j + 1) * DV)
                    pe.matmul(o_bank[at, 0:N], v[:, i, 0, h * DV:(h + 1) * DV], sm[:, h, 0:N], start=True, stop=False)
                    ins = pe.matmul(o_bank[at, HALF:N], v[:, i, 1, h * DV:(h + 1) * DV], sm[:, h, N:N + HALF],
                                    start=False, stop=True)
                ins.then_inc(o_made, 1)

            def group_statistics(tail, *free):
                pe.wait_ge(stats_ready, tail + 1)
                pe.wait_ge(*free)
                pe.matmul(ma[:, 0:4 * NP], block64[:], gs[:].rearrange("p s i n -> p (s i n)"),
                          start=True, stop=True).then_inc(stats_summed, 1)

            def project_out(tail, par, i, *free):
                bank = (ma, mb)[i]
                pe.wait_ge(gated_ready, tail + 1)
                pe.wait_ge(*free)
                for t in range(2):
                    for m in range(NP):
                        ins = pe.matmul(bank[0:HALF, t * D:(t + 1) * D], cc[:, par, i, m, t * HALF:(t + 1) * HALF],
                                        wo[:, m], start=(m == 0), stop=(m == NP - 1))
                ins.then_inc(wo_made, 1)

            def turn(tail, i, *free):
                bank = (mb, ma)[i]
                pe.wait_ge(xf_ready, tail * 2 + (i + 1))
                pe.wait_ge(*free)
                for c in range(ND):
                    for t in range(2):
                        ins = pe.transpose(bank[0:DC, c * N + t * HALF:c * N + (t + 1) * HALF],
                                           xf[:, i * 2 + t, c * DC:(c + 1) * DC], ident[0:HALF, 0:HALF])
                ins.then_inc(xf_turned, 1)

            def logits(tail):
                pe.wait_ge(xfT_copied, tail * 2 + 2)
                for t in range(4):
                    for c in range(ND):
                        ins = pe.matmul(ma[0:HALF, t * E:(t + 1) * E],
                                        xfT[:, t // 2, c, t % 2 * HALF:(t % 2 + 1) * HALF], sw[:, c],
                                        start=(c == 0), stop=(c == ND - 1))
                ins.then_inc(z_made, 1)

            def prefix(tail):
                pe.wait_ge(chosen_ready, tail + 1)
                pe.matmul(mb[0:HALF, 0:4 * E], earlier[:], chosen[:].rearrange("p t e -> p (t e)"), start=True, stop=False)
                for t in range(3):
                    for u in range(t + 1, 4):
                        pe.matmul(mb[0:HALF, u * E:(u + 1) * E], ones[:], chosen[:, t], start=False,
                                  stop=(t == 2))
                for t in range(4):
                    ins = pe.matmul(mb[0:HALF, 4 * E:5 * E], ones[:], chosen[:, t], start=(t == 0), stop=(t == 3))
                ins.then_inc(prefix_made, 1)

            def finish(p, i, hp, what):
                if i == 1:
                    what(p, 0, hp)
                elif later(p):
                    what(p - 1, 1, hp)

            def first_image(p, par):
                b = p * 2
                tail, routing = later(p), later(p) and later(p - 1)
                for t in range(2):
                    values(p, 0, t, (res_added, (p - 2) * 2 + (t + 1)) if routing else
                           (g_gated, 3 + t) if tail else None)
                if not tail:
                    pe.wait_ge(weights_in, ALL_IN)
                    pe.wait_ge(ones_made, 1)
                project(p, 0, 0)
                project(p, 0, 1)
                finish(p, 0, 2, scores)
                gates(p, 0, 0)
                gates(p, 0, 1)
                project(p, 0, 2)
                finish(p, 0, 1, outputs)
                if routing:
                    turn(p - 2, 0, g_gated, b * 2 + 2)
                    turn(p - 2, 1, g_gated, b * 2 + 1)
                project(p, 0, 3)
                finish(p, 0, 2, outputs)
                if routing:
                    logits(p - 2)
                scores(p, 0, 0)
                project(p, 0, 4)
                project(p, 0, 5)
                if routing:
                    group_statistics(p - 1, z_shifted, p - 1)
                elif tail:
                    group_statistics(p - 1, g_gated, b * 2 + 1)
                outputs(p, 0, 0)
                if routing:
                    prefix(p - 2)
                scores(p, 0, 1)

            def second_image(p, par):
                b = p * 2 + 1
                tail, routing = later(p), later(p) and later(p - 1)
                values(p, 1, 0, (stats_read, p) if tail else (g_gated, 1))
                values(p, 1, 1, (prefix_read, p - 1) if routing else (g_gated, p * 4 + 2))
                project(p, 1, 0)
                project(p, 1, 1)
                finish(p, 1, 2, scores)
                gates(p, 1, 0)
                gates(p, 1, 1)
                project(p, 1, 2)
                finish(p, 1, 1, outputs)
                if tail:
                    project_out(p - 1, 1 - par, 0, g_gated, b * 2 + 1)
                project(p, 1, 3)
                finish(p, 1, 2, outputs)
                if tail:
                    project_out(p - 1, 1 - par, 1, g_gated, b * 2 + 2)
                scores(p, 1, 0)
                project(p, 1, 4)
                project(p, 1, 5)
                outputs(p, 1, 0)
                scores(p, 1, 1)

            def pair(p, par):
                first_image(p, par)
                second_image(p, par)

            pair(0, 0)
            pair(1, 1)
            with pe.Fori(1, PAIRS // 2) as r:
                for par in range(2):
                    pair(r * 2 + par, par)
            finish(PAIRS, 0, 2, scores)
            finish(PAIRS, 0, 1, outputs)
            finish(PAIRS, 0, 2, outputs)
            for i in range(2):
                turn(PAIRS - 2, i, res_added, PAIRS * 2 - 2)
            logits(PAIRS - 2)
            group_statistics(PAIRS - 1, z_shifted, PAIRS - 1)
            prefix(PAIRS - 2)
            project_out(PAIRS - 1, 1, 0, stats_read, PAIRS)
            project_out(PAIRS - 1, 1, 1, prefix_read, PAIRS - 1)
            for i in range(2):
                turn(PAIRS - 1, i, res_added, PAIRS * 2)
            logits(PAIRS - 1)
            prefix(PAIRS - 1)

        @block.scalar
        def _(act):
            def copy_outputs(p, par, i, hp):
                act.wait_ge(o_made, (p * 2 + i) * 3 + (hp + 1))
                if i == 0 and hp == 0 and later(p) and later(p - 1):
                    act.wait_ge(wo_made, (p - 1) * 2)
                act.activation(cc[:, par, i, hp], o_bank[:, 0:N], ACT.Copy).then_inc(o_copied, 1)

            def copy_xfT(tail, i):
                act.wait_ge(xf_turned, tail * 2 + (i + 1))
                act.activation(xfT[:, i].rearrange("p c n -> p (c n)"), (mb, ma)[i][0:DC, 0:ND * N],
                               ACT.Copy).then_inc(xfT_copied, 1)

            def exponentiate(tail):
                act.wait_ge(z_shifted, tail + 1)
                act.activation(ez[:], z[:], ACT.Exp).then_inc(z_exped, 1)

            def swap(b, n):
                act.wait_ge(qk_made, b * 6 + (n + 1))
                if later(b) or n >= 3:
                    act.wait_ge(qk_rotated, b * 6 + (n - 2))
                src = qk_bank[n % 3][:, 0:2 * N].rearrange("p (i n) -> p i n", i=2)
                act.activation(swapped[0:64, n % 3], src[64:128], ACT.Copy)
                act.activation(swapped[64:128, n % 3], src[0:64], ACT.Copy).then_inc(qk_swapped, 1)

            def half_tanh(p, par, i, part):
                act.wait_ge(g_made, (p * 2 + i) * 2 + (part + 1))
                if later(p) and later(p - 1):
                    act.wait_ge(gated_ready, p - 1)
                dst, src = ((gate[:, par, i, 0:2], ma[:, 0:2 * N].rearrange("p (i n) -> p i n", i=2)),
                            (gate[:, par, i, 2], mb[:, 0:N]))[part]
                act.activation(dst, src, ACT.Tanh, scale=0.5).then_inc(g_tanh, 1)

            def finish(p, par, i, hp):
                if i == 1:
                    copy_outputs(p, par, 0, hp)
                elif later(p):
                    copy_outputs(p - 1, 1 - par, 1, hp)

            def image(p, par, i):
                b = p * 2 + i
                routing = i == 0 and later(p) and later(p - 1)
                for t in range(2):
                    act.wait_ge(v_made, b * 2 + (t + 1))
                    if later(p):
                        act.wait_ge(o_made, b * 3 - 3)
                    act.activation(v[:, i, t], (ma, mb)[t][0:HALF, 0:H * DV], ACT.Copy).then_inc(v_copied, 1)
                swap(b, 0)
                swap(b, 1)
                half_tanh(p, par, i, 0)
                half_tanh(p, par, i, 1)
                swap(b, 2)
                finish(p, par, i, 1)
                if routing:
                    copy_xfT(p - 2, 0)
                    copy_xfT(p - 2, 1)
                swap(b, 3)
                finish(p, par, i, 2)
                swap(b, 4)
                swap(b, 5)
                if routing:
                    exponentiate(p - 2)
                copy_outputs(p, par, i, 0)

            def pair(p, par):
                image(p, par, 0)
                image(p, par, 1)

            pair(0, 0)
            pair(1, 1)
            with act.Fori(1, PAIRS // 2) as r:
                for par in range(2):
                    pair(r * 2 + par, par)
            finish(PAIRS, 0, 0, 1)
            finish(PAIRS, 0, 0, 2)
            for tail in range(PAIRS - 2, PAIRS):
                for i in range(2):
                    copy_xfT(tail, i)
                exponentiate(tail)

        @block.gpsimd
        def _(pool):
            def rotate(b, n):
                pool.wait_ge(qk_swapped, b * 6 + (n + 1))
                pool.tensor_tensor(swapped[:, n % 3], swapped[:, n % 3], two(sin_t[:, n % 2]), ALU.mult).then_inc(qk_turned, 1)
                pool.wait_ge(qk_turned, b * 6 + (n + 1))
                pool.wait_ge(qk_straight, b * 6 + (n + 1))
                if later(b):
                    pool.wait_ge(s_made, b * 6 - (4 - n // 2 * 2))
                pool.tensor_tensor(rot[:, n], straight[:, n % 3], swapped[:, n % 3], ALU.add).then_inc(qk_rotated, 1)

            def dispatch(tail):
                pool.wait_ge(slots_ready, tail + 1).then_inc(alone, 1)
                for t in range(4):
                    pool.indirect_dma_start(z_dram, bass.IndirectOffsetOnAxis(ap=slot_i[:, t:t + 1], axis=0),
                                            row[:, t], None).then_inc(rows_out, 16)

            def pair(p):
                for n in range(2 * NP):
                    rotate(p * 2, n)
                if later(p) and later(p - 1):
                    dispatch(p - 2)
                for n in range(2 * NP):
                    rotate(p * 2 + 1, n)

            pool.wait_ge(weights_in, ALL_IN)
            pair(0)
            pair(1)
            with pool.Fori(2, PAIRS) as p:
                pair(p)
            dispatch(PAIRS - 2)
            dispatch(PAIRS - 1)
            pool.wait_ge(rows_out, 64 * PAIRS)

        @block.vector
        def _(dve):
            chain = Chain(dve, chain_sem)
            dve.memset(ones[:], 1.0).then_inc(ones_made, 1)
            dve.wait_ge(weights_in, ALL_IN)

            def read_group_statistics(tail):
                dve.wait_ge(stats_summed, tail + 1)
                dve.tensor_copy(gg[:].rearrange("p s i n -> p (s i n)"), ma[:, 0:4 * NP]).then_inc(stats_read, 1)

            def scale_groupnorm(tail):
                wide = [128, 2, NP]
                dve.wait_ge(stats_read, tail + 1)
                chain.link(dve.tensor_tensor(gt[:], gg[:, 0], gg[:, 0], ALU.mult))
                chain.link(dve.tensor_tensor(gv[:], gg[:, 1], gt[:], ALU.subtract))
                chain.link(dve.tensor_scalar(gv[:], gv[:], 0.0, EPS, ALU.max, ALU.add))
                rsqrt(dve, chain, gv[:], gy[:], gt[:])
                chain.link(dve.tensor_tensor(ga[:], gy[:], gnw[:].unsqueeze(1).broadcast_to(wide), ALU.mult))
                chain.link(dve.tensor_tensor(gb[:], gg[:, 0], ga[:], ALU.mult))
                chain.link(dve.tensor_tensor(gb[:], gnb[:].unsqueeze(1).broadcast_to(wide), gb[:], ALU.subtract))

            def apply_groupnorm(tail, par):
                for i in range(2):
                    for m in range(NP):
                        last = dve.tensor_scalar(cc[:, par, i, m], cc[:, par, i, m], ga[:, i, m:m + 1],
                                                 gb[:, i, m:m + 1], ALU.mult, ALU.add)
                chain.link(last)
                dve.scalar_tensor_tensor(out=cc[:, par], in0=cc[:, par], scalar=0.5, in1=gate[:, par], op0=ALU.mult,
                                         op1=ALU.mult).then_inc(gated_ready, 1)

            def gates(p, par, i):
                for part in range(2):
                    dve.wait_ge(g_tanh, (p * 2 + i) * 2 + (part + 1))
                    dst, src = ((gate[:, par, i, 0:2], ma[:, 0:2 * N].rearrange("p (i n) -> p i n", i=2)),
                                (gate[:, par, i, 2], mb[:, 0:N]))[part]
                    dve.scalar_tensor_tensor(out=dst, in0=dst, scalar=1.0, in1=src, op0=ALU.add,
                                             op1=ALU.mult).then_inc(g_gated, 1)

            def straighten(p, i, n):
                b = p * 2 + i
                dve.wait_ge(qk_swapped, b * 6 + (n + 1))
                if later(b) or n >= 3:
                    dve.wait_ge(qk_rotated, b * 6 + (n - 2))
                dve.tensor_tensor(straight[:, n % 3], qk_bank[n % 3][:, 0:2 * N].rearrange("p (i n) -> p i n", i=2),
                                  two(cos_t[:, n % 2]), ALU.mult).then_inc(qk_straight, 1)

            def decay(p, i, hp):
                b = p * 2 + i
                for j in range(2):
                    h = 2 * hp + j
                    dve.wait_ge(s_made, b * 6 + (h + 1))
                    if later(b):
                        dve.wait_ge(o_made, b * 3 - (2 - hp))
                    dve.tensor_tensor(sm[:, h], s_bank[j][0:HALF, 0:N + HALF], mask[:, h], ALU.mult).then_inc(s_decayed, 1)

            def output_statistics(p, par, i):
                dve.wait_ge(o_copied, (p * 2 + i) * 3 + 3)
                for hp in range(NP):
                    ins = dve.bn_stats(gst[:, i, hp], cc[:, par, i, hp])
                chain.link(ins, alone)
                for hp in range(NP):
                    ins = dve.bn_aggr(gmv[:, i, hp], gst[:, i, hp])
                chain.link(ins)

            def prepare_statistics():
                chain.link(dve.tensor_copy(gs[:, 0], gmv[:, :, :, 0]))
                chain.link(dve.tensor_tensor(gs[:, 1], gs[:, 0], gs[:, 0], ALU.mult))
                dve.tensor_tensor(gs[:, 1], gs[:, 1], gmv[:, :, :, 1], ALU.add).then_inc(stats_ready, 1)

            def add_residual(tail, i):
                if i == 0:
                    dve.wait_ge(res_in, tail * 16 + 16)
                    if later(tail):
                        dve.wait_ge(rows_out, tail * 64)
                dve.wait_ge(wo_made, tail * 2 + (i + 1))
                at = slice(i * 2, i * 2 + 2)
                dve.tensor_tensor(row[:, at, 0:D], (ma, mb)[i][0:HALF, 0:2 * D].rearrange("p (t f) -> p t f", t=2),
                                  hres[:, at], ALU.add).then_inc(res_added, 1)

            def row_statistics(tail):
                dve.wait_ge(res_added, tail * 2 + 2)
                for t in range(4):
                    ins = dve.bn_stats(lst[:, t], row[:, t, 0:D])
                chain.link(ins, alone)
                for t in range(4):
                    ins = dve.bn_aggr(lmv[:, t], lst[:, t])
                chain.link(ins)

            def second_layernorm(tail):
                dve.tensor_copy(row[:, :, D], lmv[:, :, 0])
                chain.link(dve.tensor_scalar(lv[:], lmv[:, :, 1], EPS, None, ALU.add))
                rsqrt(dve, chain, lv[:], ly[:], lt[:])
                dve.tensor_copy(row[:, :, D + 1], ly[:])
                for t in range(4):
                    ins = dve.tensor_scalar(xf[:, t], row[:, t, 0:D], lmv[:, t, 0:1], ly[:, t:t + 1],
                                            ALU.subtract, ALU.mult)
                    if t % 2:
                        ins.then_inc(xf_ready, 1)

            def route_tokens(tail):
                wide = [HALF, 4, E]
                dve.wait_ge(z_made, tail + 1)
                chain.link(dve.tensor_tensor(z[:], ma[0:HALF, 0:4 * E].rearrange("p (t e) -> p t e", t=4), swb[:], ALU.add))
                chain.link(dve.tensor_reduce(zmax[:], z[:], AX.X, ALU.max))
                dve.tensor_tensor(z[:], z[:], zmax[:].unsqueeze(2).broadcast_to(wide), ALU.subtract).then_inc(z_shifted, 1)
                dve.wait_ge(z_shifted, tail + 1)
                chain.link(dve.tensor_scalar(rank[:], z[:], 0.0, float(E), ALU.is_lt, ALU.mult))
                chain.link(dve.tensor_tensor(rank[:], rank[:], expert[:], ALU.add))
                chain.link(dve.tensor_reduce(route[:], rank[:], AX.X, ALU.min))
                dve.tensor_tensor(chosen[:], expert[:], route[:].unsqueeze(2).broadcast_to(wide),
                                  ALU.is_equal).then_inc(chosen_ready, 1)
                dve.wait_ge(z_exped, tail + 1)
                chain.link(dve.tensor_reduce(esum[:], ez[:], AX.X, ALU.add))
                chain.link(dve.reciprocal(row[:, :, D + 2], esum[:]))
                dve.wait_ge(chosen_ready, tail + 1)
                dve.tensor_tensor(prob.rearrange("p e t -> p t e")[:, bass.ds(tail * 4, 4), :], chosen[:],
                                  row[:, :, D + 2:D + 3].broadcast_to(wide), ALU.mult)
                chain.link(dve.tensor_copy(row[:, :, D + 3], tid[:, bass.ds(tail * 4, 4)]))

            def place_tokens(tail):
                dve.wait_ge(prefix_made, tail + 1)
                free = count[:].unsqueeze(1).broadcast_to([HALF, 4, E])
                chain.link(dve.tensor_tensor(rank[:], mb[0:HALF, 0:4 * E].rearrange("p (t e) -> p t e", t=4), free, ALU.add))
                chain.link(dve.tensor_tensor(rank[:], rank[:], chosen[:], ALU.mult))
                chain.link(dve.tensor_reduce(slot[:], rank[:], AX.X, ALU.add))
                dve.tensor_tensor(count[:], count[:], mb[0:HALF, 4 * E:5 * E], ALU.add).then_inc(prefix_read, 1)
                dve.wait_ge(prefix_read, tail + 1)
                dve.tensor_copy(slot_i[:], slot[:]).then_inc(slots_ready, 1)

            def first_image(p, par):
                tail, routing = later(p), later(p) and later(p - 1)
                straighten(p, 0, 0)
                straighten(p, 0, 1)
                if tail:
                    decay(p - 1, 1, 2)
                gates(p, par, 0)
                straighten(p, 0, 2)
                straighten(p, 0, 3)
                if tail:
                    output_statistics(p - 1, 1 - par, 1)
                    prepare_statistics()
                decay(p, 0, 0)
                straighten(p, 0, 4)
                if routing:
                    route_tokens(p - 2)
                straighten(p, 0, 5)
                if tail:
                    read_group_statistics(p - 1)
                if routing:
                    place_tokens(p - 2)
                decay(p, 0, 1)
                if tail:
                    scale_groupnorm(p - 1)

            def second_image(p, par):
                tail = later(p)
                straighten(p, 1, 0)
                straighten(p, 1, 1)
                decay(p, 0, 2)
                if tail:
                    apply_groupnorm(p - 1, 1 - par)
                gates(p, par, 1)
                straighten(p, 1, 2)
                if tail:
                    add_residual(p - 1, 0)
                straighten(p, 1, 3)
                output_statistics(p, par, 0)
                if tail:
                    add_residual(p - 1, 1)
                decay(p, 1, 0)
                straighten(p, 1, 4)
                straighten(p, 1, 5)
                decay(p, 1, 1)
                if tail:
                    row_statistics(p - 1)
                    second_layernorm(p - 1)

            def pair(p, par):
                first_image(p, par)
                second_image(p, par)

            pair(0, 0)
            pair(1, 1)
            with dve.Fori(1, PAIRS // 2) as r:
                chain.enter(r - 1, PER_ROUND)
                for par in range(2):
                    pair(r * 2 + par, par)
            chain.leave(PAIRS // 2 - 1)
            decay(PAIRS - 1, 1, 2)
            output_statistics(PAIRS - 1, 1, 1)
            prepare_statistics()
            route_tokens(PAIRS - 2)
            read_group_statistics(PAIRS - 1)
            place_tokens(PAIRS - 2)
            scale_groupnorm(PAIRS - 1)
            apply_groupnorm(PAIRS - 1, 1)
            for i in range(2):
                add_residual(PAIRS - 1, i)
            row_statistics(PAIRS - 1)
            second_layernorm(PAIRS - 1)
            route_tokens(PAIRS - 1)
            place_tokens(PAIRS - 1)


PER_ROUND = 98


def find_limits(nc, a, z_dram, limits_dram, prob, count, groups):
    with ExitStack() as ctx:
        def sb(name, shape, dt=F32):
            return ctx.enter_context(nc.sbuf_tensor("lim_" + name, shape, dt))

        def sem(name):
            return ctx.enter_context(nc.semaphore(name))

        NK = a["c_sizes"].shape[1] // E
        SPAN = 16
        steps = sb("steps", [HALF, PSTEPS + ISTEPS])
        region = sb("region", [HALF, E])
        tid = sb("tid", [HALF, NT])
        sizes = sb("sizes", [1, E, NK])
        upto = sb("upto", [1, E, E])
        number = sb("number", [1, NG])
        fill = sb("fill", [128, 2, ROW])
        ones = sb("ones", [HALF, HALF], BF16)
        hit = sb("hit", [HALF, E, NT], BF16)
        unlike = sb("unlike", [HALF, E, NT])
        late = sb("late", [HALF, E, NT])
        hits = sb("hits", [HALF, E])
        limit = sb("limit", [HALF, E, 2])
        trial = sb("trial", [HALF, E])
        good = sb("good", [HALF, E])
        short = sb("short", [HALF, E])
        kept = sb("kept", [1, E])
        over = sb("over", [1, E, NK])
        ng = sb("ng", [1, E])
        below = sb("below", [1, E, E])
        cum = sb("cum", [1, E])
        past = sb("past", [1, NG, E])
        first = sb("first", [1, NG])
        g_e = sb("g_e", [1, NG])
        g_row = sb("g_row", [1, NG])
        valid = sb("valid", [1, NG])
        ends = sb("ends", [1, E + 1], I32)
        total = ctx.enter_context(nc.psum_tensor("total", [128, 512], F32))

        tables_in, ones_made, counted, summed = sem("tables_in"), sem("lim_ones"), sem("lim_counted"), sem("lim_summed")
        chain_sem, ends_ready, limits_ready = sem("lim_chain"), sem("ends_ready"), sem("limits_ready")
        filled, limits_out = sem("filled"), sem("limits_out")
        block = ctx.enter_context(nc.Block())

        @block.sync
        def _(sp):
            for t, name in ((steps[:], "c_steps"), (region[:], "c_region"), (tid[:], "c_tid"),
                            (sizes[:].rearrange("p x y -> p (x y)"), "c_sizes"),
                            (upto[:].rearrange("p x y -> p (x y)"), "c_upto"), (number[:], "c_group"),
                            (fill[:].rearrange("p x y -> p (x y)"), "c_fill")):
                sp.dma_start(t, a[name]).then_inc(tables_in, 16)
            sp.wait_ge(tables_in, 112)
            sp.wait_ge(ends_ready, 1)
            for e in range(E + 1):
                end = sp.value_load(ends[0:1, e:e + 1], min_val=0, max_val=ZROWS - G)
                sp.dma_start(z_dram[bass.ds(end, G)].rearrange("(t p) f -> p t f", t=2), fill[:]).then_inc(filled, 16)
            sp.wait_ge(limits_ready, 1)
            sp.dma_start(limits_dram.rearrange("e x -> (e x)").unsqueeze(0),
                         limit[0:1].rearrange("p e x -> p (e x)")).then_inc(limits_out, 16)
            sp.wait_ge(filled, 16 * (E + 1))
            sp.wait_ge(limits_out, 16)

        @block.tensor
        def _(pe):
            pe.wait_ge(ones_made, 1)
            with pe.Fori(0, PSTEPS + 1 + ISTEPS) as i:
                pe.wait_ge(counted, i + 1)
                for k in range(NT // SPAN):
                    ins = pe.matmul(total[0:HALF, 0:E * SPAN], ones[:], hit[:, :, k * SPAN:(k + 1) * SPAN],
                                    start=(k == 0), stop=(k == NT // SPAN - 1))
                ins.then_inc(summed, 1)

        @block.vector
        def _(dve):
            chain = Chain(dve, chain_sem)
            wide = [HALF, E, NT]

            def count_hits(i, op, table, bound):
                dve.tensor_tensor(hit[:], table, bound.unsqueeze(2).broadcast_to(wide), op).then_inc(counted, 1)
                dve.wait_ge(summed, i + 1)
                chain.link(dve.tensor_reduce(hits[:], total[0:HALF, 0:E * SPAN].rearrange("p (e k) -> p e k", e=E),
                                             AX.X, ALU.add))

            dve.memset(ones[:], 1.0).then_inc(ones_made, 1)
            chain.link(dve.memset(limit[:], 0.0))
            dve.wait_ge(tables_in, 112)
            dve.tensor_copy(ends[:, 0:E], count[0:1])
            dve.memset(ends[:, E:E + 1], E * REGION).then_inc(ends_ready, 1)

            chain.link(dve.tensor_tensor(kept[:], count[0:1], region[0:1], ALU.subtract))
            chain.link(dve.tensor_tensor(over[:], kept[:].unsqueeze(2).broadcast_to([1, E, NK]), sizes[:], ALU.is_gt))
            chain.link(dve.tensor_reduce(ng[:], over[:], AX.X, ALU.add))
            chain.link(dve.tensor_tensor(below[:], upto[:], ng[:].unsqueeze(1).broadcast_to([1, E, E]), ALU.mult))
            chain.link(dve.tensor_reduce(cum[:], below[:], AX.X, ALU.add))
            chain.link(dve.tensor_tensor(past[:], number[:].unsqueeze(2).broadcast_to([1, NG, E]),
                                         cum[:].unsqueeze(1).broadcast_to([1, NG, E]), ALU.is_ge))
            chain.link(dve.tensor_reduce(g_e[:], past[:], AX.X, ALU.add))
            chain.link(dve.tensor_tensor(past[:], past[:], ng[:].unsqueeze(1).broadcast_to([1, NG, E]), ALU.mult))
            chain.link(dve.tensor_reduce(first[:], past[:], AX.X, ALU.add))
            chain.link(dve.tensor_tensor(first[:], number[:], first[:], ALU.subtract))
            chain.link(dve.tensor_scalar(valid[:], g_e[:], float(E), float(G), ALU.is_lt, ALU.mult))
            chain.link(dve.tensor_tensor(first[:], first[:], valid[:], ALU.mult))
            chain.link(dve.tensor_scalar(g_row[:], g_e[:], float(REGION), None, ALU.mult))
            chain.link(dve.tensor_tensor(g_row[:], g_row[:], first[:], ALU.add))
            chain.link(dve.tensor_copy(groups[:, :, 1], g_row[:]))
            chain.link(dve.tensor_scalar(groups[:, :, 0], g_e[:], float(E - 1), None, ALU.min))

            with dve.Fori(0, PSTEPS) as i:
                chain.enter(i, 4)
                step = steps[:, bass.ds(i, 1)]
                chain.link(dve.tensor_scalar(trial[:], limit[:, :, 0], step, None, ALU.add))
                count_hits(i, ALU.is_ge, prob, trial[:])
                chain.link(dve.tensor_scalar(good[:], hits[:], float(CAP), None, ALU.is_ge))
                chain.link(dve.scalar_tensor_tensor(out=limit[:, :, 0], in0=good[:], scalar=step, in1=limit[:, :, 0],
                                                    op0=ALU.mult, op1=ALU.add))
            chain.leave(PSTEPS)
            count_hits(PSTEPS, ALU.is_gt, prob, limit[:, :, 0])
            chain.link(dve.tensor_scalar(short[:], hits[:], -1.0, float(CAP), ALU.mult, ALU.add))
            chain.link(dve.tensor_tensor(unlike[:], prob, limit[:, :, 0:1].broadcast_to(wide), ALU.not_equal))
            chain.link(dve.scalar_tensor_tensor(out=late[:], in0=unlike[:], scalar=2 * EMPTY,
                                                in1=tid[:].unsqueeze(1).broadcast_to(wide), op0=ALU.mult, op1=ALU.add))
            with dve.Fori(0, ISTEPS) as i:
                chain.enter(i, 4)
                step = steps[:, bass.ds(i + PSTEPS, 1)]
                chain.link(dve.tensor_scalar(trial[:], limit[:, :, 1], step, None, ALU.add))
                count_hits(i + (PSTEPS + 1), ALU.is_lt, late[:], trial[:])
                chain.link(dve.tensor_tensor(good[:], hits[:], short[:], ALU.is_lt))
                chain.link(dve.scalar_tensor_tensor(out=limit[:, :, 1], in0=good[:], scalar=step, in1=limit[:, :, 1],
                                                    op0=ALU.mult, op1=ALU.add))
            chain.leave(ISTEPS)
            dve.tensor_scalar(limit[:, :, 1], limit[:, :, 1], 1.0, None, ALU.add).then_inc(limits_ready, 1)


def experts(nc, a, z_dram, limits_dram, groups, out):
    with ExitStack() as ctx:
        def sb(name, shape, dt=F32):
            return ctx.enter_context(nc.sbuf_tensor("ffn_" + name, shape, dt))

        def sem(name):
            return ctx.enter_context(nc.semaphore(name))

        T = G // 128
        S = SLOTS
        w1 = sb("w1", [DC, S, ND, F])
        w2 = sb("w2", [128, S, FM, D])
        b1 = sb("b1", [128, S, FM])
        b2 = sb("b2", [128, S, D])
        lim = sb("lim", [128, S, 2])
        rows = sb("rows", [128, S, T, ROW])
        xf = sb("xf", [128, S, T, D])
        xfT = sb("xfT", [DC, S, ND, G])
        hid = sb("hid", [128, S, FM, G])
        base = sb("base", [128, S, T, D])
        made = sb("made", [128, S, T, D])
        y = sb("y", [128, S, T, D])
        token = sb("token", [128, S, T], U32)
        above = sb("above", [128, S, T])
        same = sb("same", [128, S, T])
        mine = sb("mine", [128, S, T])
        rest = sb("rest", [128, S, T])
        ident = sb("ident", [128, 128])

        h_bank = [ctx.enter_context(nc.psum_tensor(f"ffn_h{i}", [128, 512], F32)) for i in range(3)]
        o_bank = [ctx.enter_context(nc.psum_tensor(f"ffn_o{i}", [128, 512], F32)) for i in range(2)]
        x_bank = [ctx.enter_context(nc.psum_tensor(f"ffn_x{i}", [128, 512], F32)) for i in range(2)]

        ident_in = sem("ident_in")
        group_in = [sem(f"group_in{s}") for s in range(S)]
        xf_made, xf_turned, xfT_copied = sem("ffn_xf_made"), sem("ffn_xf_turned"), sem("ffn_xfT_copied")
        h_made, h_active, o_made = sem("ffn_h_made"), sem("ffn_h_active"), sem("ffn_o_made")
        o_read, y_made = sem("ffn_o_read"), sem("ffn_y_made")
        y_out = [sem(f"ffn_y_out{s}") for s in range(S)]
        chain_sem, alone = sem("ffn_chain"), sem("ffn_alone")
        block = ctx.enter_context(nc.Block())
        LOADS = 6 * 16

        def group_of(i, s):
            return i * S + s

        @block.sync
        def _(sp):
            sp.dma_start(ident[:], a["c_ident"]).then_inc(ident_in, 16)

            def load(g, s):
                e = sp.value_load(groups[0:1, bass.ds(g, 1), 0], min_val=0, max_val=E - 1)
                r = sp.value_load(groups[0:1, bass.ds(g, 1), 1], min_val=0, max_val=ZROWS - G)
                sp.dma_start(rows[:, s], z_dram[bass.ds(r, G)].rearrange("(t p) f -> p t f", p=128)).then_inc(group_in[s], 16)
                sp.dma_start(w1[:, s], a["w1"][bass.ds(e, 1)].rearrange("o p c f -> (o p) c f")).then_inc(group_in[s], 16)
                sp.dma_start(w2[:, s], a["w2"][bass.ds(e, 1)].rearrange("o p m f -> (o p) m f")).then_inc(group_in[s], 16)
                sp.dma_start(b1[:, s], a["b1"][bass.ds(e, 1)].rearrange("o p m -> (o p) m")).then_inc(group_in[s], 16)
                sp.dma_start(b2[:, s], a["b2"][bass.ds(e, 1)].rearrange("o p f -> (o p) f")).then_inc(group_in[s], 16)
                sp.dma_start(lim[:, s], limits_dram[bass.ds(e, 1)].broadcast_to([128, 2])).then_inc(group_in[s], 16)

            for s in range(S):
                load(s, s)
            with sp.Fori(1, NG // S) as i:
                for s in range(S):
                    sp.wait_ge(y_made, i * S + (s + 1 - S))
                    load(i * S + s, s)

        @block.vector
        def _(dve):
            chain = Chain(dve, chain_sem)

            def normalize(i, s):
                dve.wait_ge(group_in[s], i * LOADS + LOADS)
                for t in range(T):
                    ins = dve.tensor_scalar(xf[:, s, t], rows[:, s, t, 0:D], rows[:, s, t, D:D + 1],
                                            rows[:, s, t, D + 1:D + 2], ALU.subtract, ALU.mult)
                ins.then_inc(xf_made, 1)

            def weigh(i, s):
                p, number = rows[:, s, :, D + 2], rows[:, s, :, D + 3]
                if later(i):
                    dve.wait_ge(y_out[s], i * (T * 16))
                dve.tensor_copy(token[:, s], number)
                dve.tensor_scalar(above[:, s], p, lim[:, s, 0:1], None, ALU.is_gt)
                chain.link(dve.tensor_scalar(same[:, s], p, lim[:, s, 0:1], None, ALU.is_equal))
                chain.link(dve.scalar_tensor_tensor(out=same[:, s], in0=number, scalar=lim[:, s, 1:2], in1=same[:, s],
                                                    op0=ALU.is_lt, op1=ALU.mult))
                chain.link(dve.tensor_tensor(above[:, s], above[:, s], same[:, s], ALU.add))
                chain.link(dve.tensor_tensor(mine[:, s], p, above[:, s], ALU.mult))
                chain.link(dve.tensor_tensor(rest[:, s], p, mine[:, s], ALU.subtract))
                for t in range(T):
                    ins = dve.scalar_tensor_tensor(out=base[:, s, t], in0=xf[:, s, t], scalar=rest[:, s, t:t + 1],
                                                   in1=rows[:, s, t, 0:D], op0=ALU.mult, op1=ALU.add)
                chain.link(ins)

            def combine(i, s):
                dve.wait_ge(o_made, group_of(i, s) + 1)
                src = o_bank[s % 2][:, 0:T * D].rearrange("p (t f) -> p t f", t=T)
                dve.tensor_tensor(made[:, s], src, b2[:, s].unsqueeze(1).broadcast_to([128, T, D]),
                                  ALU.add).then_inc(o_read, 1)
                dve.wait_ge(o_read, group_of(i, s) + 1)
                for t in range(T):
                    ins = dve.scalar_tensor_tensor(out=y[:, s, t], in0=made[:, s, t], scalar=mine[:, s, t:t + 1],
                                                   in1=base[:, s, t], op0=ALU.mult, op1=ALU.add)
                ins.then_inc(y_made, 1)

            def group(i, s):
                weigh(i, s)
                if s + 1 < S:
                    normalize(i, s + 1)
                elif not isinstance(i, int) or i + 1 < NG // S:
                    normalize(i + 1, 0)
                combine(i, s)

            normalize(0, 0)
            for s in range(S):
                group(0, s)
            with dve.Fori(1, NG // S - 1) as i:
                chain.enter(i - 1, 6 * S)
                for s in range(S):
                    group(i, s)
            chain.leave(NG // S - 2)
            for s in range(S):
                group(NG // S - 1, s)

        @block.tensor
        def _(pe):
            pe.wait_ge(ident_in, 16)

            def turn(i, s):
                pe.wait_ge(xf_made, group_of(i, s) + 1)
                if later(i) or s >= 2:
                    pe.wait_ge(xfT_copied, group_of(i, s) - 1)
                for c in range(ND):
                    for t in range(T):
                        ins = pe.transpose(x_bank[s % 2][0:DC, c * G + t * 128:c * G + (t + 1) * 128],
                                           xf[:, s, t, c * DC:(c + 1) * DC], ident[:])
                ins.then_inc(xf_turned, 1)

            def up(i, s):
                pe.wait_ge(xfT_copied, group_of(i, s) + 1)
                for m in range(FM):
                    if (later(i) or s) and m % 2 == 0:
                        pe.wait_ge(h_active, i * (S * FM) + (s - 1) * FM + (m + 2))
                    for c in range(ND):
                        ins = pe.matmul(h_bank[m // 2][:, m % 2 * G:(m % 2 + 1) * G], w1[:, s, c, m * 128:(m + 1) * 128],
                                        xfT[:, s, c], start=(c == 0), stop=(c == ND - 1))
                    if m % 2:
                        ins.then_inc(h_made, 1)

            def down(i, s):
                if later(i) or s >= 2:
                    pe.wait_ge(o_read, group_of(i, s) - 1)
                for t in range(T):
                    for m in range(FM):
                        if t == 0:
                            pe.wait_ge(h_active, i * (S * FM) + (s * FM + m + 1))
                        ins = pe.matmul(o_bank[s % 2][:, t * D:(t + 1) * D], hid[:, s, m, t * 128:(t + 1) * 128],
                                        w2[:, s, m], start=(m == 0), stop=(m == FM - 1))
                ins.then_inc(o_made, 1)

            def group(i, s):
                up(i, s)
                if s + 1 < S:
                    turn(i, s + 1)
                elif not isinstance(i, int) or i + 1 < NG // S:
                    turn(i + 1, 0)
                down(i, s)

            turn(0, 0)
            for s in range(S):
                group(0, s)
            with pe.Fori(1, NG // S - 1) as i:
                for s in range(S):
                    group(i, s)
            for s in range(S):
                group(NG // S - 1, s)

        @block.scalar
        def _(act):
            def copy_x(i, s):
                act.wait_ge(xf_turned, group_of(i, s) + 1)
                act.activation(xfT[:, s].rearrange("p c g -> p (c g)"), x_bank[s % 2][0:DC, 0:ND * G],
                               ACT.Copy).then_inc(xfT_copied, 1)

            def gelu(i, s):
                for m in range(FM):
                    if m % 2 == 0:
                        act.wait_ge(h_made, i * (S * FM // 2) + s * (FM // 2) + (m // 2 + 1))
                    act.activation(hid[:, s, m], h_bank[m // 2][:, m % 2 * G:(m % 2 + 1) * G], ACT.Gelu,
                                   bias=b1[:, s, m:m + 1]).then_inc(h_active, 1)

            def group(i, s):
                gelu(i, s)
                if s + 1 < S:
                    copy_x(i, s + 1)
                elif not isinstance(i, int) or i + 1 < NG // S:
                    copy_x(i + 1, 0)

            copy_x(0, 0)
            for s in range(S):
                group(0, s)
            with act.Fori(1, NG // S - 1) as i:
                for s in range(S):
                    group(i, s)
            for s in range(S):
                group(NG // S - 1, s)

        @block.gpsimd
        def _(pool):
            def scatter(i, s):
                pool.wait_ge(y_made, group_of(i, s) + 1).then_inc(alone, 1)
                for t in range(T):
                    pool.indirect_dma_start(out, bass.IndirectOffsetOnAxis(ap=token[:, s, t:t + 1], axis=0),
                                            y[:, s, t], None, bounds_check=TOKENS - 1,
                                            oob_is_err=False).then_inc(y_out[s], 16)

            with pool.Fori(0, NG // S) as i:
                for s in range(S):
                    scatter(i, s)
            for s in range(S):
                pool.wait_ge(y_out[s], 16 * T * (NG // S))


def laid_out(inputs):
    x = np.asarray(inputs["x"])
    c = np.ascontiguousarray
    x = x.reshape(B, C, 14, 16, 14, 16).transpose(2, 4, 3, 5, 1, 0).reshape(2, HALF, KC, 128, C, B)
    w = np.asarray(inputs["L0_tok_decode_weights"]).reshape(2, HALF, D, KC, 128)
    mw = np.asarray(inputs["L0_tok_merge_weights"]).reshape(2, HALF, C).transpose(1, 0, 2)
    out = {
        "pixels": c(x.transpose(1, 3, 0, 4, 2, 5)).reshape(HALF, 128, 2, C, KC * B),
        "decode": c(w.transpose(1, 4, 0, 3, 2)),
        "mw_b": np.broadcast_to(mw.reshape(1, -1), (128, HALF * 2 * C)).copy(),
        "mw_rows": c(mw),
        "dec_bias": c(np.asarray(inputs["L0_tok_decode_biases"]).reshape(2, HALF, D).transpose(1, 0, 2)),
        "merge_bias": c(np.asarray(inputs["L0_tok_merge_biases"]).reshape(2, HALF).T),
    }
    for n in ("Wq", "Wk", "Wv", "Wg"):
        out[n] = c(np.asarray(inputs["L0_attn_" + n]).reshape(ND, DC, -1).transpose(1, 0, 2))
    out["Wo"] = c(np.asarray(inputs["L0_attn_Wo"]).reshape(NP, 128, D).transpose(1, 0, 2))
    out["gn_w"] = c(np.asarray(inputs["L0_attn_gn_weight"]).reshape(NP, 128).T)
    out["gn_b"] = c(np.asarray(inputs["L0_attn_gn_bias"]).reshape(NP, 128).T)
    out["sw"] = c(np.asarray(inputs["L0_ffn_switch_w"]).reshape(ND, DC, E).transpose(1, 0, 2))
    out["sb"] = np.broadcast_to(np.tile(np.asarray(inputs["L0_ffn_switch_b"]), 4), (HALF, 4 * E)).copy()
    out["w1"] = c(np.asarray(inputs["L0_ffn_w1"]).reshape(E, ND, DC, F).transpose(0, 2, 1, 3))
    out["w2"] = c(np.asarray(inputs["L0_ffn_w2"]).reshape(E, FM, 128, D).transpose(0, 2, 1, 3))
    out["b1"] = c(np.asarray(inputs["L0_ffn_b1"]).reshape(E, FM, 128).transpose(0, 2, 1))
    out["b2"] = np.broadcast_to(np.asarray(inputs["L0_ffn_b2"])[:, None, :], (E, 128, D)).copy()
    out.update(constants())
    return out


def build(nc, a, out):
    h_dram = nc.dram_tensor("h_rows", (B, N, D), F32, kind="Internal").ap()
    bias_dram = nc.dram_tensor("bias_rows", (HALF, 2, D), F32, kind="Internal").ap()
    z_dram = nc.dram_tensor("dispatched", (ZROWS, ROW), F32, kind="Internal").ap()
    limits_dram = nc.dram_tensor("limits", (E, 2), F32, kind="Internal").ap()
    with ExitStack() as ctx:
        prob = ctx.enter_context(nc.sbuf_tensor("prob", [HALF, E, NT], F32))
        count = ctx.enter_context(nc.sbuf_tensor("count", [HALF, E], F32))
        groups = ctx.enter_context(nc.sbuf_tensor("groups", [1, NG, 2], I32))
        with nc.sbuf_tensor("xT", [DC, B, ND, N], F32) as xT:
            tokenize(nc, a, h_dram, bias_dram, xT[:])
            attend(nc, a, h_dram, z_dram, xT[:], prob[:], count)
        find_limits(nc, a, z_dram, limits_dram, prob[:], count, groups)
        experts(nc, a, z_dram, limits_dram, groups, out.rearrange("b n f -> (b n) f"))


def kernel(**inputs):
    import concourse.bacc as bacc
    from concourse.bass_utils import run_bass_kernel_spmd

    nc = bacc.Bacc("TRN2", target_bir_lowering=False, num_devices=1)
    arrays, a = {}, {}
    for name, value in laid_out(inputs).items():
        arrays["in_" + name] = value
        a[name] = nc.dram_tensor("in_" + name, value.shape, F32, kind="ExternalInput").ap()
    out = nc.dram_tensor("out", (B, N, D), F32, kind="ExternalOutput").ap()
    build(nc, a, out)
    r = run_bass_kernel_spmd(nc, [arrays], core_ids=[0])
    return r.results[0]["out"]
```

```python
from contextlib import ExitStack

import numpy as np
import concourse.bass as bass
from concourse import mybir

ALU = mybir.AluOpType
ACT = mybir.ActivationFunctionType
AX = mybir.AxisListType
F32 = mybir.dt.float32
I32 = mybir.dt.int32
U32 = mybir.dt.uint32
BF16 = mybir.dt.bfloat16

B = 64
C = 3
N = 196
PD = 256
D = 192
H = 6
DQK = 128
DV = 64
E = 8
F = 768
HALF = N // 2
KC = PD // 128
DC = 96
ND = D // DC
NP = H // 2
NT = 2 * B
PAIRS = B // 2
TOKENS = B * N
CAP = int(1.25 * TOKENS / E)
EPS = 1e-5

RING = 7
ROUNDS = HALF // RING

G = 256
FM = F // 128
REGION = TOKENS + G
ZROWS = E * REGION + G
NG = (TOKENS + E * (G - 1)) // G
SLOTS = 4
NG += -NG % SLOTS
ROW = D + 4
EMPTY = 16384.0
PSTEPS = 28
ISTEPS = 14
TRIES = 2 * SLOTS - 1
PROUNDS = PSTEPS // TRIES
EARLY = PROUNDS + ISTEPS // TRIES
ROUNDS_OF_GROUPS = NG // SLOTS
FIXES = -(-EARLY * SLOTS // (ROUNDS_OF_GROUPS - EARLY))
assert FIXES <= SLOTS and FIXES * (ROUNDS_OF_GROUPS - EARLY) == EARLY * SLOTS


def constants():
    f = np.float32
    pos = np.arange(N, dtype=f)
    half = DQK // 2
    inv = (f(1.0) / f(10000.0) ** (np.arange(half, dtype=f) / f(half))).astype(f)
    angle = pos[:, None] * inv[None, :]
    zeta = (np.arange(half, dtype=f) + f(half)) / f(DQK)
    cos_t = np.zeros((128, 2, N), f)
    sin_t = np.zeros((128, 2, N), f)
    for k, sign in enumerate((1.0, -1.0)):
        decay = zeta[None, :] ** (f(sign) * pos[:, None] / f(512.0))
        c = (np.cos(angle) * decay).T.astype(f)
        s = (np.sin(angle) * decay).T.astype(f)
        cos_t[:, k] = np.concatenate([c, c])
        sin_t[:, k] = np.concatenate([-s, s])
    gam = np.array([1.0 - 2.0 ** (-(5 + h)) for h in range(H)], dtype=f)
    diff = pos[:, None] - pos[None, :]
    dm = gam[:, None, None] ** np.maximum(diff, 0)[None] * (diff >= 0).astype(f)[None]
    row = np.maximum(dm.sum(-1, keepdims=True), 1e-6)
    dm = (dm / np.sqrt(row) * DQK ** -0.5).astype(f)
    dmt = dm.transpose(2, 0, 1)
    mask = np.concatenate([dmt[:HALF], dmt[HALF:, :, HALF:]], axis=2)
    blk = np.zeros((128, 128), f)
    blk[:64, :64] = blk[64:, 64:] = 1.0 / 64
    steps = np.zeros((PSTEPS + ISTEPS,), f)
    steps[:PSTEPS] = 0.5 ** np.arange(1, PSTEPS + 1)
    steps[PSTEPS:] = 2.0 ** np.arange(ISTEPS - 1, -1, -1)
    tid = (np.arange(NT)[None, :] * HALF + np.arange(HALF)[:, None]).astype(f)
    NK = -(-TOKENS // G)
    fill = np.zeros((128, 2 * ROW), f)
    fill[:, ROW - 1] = fill[:, 2 * ROW - 1] = EMPTY
    regs = (np.arange(E) * REGION).astype(f)
    return {
        "c_cos": cos_t.reshape(128, -1), "c_sin": sin_t.reshape(128, -1),
        "c_mask": np.ascontiguousarray(mask).reshape(HALF, -1),
        "c_block": blk, "c_ident": np.eye(128, dtype=f),
        "c_before": np.triu(np.ones((HALF, HALF), f), 1),
        "c_steps": np.broadcast_to(steps, (HALF, PSTEPS + ISTEPS)).copy(),
        "c_tid": tid,
        "c_region": np.broadcast_to(regs, (HALF, E)).copy(),
        "c_expert": np.broadcast_to(np.tile(np.arange(E, dtype=f), 4), (HALF, 4 * E)).copy(),
        "c_fill": fill,
        "c_sizes": np.broadcast_to(np.arange(NK, dtype=f) * G, (E, NK)).reshape(1, -1).copy(),
        "c_upto": np.tril(np.ones((E, E), f)).reshape(1, -1),
        "c_group": np.arange(NG, dtype=f).reshape(1, -1),
    }


class Chain:

    def __init__(self, eng, sem):
        self.eng, self.sem, self.n, self.off = eng, sem, 0, None

    def now(self):
        return self.n if self.off is None else self.off + self.n

    def enter(self, i, per):
        self.per, self.base = per, self.n
        self.off = i * per + self.base
        self.n = 0

    def leave(self, passes):
        assert self.n == self.per, (self.n, self.per)
        self.off, self.n = None, self.base + passes * self.per

    def link(self, ins, alone=None):
        self.n += 1
        ins.then_inc(self.sem, 1)
        wait = self.eng.wait_ge(self.sem, self.now())
        if alone is not None:
            wait.then_inc(alone, 1)


def later(r):
    return not isinstance(r, int) or r > 0


def before(r, s, d):
    return (r, s - d) if s >= d else (r - 1, s - d + RING)


def rsqrt(dve, chain, v, y, t):
    chain.link(dve.tensor_scalar(t.bitcast(I32), v.bitcast(I32), 1, None, ALU.logical_shift_right))
    chain.link(dve.tensor_scalar(y.bitcast(I32), t.bitcast(I32), -1, 0x5F3759DF, ALU.mult, ALU.add))
    for _ in range(3):
        chain.link(dve.scalar_tensor_tensor(out=t, in0=y, scalar=-0.5, in1=y, op0=ALU.mult, op1=ALU.mult))
        chain.link(dve.tensor_tensor(t, t, v, ALU.mult))
        chain.link(dve.scalar_tensor_tensor(out=y, in0=t, scalar=1.5, in1=y, op0=ALU.add, op1=ALU.mult))


def tokenize(nc, a, h_dram, bias_dram, xT):
    with ExitStack() as ctx:
        def sb(name, shape, dt=F32):
            return ctx.enter_context(nc.sbuf_tensor("tok_" + name, shape, dt))

        def sem(name):
            return ctx.enter_context(nc.semaphore(name))

        PIXELS, WEIGHTS = 2 * C * KC * B, 2 * KC * D
        patches = sb("patches", [128, RING, PIXELS + WEIGHTS])
        pix = patches[:, :, 0:PIXELS].rearrange("p s (u c q) -> p s u c q", u=2, c=C)
        wts = patches[:, :, PIXELS:].rearrange("p s (u k f) -> p s u k f", u=2, k=KC)
        brow = sb("brow", [1, RING, 2, D])
        mix = sb("mix", [128, RING, 2, KC * B])
        hs = sb("hs", [128, RING, D])
        xn = sb("xn", [128, RING, D])
        st = sb("st", [128, RING, 6])
        mv = sb("mv", [128, RING, 2])
        sd = sb("sd", [128, RING])
        rs = sb("rs", [128, RING])
        eps = sb("eps", [128, 1])
        ones = sb("ones", [1, B])
        ident = sb("ident", [128, 128])
        mwb = sb("mwb", [128, HALF * 2 * C])
        dbias = sb("dbias", [HALF, 2, D])
        mrow = sb("mrow", [HALF, 2, C])
        mbias = sb("mbias", [HALF, 2])
        msum = sb("msum", [HALF, 2])
        banks = [ctx.enter_context(nc.psum_tensor(f"tok{i}", [128, 512], F32)) for i in range(8)]
        HB = [0, 1, 2, 3, 0, 1, 2]
        TB = [4, 5, 6, 4, 5, 6, 7]

        const_in, bias_in = sem("tok_const_in"), sem("tok_bias_in")
        pair_in = [sem(f"tok_pair_in{s}") for s in range(RING)]
        brow_in = [sem(f"tok_brow_in{s}") for s in range(RING)]
        h_out = [sem(f"tok_h_out{s}") for s in range(RING)]
        bias_made, bias_kept = sem("bias_made"), sem("bias_kept")
        setup, scaled, half_mixed, mixed = sem("tok_setup"), sem("scaled"), sem("half_mixed"), sem("mixed")
        multiplied, h_copied, counted, rooted = sem("multiplied"), sem("h_copied"), sem("counted"), sem("rooted")
        inverted, normed, turned, xt_copied = sem("inverted"), sem("normed"), sem("turned"), sem("xt_copied")
        chain_sem, alone = sem("tok_chain"), sem("tok_alone")

        def back(banks_of, s):
            return next(d for d in range(1, RING + 1) if banks_of[(s - d) % RING] == banks_of[s])

        block = ctx.enter_context(nc.Block())

        @block.sync
        def _(sp):
            sp.dma_start(dbias[:], a["dec_bias"]).then_inc(bias_in, 16)
            sp.dma_start(mrow[:], a["mw_rows"]).then_inc(bias_in, 16)
            sp.dma_start(mbias[:], a["merge_bias"]).then_inc(bias_in, 16)
            sp.dma_start(mwb[:], a["mw_b"]).then_inc(const_in, 16)

            def load(j, s):
                sp.dma_start(patches[:, s], a["patches"][bass.ds(j, 1)].rearrange("o p x -> (o p) x")).then_inc(pair_in[s], 16)

            def load_bias(j, s):
                sp.dma_start(brow[:, s], bias_dram[bass.ds(j, 1)]).then_inc(brow_in[s], 16)

            def store(j, s):
                sp.dma_start(h_dram[bass.ds(j, 1)].rearrange("o u b f -> (o u b) f"), hs[:, s]).then_inc(h_out[s], 16)

            load(0, 0)
            sp.dma_start(ident[:], a["c_ident"]).then_inc(const_in, 16)
            load(1, 1)
            load(2, 2)
            sp.wait_ge(bias_kept, 16)
            for s in range(RING):
                if s >= 3:
                    load(s, s)
                load_bias(s, s)
            with sp.Fori(1, ROUNDS) as r:
                for s in range(RING):
                    sp.wait_ge(multiplied, (r - 1) * RING + (s + 1))
                    load(r * RING + s, s)
                    load_bias(r * RING + s, s)
                    sp.wait_ge(h_copied, (r - 1) * RING + (s + 1))
                    store((r - 1) * RING + s, s)
            for s in range(RING):
                sp.wait_ge(h_copied, (ROUNDS - 1) * RING + s + 1)
                store((ROUNDS - 1) * RING + s, s)
            for s in range(RING):
                sp.wait_ge(h_out[s], 16 * ROUNDS)

        @block.gpsimd
        def _(pool):
            pool.wait_ge(bias_made, 2)
            pool.dma_start(bias_dram.rearrange("i u f -> i (u f)"), dbias[:].rearrange("i u f -> i (u f)")).then_inc(bias_kept, 16)

        @block.scalar
        def _(act):
            act.wait_ge(const_in, 32)
            act.wait_ge(setup, 2)

            def scale_first_channel(r, s):
                act.wait_ge(pair_in[s], r * 16 + 16)
                for u in range(2):
                    ins = act.activation(mix[:, s, u], pix[:, s, u, 0], ACT.Copy,
                                         scale=mwb[:, bass.ds(r * (RING * 2 * C) + (s * 2 + u) * C, 1)])
                ins.then_inc(scaled, 1)

            def copy_h(r, s):
                act.wait_ge(multiplied, r * RING + (s + 1))
                if later(r):
                    act.wait_ge(h_out[s], r * 16)
                act.activation(hs[:, s], banks[HB[s]][:, 0:D], ACT.Copy).then_inc(h_copied, 1)

            def root(r, s):
                act.wait_ge(counted, r * RING + (s + 1))
                act.activation(sd[:, s:s + 1], mv[:, s, 1:2], ACT.Sqrt, bias=eps[:]).then_inc(rooted, 1)

            def copy_xt(r, s):
                act.wait_ge(turned, r * RING + (s + 1))
                for c in range(ND):
                    src = banks[TB[s]][0:DC, c * 128:(c + 1) * 128].rearrange("p (u b) -> p u b", u=2)
                    dst = xT.rearrange("p b c (u i) -> p c u b i", u=2)[:, c, :, :, bass.ds(r * RING + s, 1)]
                    ins = act.activation(dst.rearrange("p u b o -> p u (b o)"), src, ACT.Copy)
                ins.then_inc(xt_copied, 1)

            def step(r, s):
                scale_first_channel(r, s)
                if later(r) or s >= 1:
                    copy_h(*before(r, s, 1))
                if later(r) or s >= 2:
                    root(*before(r, s, 2))
                if later(r) or s >= 4:
                    copy_xt(*before(r, s, 4))

            for r in range(2):
                for s in range(RING):
                    step(r, s)
            with act.Fori(2, ROUNDS) as r:
                for s in range(RING):
                    step(r, s)
            copy_h(ROUNDS - 1, RING - 1)
            for s in range(RING - 2, RING):
                root(ROUNDS - 1, s)
            for s in range(RING - 4, RING):
                copy_xt(ROUNDS - 1, s)

        @block.vector
        def _(dve):
            chain = Chain(dve, chain_sem)
            dve.memset(eps[:], EPS).then_inc(setup, 1)
            dve.memset(ones[:], 1.0).then_inc(setup, 1)
            dve.wait_ge(bias_in, 48)
            chain.link(dve.tensor_reduce(msum[:], mrow[:], AX.X, ALU.add))
            for u in range(2):
                dve.tensor_scalar(dbias[:, u], dbias[:, u], msum[:, u:u + 1], mbias[:, u:u + 1],
                                  ALU.mult, ALU.add).then_inc(bias_made, 1)

            dve.wait_ge(const_in, 32)

            def merge_channels(r, s):
                dve.wait_ge(scaled, r * RING + (s + 1))
                for c in range(1, C):
                    for u in range(2):
                        ins = dve.scalar_tensor_tensor(
                            out=mix[:, s, u], in0=pix[:, s, u, c],
                            scalar=mwb[:, bass.ds(r * (RING * 2 * C) + (s * 2 + u) * C + c, 1)],
                            in1=mix[:, s, u], op0=ALU.mult, op1=ALU.add)
                    if c == 1:
                        ins.then_inc(half_mixed, 1)
                        dve.wait_ge(half_mixed, r * RING + (s + 1))
                ins.then_inc(mixed, 1)

            def count(r, s):
                dve.wait_ge(h_copied, r * RING + (s + 1))
                chain.link(dve.bn_stats(st[:, s], hs[:, s]), alone)
                dve.bn_aggr(mv[:, s], st[:, s]).then_inc(counted, 1)

            def normalize(r, s):
                dve.wait_ge(rooted, r * RING + (s + 1))
                dve.reciprocal(rs[:, s:s + 1], sd[:, s:s + 1]).then_inc(inverted, 1)
                dve.wait_ge(inverted, r * RING + (s + 1))
                dve.tensor_scalar(xn[:, s], hs[:, s], mv[:, s, 0:1], rs[:, s:s + 1],
                                  ALU.subtract, ALU.mult).then_inc(normed, 1)

            def step(r, s):
                merge_channels(r, s)
                if later(r) or s >= 1:
                    count(*before(r, s, 1))
                if later(r) or s >= 2:
                    normalize(*before(r, s, 2))

            for s in range(RING):
                step(0, s)
            with dve.Fori(1, ROUNDS) as r:
                chain.enter(r - 1, RING)
                for s in range(RING):
                    step(r, s)
            chain.leave(ROUNDS - 1)
            count(ROUNDS - 1, RING - 1)
            for s in range(RING - 2, RING):
                normalize(ROUNDS - 1, s)

        @block.tensor
        def _(pe):
            pe.wait_ge(const_in, 32)
            pe.wait_ge(setup, 2)

            def product(r, s):
                pe.wait_ge(mixed, r * RING + (s + 1))
                if later(r) or s >= back(HB, s):
                    pe.wait_ge(h_copied, r * RING + (s + 1 - back(HB, s)))
                for u in range(2):
                    out = banks[HB[s]][u * B:(u + 1) * B, 0:D]
                    for k in range(KC):
                        pe.matmul(out, mix[:, s, u, k * B:(k + 1) * B], wts[:, s, u, k], start=(k == 0), stop=False)
                    if u == 0:
                        pe.wait_ge(brow_in[s], r * 16 + 16)
                    ins = pe.matmul(out, ones[:], brow[:, s, u], start=False, stop=True)
                ins.then_inc(multiplied, 1)

            def turn(r, s):
                pe.wait_ge(normed, r * RING + (s + 1))
                if later(r) or s >= back(TB, s):
                    pe.wait_ge(xt_copied, r * RING + (s + 1 - back(TB, s)))
                for c in range(ND):
                    ins = pe.transpose(banks[TB[s]][0:DC, c * 128:(c + 1) * 128], xn[:, s, c * DC:(c + 1) * DC], ident[:])
                ins.then_inc(turned, 1)

            def step(r, s):
                product(r, s)
                if later(r) or s >= 3:
                    turn(*before(r, s, 3))

            for r in range(2):
                for s in range(RING):
                    step(r, s)
            with pe.Fori(2, ROUNDS) as r:
                for s in range(RING):
                    step(r, s)
            for s in range(RING - 3, RING):
                turn(ROUNDS - 1, s)


class Plan:

    def __init__(self, ctx, nc, a):
        def sb(name, shape, dt=F32):
            return ctx.enter_context(nc.sbuf_tensor("plan_" + name, shape, dt))

        self.NK = a["c_sizes"].shape[1] // E
        self.region = sb("region", [1, E])
        self.sizes = sb("sizes", [1, E, self.NK])
        self.upto = sb("upto", [1, E, E])
        self.number = sb("number", [1, NG])
        self.fill = sb("fill", [128, 2, ROW])
        self.kept = sb("kept", [1, E])
        self.ng = sb("ng", [1, E])
        self.cum = sb("cum", [1, E])
        self.first = sb("first", [1, NG])
        self.g_e = sb("g_e", [1, NG])
        self.g_row = sb("g_row", [1, NG])
        self.valid = sb("valid", [1, NG])
        self.ends = sb("ends", [1, E + 1], I32)
        self.loads = ((self.region[:], a["c_region"][0:1]),
                      (self.sizes[:].rearrange("p x y -> p (x y)"), a["c_sizes"]),
                      (self.upto[:].rearrange("p x y -> p (x y)"), a["c_upto"]), (self.number[:], a["c_group"]),
                      (self.fill[:].rearrange("p x y -> p (x y)"), a["c_fill"]))


def plan_groups(dve, chain, plan, over, below, past, count, groups):
    NK, kept, ng, cum, number = plan.NK, plan.kept, plan.ng, plan.cum, plan.number
    first, g_e, g_row, valid = plan.first, plan.g_e, plan.g_row, plan.valid
    chain.link(dve.tensor_tensor(kept[:], count[0:1], plan.region[:], ALU.subtract))
    chain.link(dve.tensor_tensor(over, kept[:].unsqueeze(2).broadcast_to([1, E, NK]), plan.sizes[:], ALU.is_gt))
    chain.link(dve.tensor_reduce(ng[:], over, AX.X, ALU.add))
    chain.link(dve.tensor_tensor(below, plan.upto[:], ng[:].unsqueeze(1).broadcast_to([1, E, E]), ALU.mult))
    chain.link(dve.tensor_reduce(cum[:], below, AX.X, ALU.add))
    chain.link(dve.tensor_tensor(past, number[:].unsqueeze(2).broadcast_to([1, NG, E]),
                                 cum[:].unsqueeze(1).broadcast_to([1, NG, E]), ALU.is_ge))
    chain.link(dve.tensor_reduce(g_e[:], past, AX.X, ALU.add))
    chain.link(dve.tensor_tensor(past, past, ng[:].unsqueeze(1).broadcast_to([1, NG, E]), ALU.mult))
    chain.link(dve.tensor_reduce(first[:], past, AX.X, ALU.add))
    chain.link(dve.tensor_tensor(first[:], number[:], first[:], ALU.subtract))
    chain.link(dve.tensor_scalar(valid[:], g_e[:], float(E), float(G), ALU.is_lt, ALU.mult))
    chain.link(dve.tensor_tensor(first[:], first[:], valid[:], ALU.mult))
    chain.link(dve.tensor_scalar(g_row[:], g_e[:], float(REGION), None, ALU.mult))
    chain.link(dve.tensor_tensor(g_row[:], g_row[:], first[:], ALU.add))
    chain.link(dve.tensor_copy(groups[:, :, 1], g_row[:]))
    chain.link(dve.tensor_scalar(groups[:, :, 0], g_e[:], float(E - 1), None, ALU.min))


def attend(nc, a, h_dram, z_dram, xT, prob, count, groups):
    with ExitStack() as ctx:
        def sb(name, shape, dt=F32):
            return ctx.enter_context(nc.sbuf_tensor("att_" + name, shape, dt))

        def sem(name):
            return ctx.enter_context(nc.semaphore(name))

        wq = sb("wq", [DC, ND, H * DQK])
        wk = sb("wk", [DC, ND, H * DQK])
        wv = sb("wv", [DC, ND, H * DV])
        wg = sb("wg", [DC, ND, H * DV])
        wo = sb("wo", [128, NP, D])
        gnw = sb("gnw", [128, NP])
        gnb = sb("gnb", [128, NP])
        sw = sb("sw", [DC, ND, E])
        swb = sb("swb", [HALF, 4, E])
        cos_t = sb("cos_t", [128, 2, N])
        sin_t = sb("sin_t", [128, 2, N])
        mask = sb("mask", [HALF, H, N + HALF])
        block64 = sb("block64", [128, 128])
        ident = sb("ident2", [128, 128])
        earlier = sb("earlier", [HALF, HALF])
        ones = sb("ones2", [HALF, HALF])
        tid = sb("tid", [HALF, NT])
        plan = Plan(ctx, nc, a)
        expert = sb("expert", [HALF, 4, E])

        x = sb("x", [DC, 2, ND, N])
        hres = sb("hres", [HALF, 4, D])
        v = sb("v", [HALF, 2, 2, H * DV])
        swapped = sb("swapped", [128, 3, 2, N])
        straight = sb("straight", [128, 3, 2, N])
        rot = sb("rot", [128, 2 * NP, 2, N])
        sm = sb("sm", [HALF, H, N + HALF])
        cc = sb("cc", [128, 2, 2, NP, N])
        gate = sb("gate", [128, 2, 2, NP, N])
        gst = sb("gst", [128, 2, NP, 6])
        gmv = sb("gmv", [128, 2, NP, 2])
        gs = sb("gs", [128, 2, 2, NP])
        gg = sb("gg", [128, 2, 2, NP])
        gv, gy, gt = sb("gv", [128, 2, NP]), sb("gy", [128, 2, NP]), sb("gt", [128, 2, NP])
        ga, gb = sb("ga", [128, 2, NP]), sb("gb", [128, 2, NP])
        row = sb("row", [HALF, 4, ROW])
        lst = sb("lst", [HALF, 4, 6])
        lmv = sb("lmv", [HALF, 4, 2])
        lv, lt, ly = sb("lv", [HALF, 4]), sb("lt", [HALF, 4]), sb("ly", [HALF, 4])
        xf = sb("xf", [HALF, 4, D])
        xfT = sb("xfT", [DC, 2, ND, N])
        z = sb("logits", [HALF, 4, E])
        zmax = sb("zmax", [HALF, 4])
        ez = sb("ez", [HALF, 4, E])
        rank = sb("rank", [HALF, 4, E])
        route = sb("route", [HALF, 4])
        esum = sb("esum", [HALF, 4])
        chosen = sb("chosen", [HALF, 5, E])
        slot = sb("slot", [HALF, 4])
        slot_i = sb("slot_i", [HALF, 4], U32)

        qk_bank = [ctx.enter_context(nc.psum_tensor(f"qk{i}", [128, 512], F32)) for i in range(3)]
        s_bank = [ctx.enter_context(nc.psum_tensor(f"s{i}", [128, 512], F32)) for i in range(2)]
        o_bank = ctx.enter_context(nc.psum_tensor("o_bank", [128, 512], F32))
        ma = ctx.enter_context(nc.psum_tensor("ma", [128, 512], F32))
        mb = ctx.enter_context(nc.psum_tensor("mb", [128, 512], F32))

        v_weights_in, qk_weights_in, weights_in = sem("v_weights_in"), sem("qk_weights_in"), sem("weights_in")
        ones_made = sem("ones_made")
        x_in = [sem(f"x_in{i}") for i in range(2)]
        res_in, res_added = sem("res_in"), sem("res_added")
        v_made, v_copied = sem("v_made"), sem("v_copied")
        g_made, g_tanh, g_gated = sem("g_made"), sem("g_tanh"), sem("g_gated")
        qk_made, qk_swapped, qk_straight, qk_turned, qk_rotated = (
            sem("qk_made"), sem("qk_swapped"), sem("qk_straight"), sem("qk_turned"), sem("qk_rotated"))
        s_made, s_decayed = sem("s_made"), sem("s_decayed")
        o_made, o_copied, stats_ready, stats_summed, stats_read = (
            sem("o_made"), sem("o_copied"), sem("stats_ready"), sem("stats_summed"), sem("stats_read"))
        scale_ready, outputs_normalized = sem("scale_ready"), sem("outputs_normalized")
        gated_ready, wo_made = sem("gated_ready"), sem("wo_made")
        xf_ready, xf_turned, xfT_copied = sem("xf_ready"), sem("xf_turned"), sem("xfT_copied")
        z_made, z_shifted, z_exped = sem("z_made"), sem("z_shifted"), sem("z_exped")
        chosen_ready, prefix_made, prefix_read = sem("chosen_ready"), sem("prefix_made"), sem("prefix_read")
        slots_ready, rows_out = sem("slots_ready"), sem("rows_out")
        plan_in, ends_ready, filled = sem("plan_in"), sem("ends_ready"), sem("filled")
        chain_sem, alone = sem("att_chain"), sem("att_alone")

        block = ctx.enter_context(nc.Block())
        qk_loads = [(wq, "Wq"), (wk, "Wk"), (cos_t, "c_cos"), (sin_t, "c_sin")]
        loads = [(wg, "Wg"), (wo, "Wo"), (gnw, "gn_w"), (gnb, "gn_b"),
                 (sw, "sw"), (swb, "sb"), (mask, "c_mask"),
                 (block64, "c_block"), (ident, "c_ident"), (earlier, "c_before"), (tid, "c_tid"),
                 (expert, "c_expert"), (count, "c_region")]
        QK_IN, ALL_IN = 16 * len(qk_loads), 16 * len(loads)

        def two(t):
            return t.unsqueeze(1).broadcast_to([128, 2, N])

        def mark_empty(queue, experts_of_queue):
            queue.wait_ge(plan_in, 16 * len(plan.loads))
            queue.wait_ge(ends_ready, 1)
            for e in experts_of_queue:
                end = queue.value_load(plan.ends[0:1, e:e + 1], min_val=0, max_val=ZROWS - G)
                queue.dma_start(z_dram[bass.ds(end, G)].rearrange("(t p) f -> p t f", t=2), plan.fill[:]).then_inc(filled, 16)

        @block.sync
        def _(sp):
            def load_x(b, i):
                sp.dma_start(x[:, i], xT[:, bass.ds(b, 1)].rearrange("p o c n -> p (o c) n")).then_inc(x_in[i], 16)

            def load_residual(p):
                for i in range(2):
                    sp.dma_start(hres[:, i * 2:i * 2 + 2],
                                 h_dram[:, :, bass.ds(p * 2 + i, 1)].rearrange("q t i f -> q t (i f)")).then_inc(res_in, 16)

            sp.dma_start(wv[:].rearrange("p x y -> p (x y)"), a["Wv"].rearrange("p x y -> p (x y)")).then_inc(v_weights_in, 16)
            for i in range(2):
                load_x(i, i)
            for k, (t, name) in enumerate(qk_loads + loads):
                dst = t[:] if len(t.shape) == 2 else t[:].rearrange("p x y -> p (x y)")
                src = a[name] if len(a[name].shape) == 2 else a[name].rearrange("p x y -> p (x y)")
                sp.dma_start(dst, src).then_inc(qk_weights_in if k < len(qk_loads) else weights_in, 16)
            load_residual(0)

            def next_x(p, i):
                sp.wait_ge(qk_made, p * 12 - (6 - i * 6))
                load_x(p * 2 + i, i)

            def next_residual(p):
                sp.wait_ge(res_added, p * 2)
                load_residual(p)

            next_x(1, 0)
            next_x(1, 1)
            with sp.Fori(2, PAIRS) as p:
                next_x(p, 0)
                next_residual(p - 1)
                next_x(p, 1)
            next_residual(PAIRS - 1)
            for dst, src in plan.loads:
                sp.dma_start(dst, src).then_inc(plan_in, 16)
            mark_empty(sp, range(0, E // 2))
            sp.wait_ge(filled, 16 * (E + 1))

        @block.tensor
        def _(pe):
            pe.wait_ge(v_weights_in, 16)

            def product(out, lhs, rhs):
                for c in range(ND):
                    ins = pe.matmul(out, lhs(c), rhs(c), start=(c == 0), stop=(c == ND - 1))
                return ins

            def values(p, i, t, free=None):
                b = p * 2 + i
                if t == 0:
                    pe.wait_ge(x_in[i], p * 16 + 16)
                if free is not None:
                    pe.wait_ge(*free)
                product((ma, mb)[t][0:HALF, 0:H * DV], lambda c: x[:, i, c, t * HALF:(t + 1) * HALF],
                        lambda c: wv[:, c]).then_inc(v_made, 1)

            def gates(p, i, part):
                pe.wait_ge(v_copied, (p * 2 + i) * 2 + (part + 1))
                bank = (ma, mb)[part]
                for n, m in enumerate(((0, 1), (2,))[part]):
                    ins = product(bank[:, n * N:(n + 1) * N], lambda c: wg[:, c, m * 128:(m + 1) * 128],
                                  lambda c: x[:, i, c])
                ins.then_inc(g_made, 1)

            def project(p, i, n):
                b = p * 2 + i
                if later(b) or n >= 3:
                    pe.wait_ge(qk_straight, b * 6 + (n - 2))
                w = (wq, wk)[n % 2]
                for j in range(2):
                    h = n // 2 * 2 + j
                    ins = product(qk_bank[n % 3][:, j * N:(j + 1) * N],
                                  lambda c: w[:, c, h * DQK:(h + 1) * DQK], lambda c: x[:, i, c])
                ins.then_inc(qk_made, 1)

            def scores(p, i, hp):
                b = p * 2 + i
                pe.wait_ge(qk_rotated, b * 6 + (2 * hp + 2))
                for j in range(2):
                    h = 2 * hp + j
                    if later(b) or h >= 2:
                        pe.wait_ge(s_decayed, b * 6 + (h - 1))
                    q, k = rot[:, 2 * hp, j], rot[:, 2 * hp + 1, j]
                    pe.matmul(s_bank[j][0:HALF, 0:N], k[:, 0:HALF], q[:, 0:N], start=True, stop=True)
                    pe.matmul(s_bank[j][0:HALF, N:N + HALF], k[:, HALF:N], q[:, HALF:N],
                              start=True, stop=True).then_inc(s_made, 1)

            def outputs(p, i, hp):
                b = p * 2 + i
                pe.wait_ge(s_decayed, b * 6 + (2 * hp + 2))
                if later(b) or hp >= 1:
                    pe.wait_ge(o_copied, b * 3 + hp)
                for j in range(2):
                    h = 2 * hp + j
                    at = slice(j * DV, (j + 1) * DV)
                    pe.matmul(o_bank[at, 0:N], v[:, i, 0, h * DV:(h + 1) * DV], sm[:, h, 0:N], start=True, stop=False)
                    ins = pe.matmul(o_bank[at, HALF:N], v[:, i, 1, h * DV:(h + 1) * DV], sm[:, h, N:N + HALF],
                                    start=False, stop=True)
                ins.then_inc(o_made, 1)

            def group_statistics(tail, *free):
                pe.wait_ge(stats_ready, tail + 1)
                pe.wait_ge(*free)
                pe.matmul(ma[:, 0:4 * NP], block64[:], gs[:].rearrange("p s i n -> p (s i n)"),
                          start=True, stop=True).then_inc(stats_summed, 1)

            def project_out(tail, par, i, *free):
                bank = (ma, mb)[i]
                pe.wait_ge(gated_ready, tail + 1)
                pe.wait_ge(*free)
                for t in range(2):
                    for m in range(NP):
                        ins = pe.matmul(bank[0:HALF, t * D:(t + 1) * D], cc[:, par, i, m, t * HALF:(t + 1) * HALF],
                                        wo[:, m], start=(m == 0), stop=(m == NP - 1))
                ins.then_inc(wo_made, 1)

            def turn(tail, i, *free):
                bank = (mb, ma)[i]
                pe.wait_ge(xf_ready, tail * 2 + (i + 1))
                pe.wait_ge(*free)
                for c in range(ND):
                    for t in range(2):
                        ins = pe.transpose(bank[0:DC, c * N + t * HALF:c * N + (t + 1) * HALF],
                                           xf[:, i * 2 + t, c * DC:(c + 1) * DC], ident[0:HALF, 0:HALF])
                ins.then_inc(xf_turned, 1)

            def logits(tail):
                pe.wait_ge(xfT_copied, tail * 2 + 2)
                for t in range(4):
                    for c in range(ND):
                        ins = pe.matmul(ma[0:HALF, t * E:(t + 1) * E],
                                        xfT[:, t // 2, c, t % 2 * HALF:(t % 2 + 1) * HALF], sw[:, c],
                                        start=(c == 0), stop=(c == ND - 1))
                ins.then_inc(z_made, 1)

            def prefix(tail):
                pe.wait_ge(chosen_ready, tail + 1)
                pe.matmul(mb[0:HALF, 0:5 * E], earlier[:], chosen[:].rearrange("p t e -> p (t e)"), start=True, stop=False)
                for t in range(4):
                    ins = pe.matmul(mb[0:HALF, (t + 1) * E:5 * E], ones[:],
                                    chosen[:, t].unsqueeze(1).broadcast_to([HALF, 4 - t, E]), start=False, stop=(t == 3))
                ins.then_inc(prefix_made, 1)

            def finish(p, i, hp, what):
                if i == 1:
                    what(p, 0, hp)
                elif later(p):
                    what(p - 1, 1, hp)

            def first_image(p, par):
                b = p * 2
                tail, routing = later(p), later(p) and later(p - 1)
                for t in range(2):
                    values(p, 0, t, (res_added, (p - 2) * 2 + (t + 1)) if routing else
                           (g_gated, 3 + t) if tail else None)
                if not tail:
                    pe.wait_ge(qk_weights_in, QK_IN)
                project(p, 0, 0)
                project(p, 0, 1)
                if not tail:
                    pe.wait_ge(weights_in, ALL_IN)
                    pe.wait_ge(ones_made, 1)
                finish(p, 0, 2, scores)
                gates(p, 0, 0)
                gates(p, 0, 1)
                project(p, 0, 2)
                finish(p, 0, 1, outputs)
                if routing:
                    turn(p - 2, 0, g_gated, b * 2 + 2)
                    turn(p - 2, 1, g_gated, b * 2 + 1)
                project(p, 0, 3)
                finish(p, 0, 2, outputs)
                if routing:
                    logits(p - 2)
                scores(p, 0, 0)
                project(p, 0, 4)
                project(p, 0, 5)
                if routing:
                    group_statistics(p - 1, z_shifted, p - 1)
                elif tail:
                    group_statistics(p - 1, g_gated, b * 2 + 1)
                outputs(p, 0, 0)
                scores(p, 0, 1)
                if routing:
                    prefix(p - 2)

            def second_image(p, par):
                b = p * 2 + 1
                tail, routing = later(p), later(p) and later(p - 1)
                values(p, 1, 0, (stats_read, p) if tail else (g_gated, 1))
                project(p, 1, 0)
                values(p, 1, 1, (prefix_read, p - 1) if routing else (g_gated, p * 4 + 2))
                project(p, 1, 1)
                finish(p, 1, 2, scores)
                gates(p, 1, 0)
                gates(p, 1, 1)
                project(p, 1, 2)
                finish(p, 1, 1, outputs)
                project(p, 1, 3)
                finish(p, 1, 2, outputs)
                if tail:
                    project_out(p - 1, 1 - par, 0, g_gated, b * 2 + 1)
                scores(p, 1, 0)
                project(p, 1, 4)
                if tail:
                    project_out(p - 1, 1 - par, 1, g_gated, b * 2 + 2)
                project(p, 1, 5)
                outputs(p, 1, 0)
                scores(p, 1, 1)

            def pair(p, par):
                first_image(p, par)
                second_image(p, par)

            pair(0, 0)
            pair(1, 1)
            with pe.Fori(1, PAIRS // 2) as r:
                for par in range(2):
                    pair(r * 2 + par, par)
            for i in range(2):
                turn(PAIRS - 2, i, res_added, PAIRS * 2 - 2)
            finish(PAIRS, 0, 2, scores)
            logits(PAIRS - 2)
            finish(PAIRS, 0, 1, outputs)
            finish(PAIRS, 0, 2, outputs)
            group_statistics(PAIRS - 1, z_shifted, PAIRS - 1)
            prefix(PAIRS - 2)
            project_out(PAIRS - 1, 1, 0, stats_read, PAIRS)
            project_out(PAIRS - 1, 1, 1, prefix_read, PAIRS - 1)
            for i in range(2):
                turn(PAIRS - 1, i, res_added, PAIRS * 2)
            logits(PAIRS - 1)
            prefix(PAIRS - 1)

        @block.scalar
        def _(act):
            def copy_outputs(p, par, i, hp):
                act.wait_ge(o_made, (p * 2 + i) * 3 + (hp + 1))
                if i == 0 and hp == 0 and later(p) and later(p - 1):
                    act.wait_ge(wo_made, (p - 1) * 2)
                act.activation(cc[:, par, i, hp], o_bank[:, 0:N], ACT.Copy).then_inc(o_copied, 1)

            def copy_xfT(tail, i):
                act.wait_ge(xf_turned, tail * 2 + (i + 1))
                act.activation(xfT[:, i].rearrange("p c n -> p (c n)"), (mb, ma)[i][0:DC, 0:ND * N],
                               ACT.Copy).then_inc(xfT_copied, 1)

            def exponentiate(tail):
                act.wait_ge(z_shifted, tail + 1)
                act.activation(ez[:], z[:], ACT.Exp).then_inc(z_exped, 1)

            def swap(b, n):
                act.wait_ge(qk_made, b * 6 + (n + 1))
                if later(b) or n >= 3:
                    act.wait_ge(qk_rotated, b * 6 + (n - 2))
                src = qk_bank[n % 3][:, 0:2 * N].rearrange("p (i n) -> p i n", i=2)
                act.activation(swapped[0:64, n % 3], src[64:128], ACT.Copy)
                act.activation(swapped[64:128, n % 3], src[0:64], ACT.Copy).then_inc(qk_swapped, 1)

            def copy_values(b, i, t):
                act.wait_ge(v_made, b * 2 + (t + 1))
                if not isinstance(b, int) or b >= 2:
                    act.wait_ge(o_made, b * 3 - 3)
                act.activation(v[:, i, t], (ma, mb)[t][0:HALF, 0:H * DV], ACT.Copy).then_inc(v_copied, 1)

            def half_tanh(p, par, i, part):
                act.wait_ge(g_made, (p * 2 + i) * 2 + (part + 1))
                if later(p) and later(p - 1):
                    act.wait_ge(gated_ready, p - 1)
                dst, src = ((gate[:, par, i, 0:2], ma[:, 0:2 * N].rearrange("p (i n) -> p i n", i=2)),
                            (gate[:, par, i, 2], mb[:, 0:N]))[part]
                act.activation(dst, src, ACT.Tanh, scale=0.5).then_inc(g_tanh, 1)

            def normalize_outputs(tail, par):
                act.wait_ge(scale_ready, tail + 1)
                for m in range(NP):
                    ins = act.activation(cc[:, par, 1, m], cc[:, par, 1, m], ACT.Identity,
                                         bias=gb[:, 1, m:m + 1], scale=ga[:, 1, m:m + 1])
                ins.then_inc(outputs_normalized, 1)

            def finish(p, par, i, hp):
                if i == 1:
                    copy_outputs(p, par, 0, hp)
                elif later(p):
                    copy_outputs(p - 1, 1 - par, 1, hp)

            def image(p, par, i):
                b = p * 2 + i
                routing = i == 0 and later(p) and later(p - 1)
                copy_values(b, i, 0)
                if i == 0:
                    copy_values(b, i, 1)
                    swap(b, 0)
                else:
                    swap(b, 0)
                    copy_values(b, i, 1)
                swap(b, 1)
                half_tanh(p, par, i, 0)
                half_tanh(p, par, i, 1)
                if i == 1 and later(p):
                    normalize_outputs(p - 1, 1 - par)
                swap(b, 2)
                finish(p, par, i, 1)
                if routing:
                    copy_xfT(p - 2, 0)
                    copy_xfT(p - 2, 1)
                swap(b, 3)
                finish(p, par, i, 2)
                swap(b, 4)
                swap(b, 5)
                if routing:
                    exponentiate(p - 2)
                copy_outputs(p, par, i, 0)

            def pair(p, par):
                image(p, par, 0)
                image(p, par, 1)

            pair(0, 0)
            pair(1, 1)
            with act.Fori(1, PAIRS // 2) as r:
                for par in range(2):
                    pair(r * 2 + par, par)
            for i in range(2):
                copy_xfT(PAIRS - 2, i)
            exponentiate(PAIRS - 2)
            finish(PAIRS, 0, 0, 1)
            finish(PAIRS, 0, 0, 2)
            normalize_outputs(PAIRS - 1, 1)
            for i in range(2):
                copy_xfT(PAIRS - 1, i)
            exponentiate(PAIRS - 1)
            mark_empty(act, range(E // 2, E + 1))

        @block.gpsimd
        def _(pool):
            def rotate(b, n):
                pool.wait_ge(qk_swapped, b * 6 + (n + 1))
                pool.tensor_tensor(swapped[:, n % 3], swapped[:, n % 3], two(sin_t[:, n % 2]), ALU.mult).then_inc(qk_turned, 1)
                pool.wait_ge(qk_turned, b * 6 + (n + 1))
                pool.wait_ge(qk_straight, b * 6 + (n + 1))
                if later(b):
                    pool.wait_ge(s_made, b * 6 - (4 - n // 2 * 2))
                pool.tensor_tensor(rot[:, n], straight[:, n % 3], swapped[:, n % 3], ALU.add).then_inc(qk_rotated, 1)

            def dispatch(tail):
                pool.wait_ge(slots_ready, tail + 1).then_inc(alone, 1)
                for t in range(4):
                    pool.indirect_dma_start(z_dram, bass.IndirectOffsetOnAxis(ap=slot_i[:, t:t + 1], axis=0),
                                            row[:, t], None).then_inc(rows_out, 16)

            def pair(p):
                for n in range(2 * NP):
                    rotate(p * 2, n)
                if later(p) and later(p - 1):
                    dispatch(p - 2)
                for n in range(2 * NP):
                    rotate(p * 2 + 1, n)

            pool.wait_ge(qk_weights_in, QK_IN)
            pair(0)
            pair(1)
            with pool.Fori(2, PAIRS) as p:
                pair(p)
            dispatch(PAIRS - 2)
            dispatch(PAIRS - 1)
            pool.wait_ge(rows_out, 64 * PAIRS)

        @block.vector
        def _(dve):
            chain = Chain(dve, chain_sem)
            dve.memset(chosen[:], 0.0)
            dve.memset(ones[:], 1.0).then_inc(ones_made, 1)
            dve.wait_ge(ones_made, 1)
            dve.wait_ge(qk_weights_in, QK_IN)

            def read_group_statistics(tail):
                dve.wait_ge(stats_summed, tail + 1)
                dve.tensor_copy(gg[:].rearrange("p s i n -> p (s i n)"), ma[:, 0:4 * NP]).then_inc(stats_read, 1)

            def scale_groupnorm(tail):
                wide = [128, 2, NP]
                dve.wait_ge(stats_read, tail + 1)
                chain.link(dve.tensor_tensor(gt[:], gg[:, 0], gg[:, 0], ALU.mult))
                chain.link(dve.tensor_tensor(gv[:], gg[:, 1], gt[:], ALU.subtract))
                chain.link(dve.tensor_scalar(gv[:], gv[:], 0.0, EPS, ALU.max, ALU.add))
                rsqrt(dve, chain, gv[:], gy[:], gt[:])
                chain.link(dve.tensor_tensor(ga[:], gy[:], gnw[:].unsqueeze(1).broadcast_to(wide), ALU.mult))
                chain.link(dve.tensor_tensor(gb[:], gg[:, 0], ga[:], ALU.mult))
                dve.tensor_tensor(gb[:], gnb[:].unsqueeze(1).broadcast_to(wide), gb[:], ALU.subtract).then_inc(scale_ready, 1)

            def gate_outputs(tail, par):
                dve.wait_ge(scale_ready, tail + 1)
                for m in range(NP):
                    last = dve.tensor_scalar(cc[:, par, 0, m], cc[:, par, 0, m], ga[:, 0, m:m + 1],
                                             gb[:, 0, m:m + 1], ALU.mult, ALU.add)
                chain.link(last)
                dve.wait_ge(outputs_normalized, tail + 1)
                dve.scalar_tensor_tensor(out=cc[:, par], in0=cc[:, par], scalar=0.5, in1=gate[:, par], op0=ALU.mult,
                                         op1=ALU.mult).then_inc(gated_ready, 1)

            def gates(p, par, i):
                for part in range(2):
                    dve.wait_ge(g_tanh, (p * 2 + i) * 2 + (part + 1))
                    dst, src = ((gate[:, par, i, 0:2], ma[:, 0:2 * N].rearrange("p (i n) -> p i n", i=2)),
                                (gate[:, par, i, 2], mb[:, 0:N]))[part]
                    dve.scalar_tensor_tensor(out=dst, in0=dst, scalar=1.0, in1=src, op0=ALU.add,
                                             op1=ALU.mult).then_inc(g_gated, 1)

            def straighten(p, i, n):
                b = p * 2 + i
                dve.wait_ge(qk_swapped, b * 6 + (n + 1))
                if later(b) or n >= 3:
                    dve.wait_ge(qk_rotated, b * 6 + (n - 2))
                dve.tensor_tensor(straight[:, n % 3], qk_bank[n % 3][:, 0:2 * N].rearrange("p (i n) -> p i n", i=2),
                                  two(cos_t[:, n % 2]), ALU.mult).then_inc(qk_straight, 1)

            def decay(p, i, hp):
                b = p * 2 + i
                for j in range(2):
                    h = 2 * hp + j
                    dve.wait_ge(s_made, b * 6 + (h + 1))
                    if later(b):
                        dve.wait_ge(o_made, b * 3 - (2 - hp))
                    dve.tensor_tensor(sm[:, h], s_bank[j][0:HALF, 0:N + HALF], mask[:, h], ALU.mult).then_inc(s_decayed, 1)

            def output_statistics(p, par, i):
                dve.wait_ge(o_copied, (p * 2 + i) * 3 + 3)
                for hp in range(NP):
                    ins = dve.bn_stats(gst[:, i, hp], cc[:, par, i, hp])
                chain.link(ins, alone)
                for hp in range(NP):
                    ins = dve.bn_aggr(gmv[:, i, hp], gst[:, i, hp])
                chain.link(ins)

            def prepare_statistics():
                chain.link(dve.tensor_copy(gs[:, 0], gmv[:, :, :, 0]))
                chain.link(dve.tensor_tensor(gs[:, 1], gs[:, 0], gs[:, 0], ALU.mult))
                dve.tensor_tensor(gs[:, 1], gs[:, 1], gmv[:, :, :, 1], ALU.add).then_inc(stats_ready, 1)

            def add_residual(tail, i):
                if i == 0:
                    dve.wait_ge(res_in, tail * 32 + 32)
                    if later(tail):
                        dve.wait_ge(rows_out, tail * 64)
                dve.wait_ge(wo_made, tail * 2 + (i + 1))
                at = slice(i * 2, i * 2 + 2)
                dve.tensor_tensor(row[:, at, 0:D], (ma, mb)[i][0:HALF, 0:2 * D].rearrange("p (t f) -> p t f", t=2),
                                  hres[:, at], ALU.add).then_inc(res_added, 1)

            def row_statistics(tail):
                dve.wait_ge(res_added, tail * 2 + 2)
                for t in range(4):
                    ins = dve.bn_stats(lst[:, t], row[:, t, 0:D])
                chain.link(ins, alone)
                for t in range(4):
                    ins = dve.bn_aggr(lmv[:, t], lst[:, t])
                chain.link(ins)

            def second_layernorm(tail):
                dve.tensor_copy(row[:, :, D], lmv[:, :, 0])
                chain.link(dve.tensor_scalar(lv[:], lmv[:, :, 1], EPS, None, ALU.add))
                rsqrt(dve, chain, lv[:], ly[:], lt[:])
                dve.tensor_copy(row[:, :, D + 1], ly[:])
                for t in range(4):
                    ins = dve.tensor_scalar(xf[:, t], row[:, t, 0:D], lmv[:, t, 0:1], ly[:, t:t + 1],
                                            ALU.subtract, ALU.mult)
                    if t % 2:
                        ins.then_inc(xf_ready, 1)

            def shift_logits(tail):
                wide = [HALF, 4, E]
                dve.wait_ge(z_made, tail + 1)
                chain.link(dve.tensor_tensor(z[:], ma[0:HALF, 0:4 * E].rearrange("p (t e) -> p t e", t=4), swb[:], ALU.add))
                chain.link(dve.tensor_reduce(zmax[:], z[:], AX.X, ALU.max))
                dve.tensor_tensor(z[:], z[:], zmax[:].unsqueeze(2).broadcast_to(wide), ALU.subtract).then_inc(z_shifted, 1)

            def route_tokens(tail):
                wide = [HALF, 4, E]
                dve.wait_ge(z_shifted, tail + 1)
                chain.link(dve.tensor_scalar(rank[:], z[:], 0.0, float(E), ALU.is_lt, ALU.mult))
                chain.link(dve.tensor_tensor(rank[:], rank[:], expert[:], ALU.add))
                chain.link(dve.tensor_reduce(route[:], rank[:], AX.X, ALU.min))
                dve.tensor_tensor(chosen[:, 0:4], expert[:], route[:].unsqueeze(2).broadcast_to(wide),
                                  ALU.is_equal).then_inc(chosen_ready, 1)
                dve.wait_ge(z_exped, tail + 1)
                chain.link(dve.tensor_reduce(esum[:], ez[:], AX.X, ALU.add))
                chain.link(dve.reciprocal(row[:, :, D + 2], esum[:]))
                dve.wait_ge(chosen_ready, tail + 1)
                dve.tensor_tensor(prob.rearrange("p e t -> p t e")[:, bass.ds(tail * 4, 4), :], chosen[:, 0:4],
                                  row[:, :, D + 2:D + 3].broadcast_to(wide), ALU.mult)
                chain.link(dve.tensor_copy(row[:, :, D + 3], tid[:, bass.ds(tail * 4, 4)]))

            def place_tokens(tail):
                dve.wait_ge(prefix_made, tail + 1)
                free = count[:].unsqueeze(1).broadcast_to([HALF, 4, E])
                chain.link(dve.tensor_tensor(rank[:], mb[0:HALF, 0:4 * E].rearrange("p (t e) -> p t e", t=4), free, ALU.add))
                dve.tensor_tensor(count[:], count[:], mb[0:HALF, 4 * E:5 * E], ALU.add).then_inc(prefix_read, 1)
                dve.wait_ge(prefix_read, tail + 1)
                chain.link(dve.tensor_tensor(rank[:], rank[:], chosen[:, 0:4], ALU.mult))
                chain.link(dve.tensor_reduce(slot[:], rank[:], AX.X, ALU.add))
                dve.tensor_copy(slot_i[:], slot[:]).then_inc(slots_ready, 1)

            def first_image(p, par):
                tail, routing = later(p), later(p) and later(p - 1)
                straighten(p, 0, 0)
                straighten(p, 0, 1)
                if tail:
                    decay(p - 1, 1, 2)
                else:
                    dve.wait_ge(weights_in, ALL_IN)
                gates(p, par, 0)
                straighten(p, 0, 2)
                straighten(p, 0, 3)
                if tail:
                    output_statistics(p - 1, 1 - par, 1)
                    prepare_statistics()
                decay(p, 0, 0)
                if routing:
                    shift_logits(p - 2)
                straighten(p, 0, 4)
                if routing:
                    route_tokens(p - 2)
                if tail:
                    read_group_statistics(p - 1)
                straighten(p, 0, 5)
                decay(p, 0, 1)
                if routing:
                    place_tokens(p - 2)
                if tail:
                    scale_groupnorm(p - 1)

            def second_image(p, par):
                tail = later(p)
                straighten(p, 1, 0)
                straighten(p, 1, 1)
                decay(p, 0, 2)
                gates(p, par, 1)
                if tail:
                    gate_outputs(p - 1, 1 - par)
                straighten(p, 1, 2)
                straighten(p, 1, 3)
                output_statistics(p, par, 0)
                if tail:
                    add_residual(p - 1, 0)
                decay(p, 1, 0)
                straighten(p, 1, 4)
                if tail:
                    add_residual(p - 1, 1)
                straighten(p, 1, 5)
                decay(p, 1, 1)
                if tail:
                    row_statistics(p - 1)
                    second_layernorm(p - 1)

            def pair(p, par):
                first_image(p, par)
                second_image(p, par)

            pair(0, 0)
            pair(1, 1)
            with dve.Fori(1, PAIRS // 2) as r:
                chain.enter(r - 1, PER_ROUND)
                for par in range(2):
                    pair(r * 2 + par, par)
            chain.leave(PAIRS // 2 - 1)
            decay(PAIRS - 1, 1, 2)
            shift_logits(PAIRS - 2)
            route_tokens(PAIRS - 2)
            output_statistics(PAIRS - 1, 1, 1)
            prepare_statistics()
            read_group_statistics(PAIRS - 1)
            scale_groupnorm(PAIRS - 1)
            place_tokens(PAIRS - 2)
            gate_outputs(PAIRS - 1, 1)
            for i in range(2):
                add_residual(PAIRS - 1, i)
            row_statistics(PAIRS - 1)
            second_layernorm(PAIRS - 1)
            shift_logits(PAIRS - 1)
            route_tokens(PAIRS - 1)
            place_tokens(PAIRS - 1)
            dve.memset(plan.ends[:, E:E + 1], E * REGION)
            dve.tensor_copy(plan.ends[:, 0:E], count[0:1]).then_inc(ends_ready, 1)
            dve.wait_ge(plan_in, 16 * len(plan.loads))
            scratch = [straight[0:1, i].rearrange("p j n -> p (j n)") for i in range(2)]
            scratch.append(swapped[0:1].rearrange("p i j n -> p (i j n)"))
            plan_groups(dve, chain, plan,
                        scratch[0][:, 0:E * plan.NK].rearrange("p (e k) -> p e k", e=E),
                        scratch[1][:, 0:E * E].rearrange("p (e k) -> p e k", e=E),
                        scratch[2][:, 0:NG * E].rearrange("p (g e) -> p g e", e=E), count, groups)


PER_ROUND = 96


def experts(nc, a, z_dram, limits_dram, prob, groups, out):
    with ExitStack() as ctx:
        def sb(name, shape, dt=F32):
            return ctx.enter_context(nc.sbuf_tensor("ffn_" + name, shape, dt))

        def sem(name):
            return ctx.enter_context(nc.semaphore(name))

        T = G // 128
        S = SLOTS
        w1 = sb("w1", [DC, S, ND, F])
        w2 = sb("w2", [128, S, FM, D])
        b1 = sb("b1", [128, S, FM])
        b2 = sb("b2", [128, S, D])
        lim = sb("lim", [128, S, 2])
        rows = sb("rows", [128, S, T, ROW])
        xf = sb("xf", [128, S, T, D])
        xfT = sb("xfT", [DC, S, ND, G])
        hid = sb("hid", [128, S, FM, G])
        base = sb("base", [128, S, T, D])
        made = sb("made", [128, S, T, D])
        y = sb("y", [128, S, T, D])
        token = sb("token", [128, S, T], U32)
        above = sb("above", [128, S, T])
        same = sb("same", [128, S, T])
        mine = sb("mine", [128, S, T])
        rest = sb("rest", [128, S, T])
        ident = sb("ident", [128, 128])
        fix_rows = sb("fix_rows", [128, FIXES, T, ROW])
        fix_lim = sb("fix_lim", [128, FIXES, 2])
        fix_kept = sb("fix_kept", [128, FIXES, T])
        fix_same = sb("fix_same", [128, FIXES, T])
        fix_xf = sb("fix_xf", [128, FIXES, T, D])
        fix_y = sb("fix_y", [128, FIXES, T, D])
        fix_token = sb("fix_token", [128, FIXES, T], U32)
        steps = sb("steps", [HALF, PSTEPS + ISTEPS])
        tid = sb("tid", [HALF, NT])
        ones = sb("ones", [HALF, HALF], BF16)
        hit = sb("hit", [HALF, E, NT], BF16)
        twos = sb("twos", [HALF, E, NT // 2], BF16)
        fours = sb("fours", [HALF, E, NT // 4], BF16)
        unlike = sb("unlike", [HALF, E, NT])
        late = sb("late", [HALF, E, NT])
        hits = sb("hits", [HALF, E])
        limit = sb("limit", [HALF, E, 2])
        trial = sb("trial", [HALF, E])
        good = sb("good", [HALF, E])
        short = sb("short", [HALF, E])
        SPAN = 16

        total = ctx.enter_context(nc.psum_tensor("total", [128, 512], F32))
        h_bank = [ctx.enter_context(nc.psum_tensor(f"ffn_h{i}", [128, 512], F32)) for i in range(3)]
        o_bank = [ctx.enter_context(nc.psum_tensor(f"ffn_o{i}", [128, 512], F32)) for i in range(2)]
        x_bank = [ctx.enter_context(nc.psum_tensor(f"ffn_x{i}", [128, 512], F32)) for i in range(2)]

        ident_in = sem("ident_in")
        rows_in = [sem(f"ffn_rows_in{s}") for s in range(S)]
        weights_in = [sem(f"ffn_weights_in{s}") for s in range(S)]
        xf_made, xf_turned, xfT_copied = sem("ffn_xf_made"), sem("ffn_xf_turned"), sem("ffn_xfT_copied")
        h_made, h_active, o_made = sem("ffn_h_made"), sem("ffn_h_active"), sem("ffn_o_made")
        o_read, y_made = sem("ffn_o_read"), sem("ffn_y_made")
        y_out = [sem(f"ffn_y_out{s}") for s in range(S)]
        chain_sem, alone = sem("ffn_chain"), sem("ffn_alone")
        block = ctx.enter_context(nc.Block())
        lim_in = [sem(f"lim_in{s}") for s in range(S)]
        fix_in = [sem(f"fix_in{j}") for j in range(FIXES)]
        fix_out = [sem(f"fix_out{j}") for j in range(FIXES)]
        fix_made, tables_in, ones_made = sem("fix_made"), sem("search_tables_in"), sem("search_ones")
        counted, summed, limits_ready, limits_out = sem("counted"), sem("summed"), sem("limits_ready"), sem("limits_out")
        WEIGHTS_IN = 4 * 16
        LAST = ROUNDS_OF_GROUPS - 1

        def group_of(i, s):
            return i * S + s

        @block.sync
        def _(sp):
            def load(g, s):
                e = sp.value_load(groups[0:1, bass.ds(g, 1), 0], min_val=0, max_val=E - 1)
                r = sp.value_load(groups[0:1, bass.ds(g, 1), 1], min_val=0, max_val=ZROWS - G)
                sp.dma_start(rows[:, s], z_dram[bass.ds(r, G)].rearrange("(t p) f -> p t f", p=128)).then_inc(rows_in[s], 16)
                sp.dma_start(w1[:, s], a["w1"][bass.ds(e, 1)].rearrange("o p c f -> (o p) c f")).then_inc(weights_in[s], 16)
                sp.dma_start(w2[:, s], a["w2"][bass.ds(e, 1)].rearrange("o p m f -> (o p) m f")).then_inc(weights_in[s], 16)
                sp.dma_start(b1[:, s], a["b1"][bass.ds(e, 1)].rearrange("o p m -> (o p) m")).then_inc(weights_in[s], 16)
                sp.dma_start(b2[:, s], a["b2"][bass.ds(e, 1)].rearrange("o p f -> (o p) f")).then_inc(weights_in[s], 16)

            def load_limit(g, s):
                e = sp.value_load(groups[0:1, bass.ds(g, 1), 0], min_val=0, max_val=E - 1)
                sp.dma_start(lim[:, s], limits_dram[bass.ds(e, 1)].broadcast_to([128, 2])).then_inc(lim_in[s], 16)

            def load_fix(f, j):
                e = sp.value_load(groups[0:1, bass.ds(f, 1), 0], min_val=0, max_val=E - 1)
                r = sp.value_load(groups[0:1, bass.ds(f, 1), 1], min_val=0, max_val=ZROWS - G)
                sp.dma_start(fix_rows[:, j], z_dram[bass.ds(r, G)].rearrange("(t p) f -> p t f", p=128)).then_inc(fix_in[j], 16)
                sp.dma_start(fix_lim[:, j], limits_dram[bass.ds(e, 1)].broadcast_to([128, 2])).then_inc(fix_in[j], 16)

            def free_slot(i, s):
                sp.wait_ge(y_made, i * S + (s + 1 - S))

            load(0, 0)
            sp.dma_start(ident[:], a["c_ident"]).then_inc(ident_in, 16)
            sp.dma_start(steps[:], a["c_steps"]).then_inc(tables_in, 16)
            sp.dma_start(tid[:], a["c_tid"]).then_inc(tables_in, 16)
            for s in range(1, S):
                load(s, s)
            with sp.Fori(1, EARLY) as i:
                for s in range(S):
                    free_slot(i, s)
                    load(i * S + s, s)
            for s in range(S - 1):
                free_slot(EARLY, s)
                load(EARLY * S + s, s)
            sp.wait_ge(limits_ready, EARLY - PROUNDS)
            sp.dma_start(limits_dram.rearrange("e x -> (e x)").unsqueeze(0),
                         limit[0:1].rearrange("p e x -> p (e x)")).then_inc(limits_out, 16)
            sp.wait_ge(limits_out, 16)
            for s in range(S):
                load_limit(EARLY * S + s, s)
            free_slot(EARLY, S - 1)
            load(EARLY * S + S - 1, S - 1)
            for j in range(FIXES):
                load_fix(j, j)
            with sp.Fori(EARLY + 1, ROUNDS_OF_GROUPS) as i:
                for s in range(S):
                    free_slot(i, s)
                    load(i * S + s, s)
                    load_limit(i * S + s, s)
                    if s < FIXES:
                        sp.wait_ge(fix_made, i * FIXES + (s + 1 - (EARLY + 1) * FIXES))
                        load_fix(i * FIXES + (s - EARLY * FIXES), s)

        @block.vector
        def _(dve):
            chain = Chain(dve, chain_sem)

            wide = [HALF, E, NT]

            def normalize(i, s):
                dve.wait_ge(rows_in[s], i * 16 + 16)
                for t in range(T):
                    ins = dve.tensor_scalar(xf[:, s, t], rows[:, s, t, 0:D], rows[:, s, t, D:D + 1],
                                            rows[:, s, t, D + 1:D + 2], ALU.subtract, ALU.mult)
                ins.then_inc(xf_made, 1)

            def number_tokens(i, s):
                if later(i):
                    dve.wait_ge(y_out[s], i * (T * 16))
                return dve.tensor_copy(token[:, s], rows[:, s, :, D + 3])

            def weigh(i, s):
                p, number = rows[:, s, :, D + 2], rows[:, s, :, D + 3]
                dve.wait_ge(lim_in[s], i * 16 - (EARLY - 1) * 16)
                dve.tensor_scalar(above[:, s], p, lim[:, s, 0:1], None, ALU.is_gt)
                chain.link(dve.tensor_scalar(same[:, s], p, lim[:, s, 0:1], None, ALU.is_equal))
                chain.link(dve.scalar_tensor_tensor(out=same[:, s], in0=number, scalar=lim[:, s, 1:2], in1=same[:, s],
                                                    op0=ALU.is_le, op1=ALU.mult))
                chain.link(dve.tensor_tensor(above[:, s], above[:, s], same[:, s], ALU.add))
                chain.link(dve.tensor_tensor(mine[:, s], p, above[:, s], ALU.mult))
                chain.link(dve.tensor_tensor(rest[:, s], p, mine[:, s], ALU.subtract))
                for t in range(T):
                    ins = dve.scalar_tensor_tensor(out=base[:, s, t], in0=xf[:, s, t], scalar=rest[:, s, t:t + 1],
                                                   in1=rows[:, s, t, 0:D], op0=ALU.mult, op1=ALU.add)
                chain.link(ins)

            def combine(i, s, weight, rest):
                dve.wait_ge(o_made, group_of(i, s) + 1)
                src = o_bank[s % 2][:, 0:T * D].rearrange("p (t f) -> p t f", t=T)
                dve.tensor_tensor(made[:, s], src, b2[:, s].unsqueeze(1).broadcast_to([128, T, D]),
                                  ALU.add).then_inc(o_read, 1)
                dve.wait_ge(o_read, group_of(i, s) + 1)
                for t in range(T):
                    ins = dve.scalar_tensor_tensor(out=y[:, s, t], in0=made[:, s, t], scalar=weight(t),
                                                   in1=rest(t), op0=ALU.mult, op1=ALU.add)
                ins.then_inc(y_made, 1)

            def normalize_next(i, s):
                if s + 1 < S:
                    normalize(i, s + 1)
                elif not (isinstance(i, int) and i == LAST):
                    normalize(i + 1, 0)

            def fold_hits(compared):
                chain.link(compared)
                chain.link(dve.tensor_tensor(twos[:], hit[:, :, 0:NT // 2], hit[:, :, NT // 2:], ALU.add))
                dve.tensor_tensor(fours[:], twos[:, :, 0:NT // 4], twos[:, :, NT // 4:], ALU.add).then_inc(counted, 1)

            def try_limit(k, phase):
                step = steps[:, bass.ds(k, 1)]
                chain.link(dve.tensor_scalar(trial[:], limit[:, :, phase], step, None, ALU.add))
                table, op = ((prob, ALU.is_ge), (late[:], ALU.is_lt))[phase]
                fold_hits(dve.tensor_tensor(hit[:], table, trial[:].unsqueeze(2).broadcast_to(wide), op))

            def sum_hits(n):
                dve.wait_ge(summed, n + 1)
                chain.link(dve.tensor_reduce(hits[:], total[0:HALF, 0:E * SPAN].rearrange("p (e k) -> p e k", e=E),
                                             AX.X, ALU.add))

            def judge(k, phase):
                sum_hits(k + phase)
                if phase == 0:
                    chain.link(dve.tensor_scalar(good[:], hits[:], float(CAP), None, ALU.is_ge))
                else:
                    chain.link(dve.tensor_tensor(good[:], hits[:], short[:], ALU.is_lt))
                chain.link(dve.scalar_tensor_tensor(out=limit[:, :, phase], in0=good[:], scalar=steps[:, bass.ds(k, 1)],
                                                    in1=limit[:, :, phase], op0=ALU.mult, op1=ALU.add))

            def early_group(i, s, phase):
                number_tokens(i, s)
                normalize_next(i, s)
                k = i * TRIES + 2 * s
                if s:
                    judge(k - 1, phase)
                try_limit(k, phase)
                judge(k, phase)
                if s + 1 < S:
                    try_limit(k + 1, phase)
                elif phase == 1:
                    dve.nop().then_inc(limits_ready, 1)
                combine(i, s, lambda t: rows[:, s, t, D + 2:D + 3], lambda t: rows[:, s, t, 0:D])

            def settle_ties():
                fold_hits(dve.tensor_tensor(hit[:], prob, limit[:, :, 0:1].broadcast_to(wide), ALU.is_gt))
                sum_hits(PSTEPS)
                chain.link(dve.tensor_scalar(short[:], hits[:], -1.0, float(CAP), ALU.mult, ALU.add))
                chain.link(dve.tensor_tensor(unlike[:], prob, limit[:, :, 0:1].broadcast_to(wide), ALU.not_equal))
                chain.link(dve.scalar_tensor_tensor(out=late[:], in0=unlike[:], scalar=2 * EMPTY,
                                                    in1=tid[:].unsqueeze(1).broadcast_to(wide), op0=ALU.mult, op1=ALU.add))

            def fix(i, j):
                dve.wait_ge(fix_in[j], i * 32 - (EARLY - 1) * 32)
                p, number = fix_rows[:, j, :, D + 2], fix_rows[:, j, :, D + 3]
                if not isinstance(i, int) or i > EARLY:
                    dve.wait_ge(fix_out[j], i * (T * 16) - EARLY * T * 16)
                for t in range(T):
                    dve.tensor_scalar(fix_xf[:, j, t], fix_rows[:, j, t, 0:D], fix_rows[:, j, t, D:D + 1],
                                      fix_rows[:, j, t, D + 1:D + 2], ALU.subtract, ALU.mult)
                dve.tensor_scalar(fix_kept[:, j], p, fix_lim[:, j, 0:1], None, ALU.is_gt)
                chain.link(dve.tensor_scalar(fix_same[:, j], p, fix_lim[:, j, 0:1], None, ALU.is_equal))
                chain.link(dve.scalar_tensor_tensor(out=fix_same[:, j], in0=number, scalar=fix_lim[:, j, 1:2],
                                                    in1=fix_same[:, j], op0=ALU.is_le, op1=ALU.mult))
                for t in range(T):
                    dve.scalar_tensor_tensor(out=fix_y[:, j, t], in0=fix_xf[:, j, t], scalar=fix_rows[:, j, t, D + 2:D + 3],
                                             in1=fix_rows[:, j, t, 0:D], op0=ALU.mult, op1=ALU.add)
                chain.link(dve.tensor_tensor(fix_kept[:, j], fix_kept[:, j], fix_same[:, j], ALU.add))
                chain.link(dve.scalar_tensor_tensor(out=fix_kept[:, j], in0=fix_kept[:, j], scalar=EMPTY, in1=number,
                                                    op0=ALU.mult, op1=ALU.add))
                dve.tensor_copy(fix_token[:, j], fix_kept[:, j]).then_inc(fix_made, 1)

            def late_group(i, s):
                number_tokens(i, s)
                normalize_next(i, s)
                weigh(i, s)
                if s < FIXES:
                    fix(i, s)
                combine(i, s, lambda t: mine[:, s, t:t + 1], lambda t: base[:, s, t])

            dve.memset(ones[:], 1.0).then_inc(ones_made, 1)
            chain.link(dve.memset(limit[:], 0.0))
            dve.wait_ge(tables_in, 32)
            normalize(0, 0)
            for s in range(S):
                early_group(0, s, 0)
            with dve.Fori(1, PROUNDS) as i:
                chain.enter(i - 1, 6 * TRIES)
                for s in range(S):
                    early_group(i, s, 0)
            chain.leave(PROUNDS - 1)
            settle_ties()
            with dve.Fori(PROUNDS, EARLY) as i:
                chain.enter(i - PROUNDS, 6 * TRIES)
                for s in range(S):
                    early_group(i, s, 1)
            chain.leave(EARLY - PROUNDS)
            for s in range(S):
                late_group(EARLY, s)
            with dve.Fori(EARLY + 1, LAST) as i:
                chain.enter(i - EARLY - 1, 6 * S + 4 * FIXES)
                for s in range(S):
                    late_group(i, s)
            chain.leave(LAST - EARLY - 1)
            for s in range(S):
                late_group(LAST, s)

        @block.tensor
        def _(pe):
            pe.wait_ge(ident_in, 16)

            def turn(i, s):
                pe.wait_ge(xf_made, group_of(i, s) + 1)
                if later(i) or s >= 2:
                    pe.wait_ge(xfT_copied, group_of(i, s) - 1)
                for c in range(ND):
                    for t in range(T):
                        ins = pe.transpose(x_bank[s % 2][0:DC, c * G + t * 128:c * G + (t + 1) * 128],
                                           xf[:, s, t, c * DC:(c + 1) * DC], ident[:])
                ins.then_inc(xf_turned, 1)

            def up(i, s):
                pe.wait_ge(weights_in[s], i * WEIGHTS_IN + WEIGHTS_IN)
                pe.wait_ge(xfT_copied, group_of(i, s) + 1)
                for m in range(FM):
                    if (later(i) or s) and m % 2 == 0:
                        pe.wait_ge(h_active, i * (S * FM) + (s - 1) * FM + (m + 2))
                    for c in range(ND):
                        ins = pe.matmul(h_bank[m // 2][:, m % 2 * G:(m % 2 + 1) * G], w1[:, s, c, m * 128:(m + 1) * 128],
                                        xfT[:, s, c], start=(c == 0), stop=(c == ND - 1))
                    if m % 2:
                        ins.then_inc(h_made, 1)

            def down(i, s):
                if later(i) or s >= 2:
                    pe.wait_ge(o_read, group_of(i, s) - 1)
                for t in range(T):
                    for m in range(FM):
                        if t == 0:
                            pe.wait_ge(h_active, i * (S * FM) + (s * FM + m + 1))
                        ins = pe.matmul(o_bank[s % 2][:, t * D:(t + 1) * D], hid[:, s, m, t * 128:(t + 1) * 128],
                                        w2[:, s, m], start=(m == 0), stop=(m == FM - 1))
                ins.then_inc(o_made, 1)

            def count_hits(n):
                pe.wait_ge(counted, n + 1)
                spans = NT // 4 // SPAN
                for k in range(spans):
                    ins = pe.matmul(total[0:HALF, 0:E * SPAN], ones[:], fours[:, :, k * SPAN:(k + 1) * SPAN],
                                    start=(k == 0), stop=(k == spans - 1))
                ins.then_inc(summed, 1)

            def turn_next(i, s):
                if s + 1 < S:
                    turn(i, s + 1)
                elif not (isinstance(i, int) and i == LAST):
                    turn(i + 1, 0)

            def early_group(i, s, phase):
                up(i, s)
                turn_next(i, s)
                count_hits(i * TRIES + (2 * s + phase))
                down(i, s)
                if s + 1 < S:
                    count_hits(i * TRIES + (2 * s + 1 + phase))

            def late_group(i, s):
                up(i, s)
                turn_next(i, s)
                down(i, s)

            turn(0, 0)
            pe.wait_ge(ones_made, 1)
            for s in range(S):
                early_group(0, s, 0)
            with pe.Fori(1, PROUNDS) as i:
                for s in range(S):
                    early_group(i, s, 0)
            count_hits(PSTEPS)
            with pe.Fori(PROUNDS, EARLY) as i:
                for s in range(S):
                    early_group(i, s, 1)
            with pe.Fori(EARLY, LAST) as i:
                for s in range(S):
                    late_group(i, s)
            for s in range(S):
                late_group(LAST, s)

        @block.scalar
        def _(act):
            def copy_x(i, s):
                act.wait_ge(xf_turned, group_of(i, s) + 1)
                act.activation(xfT[:, s].rearrange("p c g -> p (c g)"), x_bank[s % 2][0:DC, 0:ND * G],
                               ACT.Copy).then_inc(xfT_copied, 1)

            def gelu(i, s):
                for m in range(FM):
                    if m % 2 == 0:
                        act.wait_ge(h_made, i * (S * FM // 2) + s * (FM // 2) + (m // 2 + 1))
                    act.activation(hid[:, s, m], h_bank[m // 2][:, m % 2 * G:(m % 2 + 1) * G], ACT.Gelu,
                                   bias=b1[:, s, m:m + 1]).then_inc(h_active, 1)

            def group(i, s):
                gelu(i, s)
                if s + 1 < S:
                    copy_x(i, s + 1)
                elif not isinstance(i, int) or i + 1 < NG // S:
                    copy_x(i + 1, 0)

            copy_x(0, 0)
            for s in range(S):
                group(0, s)
            with act.Fori(1, NG // S - 1) as i:
                for s in range(S):
                    group(i, s)
            for s in range(S):
                group(NG // S - 1, s)

        @block.gpsimd
        def _(pool):
            def scatter(i, s):
                pool.wait_ge(y_made, group_of(i, s) + 1).then_inc(alone, 1)
                for t in range(T):
                    pool.indirect_dma_start(out, bass.IndirectOffsetOnAxis(ap=token[:, s, t:t + 1], axis=0),
                                            y[:, s, t], None, bounds_check=TOKENS - 1,
                                            oob_is_err=False).then_inc(y_out[s], 16)

            def scatter_fix(i, j):
                pool.wait_ge(fix_made, i * FIXES + (j + 1 - EARLY * FIXES)).then_inc(alone, 1)
                for t in range(T):
                    pool.indirect_dma_start(out, bass.IndirectOffsetOnAxis(ap=fix_token[:, j, t:t + 1], axis=0),
                                            fix_y[:, j, t], None, bounds_check=TOKENS - 1,
                                            oob_is_err=False).then_inc(fix_out[j], 16)

            with pool.Fori(0, EARLY) as i:
                for s in range(S):
                    scatter(i, s)
            for s in range(S):
                pool.wait_ge(y_out[s], 16 * T * EARLY)
            with pool.Fori(EARLY, ROUNDS_OF_GROUPS) as i:
                for s in range(S):
                    if s < FIXES:
                        scatter_fix(i, s)
                    scatter(i, s)
            for s in range(S):
                pool.wait_ge(y_out[s], 16 * T * ROUNDS_OF_GROUPS)
            for j in range(FIXES):
                pool.wait_ge(fix_out[j], 16 * T * (ROUNDS_OF_GROUPS - EARLY))


def laid_out(inputs):
    x = np.asarray(inputs["x"])
    c = np.ascontiguousarray
    x = x.reshape(B, C, 14, 16, 14, 16).transpose(2, 4, 3, 5, 1, 0).reshape(2, HALF, KC, 128, C, B)
    w = np.asarray(inputs["L0_tok_decode_weights"]).reshape(2, HALF, D, KC, 128)
    mw = np.asarray(inputs["L0_tok_merge_weights"]).reshape(2, HALF, C).transpose(1, 0, 2)
    out = {
        "patches": np.concatenate([x.transpose(1, 3, 0, 4, 2, 5).reshape(HALF, 128, -1),
                                   w.transpose(1, 4, 0, 3, 2).reshape(HALF, 128, -1)], axis=2),
        "mw_b": np.broadcast_to(mw.reshape(1, -1), (128, HALF * 2 * C)).copy(),
        "mw_rows": c(mw),
        "dec_bias": c(np.asarray(inputs["L0_tok_decode_biases"]).reshape(2, HALF, D).transpose(1, 0, 2)),
        "merge_bias": c(np.asarray(inputs["L0_tok_merge_biases"]).reshape(2, HALF).T),
    }
    for n in ("Wq", "Wk", "Wv", "Wg"):
        out[n] = c(np.asarray(inputs["L0_attn_" + n]).reshape(ND, DC, -1).transpose(1, 0, 2))
    out["Wo"] = c(np.asarray(inputs["L0_attn_Wo"]).reshape(NP, 128, D).transpose(1, 0, 2))
    out["gn_w"] = c(np.asarray(inputs["L0_attn_gn_weight"]).reshape(NP, 128).T)
    out["gn_b"] = c(np.asarray(inputs["L0_attn_gn_bias"]).reshape(NP, 128).T)
    out["sw"] = c(np.asarray(inputs["L0_ffn_switch_w"]).reshape(ND, DC, E).transpose(1, 0, 2))
    out["sb"] = np.broadcast_to(np.tile(np.asarray(inputs["L0_ffn_switch_b"]), 4), (HALF, 4 * E)).copy()
    out["w1"] = c(np.asarray(inputs["L0_ffn_w1"]).reshape(E, ND, DC, F).transpose(0, 2, 1, 3))
    out["w2"] = c(np.asarray(inputs["L0_ffn_w2"]).reshape(E, FM, 128, D).transpose(0, 2, 1, 3))
    out["b1"] = c(np.asarray(inputs["L0_ffn_b1"]).reshape(E, FM, 128).transpose(0, 2, 1))
    out["b2"] = np.broadcast_to(np.asarray(inputs["L0_ffn_b2"])[:, None, :], (E, 128, D)).copy()
    out.update(constants())
    return out


def build(nc, a, out):
    h_dram = nc.dram_tensor("h_rows", (HALF, 2, B, D), F32, kind="Internal").ap()
    bias_dram = nc.dram_tensor("bias_rows", (HALF, 2, D), F32, kind="Internal").ap()
    z_dram = nc.dram_tensor("dispatched", (ZROWS, ROW), F32, kind="Internal").ap()
    limits_dram = nc.dram_tensor("limits", (E, 2), F32, kind="Internal").ap()
    with ExitStack() as ctx:
        prob = ctx.enter_context(nc.sbuf_tensor("prob", [HALF, E, NT], F32))
        count = ctx.enter_context(nc.sbuf_tensor("count", [HALF, E], F32))
        groups = ctx.enter_context(nc.sbuf_tensor("groups", [1, NG, 2], I32))
        with nc.sbuf_tensor("xT", [DC, B, ND, N], F32) as xT:
            tokenize(nc, a, h_dram, bias_dram, xT[:])
            attend(nc, a, h_dram, z_dram, xT[:], prob[:], count, groups)
        experts(nc, a, z_dram, limits_dram, prob[:], groups, out.rearrange("b n f -> (b n) f"))


def kernel(**inputs):
    import concourse.bacc as bacc
    from concourse.bass_utils import run_bass_kernel_spmd

    nc = bacc.Bacc("TRN2", target_bir_lowering=False, num_devices=1)
    arrays, a = {}, {}
    for name, value in laid_out(inputs).items():
        arrays["in_" + name] = value
        a[name] = nc.dram_tensor("in_" + name, value.shape, F32, kind="ExternalInput").ap()
    out = nc.dram_tensor("out", (B, N, D), F32, kind="ExternalOutput").ap()
    build(nc, a, out)
    r = run_bass_kernel_spmd(nc, [arrays], core_ids=[0])
    return r.results[0]["out"]
```
